# Optimizing a Trainium2 kernel written in Bass

```python
import numpy as np
import jax
import jax.numpy as jnp

def _softmax(x, axis=-1):
    return jax.nn.softmax(x, axis=axis)

def _gelu(x):
    return jax.nn.gelu(x, approximate=True)

def _silu(x):
    return jax.nn.silu(x)

def _sigmoid(x):
    return jax.nn.sigmoid(x)

def _layernorm(x, axis=-1, eps=1e-05):
    m = jnp.mean(x, axis=axis, keepdims=True)
    v = jnp.var(x, axis=axis, keepdims=True)
    return (x - m) / jnp.sqrt(v + eps)

def _scatter_add(tgt, idx, src, axis=0):
    return tgt.at[idx].add(src)

def _segment_sum(src, seg, n):
    return jax.ops.segment_sum(src, seg, n)
kernel_name = 'mk_decoder_preln_d1_seqx_r8_f1216f'

def setup_inputs(seed: int=0):
    np.random.seed(seed)
    _w = jnp.asarray

    def _rec_inputs():
        import jax
        import jax.numpy as jnp
        _rk = jax.random.key(seed)
        x = -0.0002928 + 1 * jax.random.normal(jax.random.fold_in(_rk, 1), (8, 128, 128), jnp.float32)
        _lenS = 128 - jax.random.randint(jax.random.fold_in(_rk, 7), (8,), 0, max(1, 128 // 4) + 1, jnp.int32)
        _lenS2 = 77 - jax.random.randint(jax.random.fold_in(_rk, 8), (8,), 0, max(1, 77 // 4) + 1, jnp.int32)
        _ctx_768P = jax.random.normal(jax.random.fold_in(_rk, 11), (8, 16, 96), jnp.float32)
        _ctx_768c = jax.random.dirichlet(jax.random.fold_in(_rk, 511), 0.3 * jnp.ones((16,), jnp.float32), (8, 77))
        _ctx_768t = jnp.einsum('bsk,bkd->bsd', _ctx_768c, _ctx_768P)
        _ctx_768t = _ctx_768t * jax.lax.rsqrt(jnp.mean(jnp.square(_ctx_768t)) + 1e-12) * 0.953939
        ctx_768 = -0.00055796 + 0.999787 * (_ctx_768t + 0.3 * jax.random.normal(jax.random.fold_in(_rk, 611), (8, 77, 96), jnp.float32))
        return (x, ctx_768)
    x, ctx_768 = _rec_inputs()

    def _L0_attn_setup():
        import jax, jax.numpy as jnp
        import numpy as np
        D_MODEL, N_HEADS, N_KV, HEAD_DIM, D_LAT = (128, 8, 2, 128, 32)
        N_REP = N_HEADS // N_KV
        B, T = (2, 256)
        key = jax.random.key(seed)
        ks = jax.random.split(key, 8)
        s = lambda fan_in: 1.0 / np.sqrt(fan_in)
        return {'x': jax.random.normal(ks[0], (B, T, D_MODEL), jnp.float32), 'wq': jax.random.normal(ks[1], (D_MODEL, N_HEADS * HEAD_DIM), jnp.float32) * s(D_MODEL), 'wk_down': jax.random.normal(ks[2], (D_MODEL, N_KV * D_LAT), jnp.float32) * s(D_MODEL), 'wv_down': jax.random.normal(ks[3], (D_MODEL, N_KV * D_LAT), jnp.float32) * s(D_MODEL), 'wk_up': jax.random.normal(ks[4], (D_LAT, HEAD_DIM), jnp.float32) * s(D_LAT), 'wv_up': jax.random.normal(ks[5], (D_LAT, HEAD_DIM), jnp.float32) * s(D_LAT), 'wo': jax.random.normal(ks[6], (N_HEADS * HEAD_DIM, D_MODEL), jnp.float32) * s(N_HEADS * HEAD_DIM)}
    _L0_attn_all = _L0_attn_setup()
    _L0_attn_in = {k: v for k, v in _L0_attn_all.items() if k in ('wq', 'wk_down', 'wv_down', 'wk_up', 'wv_up', 'wo')}
    del _L0_attn_all

    def _L0_xattn_setup():
        import jax, jax.numpy as jnp
        import numpy as np
        HEADS = 16
        DIM_HEAD = 64
        key = jax.random.key(seed)
        ks = jax.random.split(key, 7)
        b, n, m = (2, 256, 128)
        query_dim, context_dim = (128, 96)
        inner = HEADS * DIM_HEAD
        s_q = 1.0 / np.sqrt(query_dim)
        s_c = 1.0 / np.sqrt(context_dim)
        s_i = 1.0 / np.sqrt(inner)
        return {'x': jax.random.normal(ks[0], (b, n, query_dim), jnp.float32), 'context': jax.random.normal(ks[1], (b, m, context_dim), jnp.float32), 'Wq': jax.random.normal(ks[2], (query_dim, inner), jnp.float32) * s_q, 'Wk': jax.random.normal(ks[3], (context_dim, inner), jnp.float32) * s_c, 'Wv': jax.random.normal(ks[4], (context_dim, inner), jnp.float32) * s_c, 'Wo': jax.random.normal(ks[5], (inner, query_dim), jnp.float32) * s_i, 'bo': jax.random.normal(ks[6], (query_dim,), jnp.float32) * 0.01}
    _L0_xattn_all = _L0_xattn_setup()
    _L0_xattn_in = {k: v for k, v in _L0_xattn_all.items() if k in ('Wq', 'Wk', 'Wv', 'Wo', 'bo')}
    del _L0_xattn_all

    def _L0_ffn_setup():
        import jax, jax.numpy as jnp
        import numpy as np
        B, T, C, H, E = (1, 32, 128, 256, 8)
        STD = 0.02
        key = jax.random.key(seed)
        ks = jax.random.split(key, 8)
        f32 = jnp.float32
        return {'x': jax.random.normal(ks[0], (B, T, C), f32), 'up': jax.random.normal(ks[1], (E, H, C), f32) * STD, 'gate': jax.random.normal(ks[2], (E, H, C), f32) * STD, 'down': jax.random.normal(ks[3], (E, C, H), f32) * STD, 'router': jax.random.normal(ks[4], (E, C), f32) * STD, 'w_up_s': jax.random.normal(ks[5], (H, C), f32) * STD, 'w_gate_s': jax.random.normal(ks[6], (H, C), f32) * STD, 'w_down_s': jax.random.normal(ks[7], (C, H), f32) * STD}
    _L0_ffn_all = _L0_ffn_setup()
    _L0_ffn_in = {k: v for k, v in _L0_ffn_all.items() if k in ('up', 'gate', 'down', 'router', 'w_up_s', 'w_gate_s', 'w_down_s')}
    del _L0_ffn_all
    return {'x': x, 'ctx_768': ctx_768, 'L0_attn_wq': _L0_attn_in['wq'], 'L0_attn_wk_down': _L0_attn_in['wk_down'], 'L0_attn_wv_down': _L0_attn_in['wv_down'], 'L0_attn_wk_up': _L0_attn_in['wk_up'], 'L0_attn_wv_up': _L0_attn_in['wv_up'], 'L0_attn_wo': _L0_attn_in['wo'], 'L0_xattn_Wq': _L0_xattn_in['Wq'], 'L0_xattn_Wk': _L0_xattn_in['Wk'], 'L0_xattn_Wv': _L0_xattn_in['Wv'], 'L0_xattn_Wo': _L0_xattn_in['Wo'], 'L0_xattn_bo': _L0_xattn_in['bo'], 'L0_ffn_up': _L0_ffn_in['up'], 'L0_ffn_gate': _L0_ffn_in['gate'], 'L0_ffn_down': _L0_ffn_in['down'], 'L0_ffn_router': _L0_ffn_in['router'], 'L0_ffn_w_up_s': _L0_ffn_in['w_up_s'], 'L0_ffn_w_gate_s': _L0_ffn_in['w_gate_s'], 'L0_ffn_w_down_s': _L0_ffn_in['w_down_s']}

def reference(x, ctx_768, L0_attn_wq, L0_attn_wk_down, L0_attn_wv_down, L0_attn_wk_up, L0_attn_wv_up, L0_attn_wo, L0_xattn_Wq, L0_xattn_Wk, L0_xattn_Wv, L0_xattn_Wo, L0_xattn_bo, L0_ffn_up, L0_ffn_gate, L0_ffn_down, L0_ffn_router, L0_ffn_w_up_s, L0_ffn_w_gate_s, L0_ffn_w_down_s):
    import jax
    import jax.numpy as jnp

    def _L0_attn_ref(x, wq, wk_down, wv_down, wk_up, wv_up, wo):
        import jax, jax.numpy as jnp
        import numpy as np
        D_MODEL, N_HEADS, N_KV, HEAD_DIM, D_LAT = (128, 8, 2, 128, 32)
        N_REP = N_HEADS // N_KV
        B, T = (2, 256)
        Bq, Tq, _ = x.shape
        scale = HEAD_DIM ** (-0.5)
        q = (x @ wq).reshape(Bq, Tq, N_KV, N_REP, HEAD_DIM)
        k_lat = (x @ wk_down).reshape(Bq, Tq, N_KV, D_LAT)
        v_lat = (x @ wv_down).reshape(Bq, Tq, N_KV, D_LAT)
        k = jnp.einsum('bkhl,ld->bkhd', k_lat, wk_up)
        v = jnp.einsum('bkhl,ld->bkhd', v_lat, wv_up)
        scores = jnp.einsum('bqhrd,bkhd->bhrqk', q, k) * scale
        causal = jnp.tril(jnp.ones((Tq, Tq), dtype=bool))
        scores = jnp.where(causal, scores, jnp.finfo(scores.dtype).min)
        probs = jax.nn.softmax(scores, axis=-1)
        y = jnp.einsum('bhrqk,bkhd->bqhrd', probs, v)
        y = y.reshape(Bq, Tq, N_HEADS * HEAD_DIM)
        return y @ wo

    def _L0_xattn_ref(x, context, Wq, Wk, Wv, Wo, bo):
        import jax, jax.numpy as jnp
        import numpy as np
        HEADS = 16
        DIM_HEAD = 64
        b, n, _ = x.shape
        h, d = (HEADS, DIM_HEAD)
        scale = d ** (-0.5)
        q = (x @ Wq).reshape(b, n, h, d).transpose(0, 2, 1, 3)
        k = (context @ Wk).reshape(b, -1, h, d).transpose(0, 2, 1, 3)
        v = (context @ Wv).reshape(b, -1, h, d).transpose(0, 2, 1, 3)
        sim = jnp.einsum('bhid,bhjd->bhij', q, k) * scale
        attn = jax.nn.softmax(sim, axis=-1)
        out = jnp.einsum('bhij,bhjd->bhid', attn, v)
        out = out.transpose(0, 2, 1, 3).reshape(b, n, h * d)
        return out @ Wo + bo

    def _L0_ffn_ref(x, up, gate, down, router, w_up_s, w_gate_s, w_down_s):
        import jax, jax.numpy as jnp
        import numpy as np
        B, T, C, H, E = (1, 32, 128, 256, 8)
        STD = 0.02
        b, t, c = x.shape
        x_ = x.reshape(b * t, c)
        logits = x_ @ router.T
        idx = jnp.argmax(logits, axis=-1)
        onehot = jax.nn.one_hot(idx, router.shape[0], dtype=x.dtype)
        u = jnp.einsum('bc,ehc->ebh', x_, up)
        g = jnp.einsum('bc,ehc->ebh', x_, gate)
        h = jax.nn.silu(g) * u
        ye = jnp.einsum('ebh,ech->ebc', h, down)
        y = jnp.einsum('ebc,be->bc', ye, onehot)
        ys = jax.nn.silu(x_ @ w_gate_s.T) * (x_ @ w_up_s.T) @ w_down_s.T
        return (y + ys).reshape(b, t, c)
    x = x + _L0_attn_ref(_layernorm(x, axis=-1), L0_attn_wq, L0_attn_wk_down, L0_attn_wv_down, L0_attn_wk_up, L0_attn_wv_up, L0_attn_wo)
    x = x + _L0_xattn_ref(_layernorm(x, axis=-1), ctx_768, L0_xattn_Wq, L0_xattn_Wk, L0_xattn_Wv, L0_xattn_Wo, L0_xattn_bo)
    x = x + _L0_ffn_ref(_layernorm(x, axis=-1), L0_ffn_up, L0_ffn_gate, L0_ffn_down, L0_ffn_router, L0_ffn_w_up_s, L0_ffn_w_gate_s, L0_ffn_w_down_s)
    return x

_drawn_inputs = setup_inputs


def setup_inputs(seed=0):
    import zlib

    import numpy as np

    out = dict(_drawn_inputs(seed))
    spreads = {}
    factors = {'L0_xattn_bo': 6.243,
     'L0_ffn_up': 7.953,
     'L0_ffn_gate': 7.907,
     'L0_ffn_down': 7.888,
     'L0_ffn_router': 8.0,
     'L0_ffn_w_up_s': 8.0,
     'L0_ffn_w_gate_s': 7.962,
     'L0_ffn_w_down_s': 7.969}
    for name, (base, spread) in spreads.items():
        noise = np.random.default_rng([zlib.crc32(name.encode()), seed]).standard_normal(out[name].shape)
        drawn = base * np.exp(spread * noise) if base else spread * noise
        out[name] = jnp.asarray(drawn.astype(out[name].dtype))
    for name, factor in factors.items():
        out[name] = (out[name] * factor).astype(out[name].dtype)
    return out
```

```python
from contextlib import ExitStack

import concourse.bass as bass
from concourse import mybir

F32 = mybir.dt.float32
BF16 = mybir.dt.bfloat16
I32 = mybir.dt.int32
U32 = mybir.dt.uint32
ALU = mybir.AluOpType
ACT = mybir.ActivationFunctionType
AX_X = mybir.AxisListType.X


def build_layer(nc, x, ctxT, wqT, wkd, wvd, wkuT, wvuT, wo, xwqT, xwkT, xwv, xwo, xbo, ug, dn, router, ug_s, dn_s, ident, mask, tri, steps, out):
    P = 128
    NB, T, C = x.shape
    CC, NK = ctxT.shape[0], ctxT.shape[1] // NB
    H = wqT.shape[1]
    L = wkuT.shape[1]
    KV = wkd.shape[1] // L
    REP = H // KV
    XH = 16
    XD = xwv.shape[1] // XH
    XP = XH // 2
    SCALE = float(wqT.shape[0]) ** -0.5
    XSCALE = float(XD) ** -0.5
    EPS = 1e-5
    HALF = NB // 2 * NK
    E = router.shape[1]
    HID = ug.shape[2] // 2
    HK = HID // P
    NT = (NB * T - E) // P + E
    CH = [(0, 5), (5, 10), (10, XH)]

    with ExitStack() as ctx:
        def sb(name, shape, dt=F32):
            return ctx.enter_context(nc.sbuf_tensor(name, shape, dt))

        def sem(name):
            return ctx.enter_context(nc.semaphore(name))

        bank = [ctx.enter_context(nc.psum_tensor(f"bank{n}", [P, 512], F32)) for n in range(8)]

        identity = sb("identity", [P, P])
        identity_bf = sb("identity_bf", [P, P], BF16)
        causal = sb("causal", [P, REP, T], BF16)
        causal_in = sb("causal_in", [P, T])
        group_rows = sb("group_rows", [P, REP])
        minus_half = sb("minus_half", [P, 1])
        ctxT_s = sb("ctxT_s", [CC, NB * NK])
        wqT_s = sb("wqT_s", [P, H, C])
        wkuT_s = sb("wkuT_s", [P, L])
        wvuT_s = sb("wvuT_s", [P, L])
        wo_s = sb("wo_s", [P, H, C])
        wkd_s = sb("wkd_s", [C, KV * L])
        wkd_rep = sb("wkd_rep", [C, KV, REP, L])
        wvd_s = sb("wvd_s", [C, KV * L])
        xwqT_s = sb("xwqT_s", [P, XP, C])
        xwkT_s = sb("xwkT_s", [P, XP, CC])
        xwv_s = sb("xwv_s", [CC, XH * XD])
        xwo_s = sb("xwo_s", [P, XP, C])
        ug_w = sb("ug_w", [C, E * 2 * HID])
        dn_w = sb("dn_w", [P, E * HK * C])
        router_w = sb("router_w", [C, E])
        ugs_w = sb("ugs_w", [C, 2 * HID])
        dns_w = sb("dns_w", [P, HK, C])
        tri_in = sb("tri_in", [P, P])
        tri_bf = sb("tri_bf", [P, P], BF16)
        ones_bf = sb("ones_bf", [P, P], BF16)
        steps_s = sb("steps_s", [P, 2 * E + NT])
        bo_row = sb("bo_row", [P, C])
        qlat_w = sb("qlat_w", [C, H * L])
        ylat_w = sb("ylat_w", [P, KV, C])
        xqk_w = sb("xqk_w", [CC, XH, C])
        G = sb("G", [C, NB * XH * NK])
        G4 = G[:, :].rearrange("c (b h k) -> c b h k", b=NB, h=XH)

        xs = sb("xs", [T, NB * C])
        a_stat = sb("a_stat", [T, NB, 6])
        a_mv = sb("a_mv", [T, NB, 2])
        a_ve = sb("a_ve", [T, NB])
        a_rstd = sb("a_rstd", [T, NB])
        a_xn = sb("a_xn", [T, NB, C])
        a_xnT = sb("a_xnT", [C, NB * T])
        v_all = sb("v_all", [T, NB * KV * L])
        c_stat = sb("c_stat", [T, 6])
        c_mv = sb("c_mv", [T, 2])
        c_ve = sb("c_ve", [T, 1])
        c_rstd = sb("c_rstd", [T, 1])
        q_s = sb("q_s", [P, KV, T])
        k_bd = sb("k_bd", [P, KV, REP, T])
        v_s = sb("v_s", [T, KV * L])
        a_max = sb("a_max", [T, H])
        a_nmax = sb("a_nmax", [T, H])
        a_sum = sb("a_sum", [T, H])
        a_rec = sb("a_rec", [T, H])
        a_p = sb("a_p", [T, H, T])
        a_pT = sb("a_pT", [T, H, T])
        a_oT = sb("a_oT", [P, KV, T])
        c_xn = sb("c_xn", [T, C])
        c_xnT = sb("c_xnT", [C, T])
        c_max = sb("c_max", [T, XH])
        c_sum = sb("c_sum", [T, XH])
        c_rec = sb("c_rec", [T, XH])
        c_p = sb("c_p", [T, XH, NK])
        c_pT = sb("c_pT", [NK, XH, T])
        ctx_b = sb("ctx_b", [CC, NK])
        xv_s = sb("xv_s", [NK, XH * XD])
        c_oT = sb("c_oT", [P, XP, T])

        r_stat = sb("r_stat", [T, 6])
        r_mv = sb("r_mv", [T, 2])
        r_ve = sb("r_ve", [T, 1])
        r_rstd = sb("r_rstd", [T, 1])
        r_xn = sb("r_xn", [T, C])
        r_xnT = sb("r_xnT", [C, T])
        r_log = sb("r_log", [T, E])
        r_top = sb("r_top", [T, 8])
        r_idx = sb("r_idx", [T, 8], U32)
        xn_all = sb("xn_all", [T, NB * C])
        xnT_all = sb("xnT_all", [C, NB * T])
        pick = sb("pick", [T, NB])
        hot = sb("hot", [T, NB, E])
        hot_bf = sb("hot_bf", [T, NB + 1, E], BF16)
        full = sb("full", [T, E, E])
        n_tiles = sb("n_tiles", [T, E])
        tile_end = sb("tile_end", [T, E])
        one_row = sb("one_row", [T, E])
        start = sb("start", [T, E])
        place = sb("place", [T, NB, E])
        slot_f = sb("slot_f", [T, NB])
        slot = sb("slot", [T, NB], U32)
        done_by = sb("done_by", [T, NT, E])
        owner_f = sb("owner_f", [T, NT])
        owner = sb("owner", [T, NT], I32)
        RING = 4
        xg = [sb(f"xg{n}", [P, C]) for n in range(RING)]
        xgT = [sb(f"xgT{n}", [C, P]) for n in range(2)]
        th = [sb(f"th{n}", [P, HID]) for n in range(2)]
        hu = [sb(f"hu{n}", [P, HID]) for n in range(2)]
        hg = [sb(f"hg{n}", [P, HID]) for n in range(2)]
        hT = [sb(f"hT{n}", [P, HK, P]) for n in range(2)]
        yg = [sb(f"yg{n}", [P, C]) for n in range(RING)]
        s_th = [sb(f"s_th{n}", [P, 512]) for n in range(2)]
        s_hu = [sb(f"s_hu{n}", [P, 512]) for n in range(2)]
        s_hT = sb("s_hT", [P, HK, NB * T])
        yt = sb("yt", [T, NB, C])
        x_slots = nc.dram_tensor("x_slots", (NT * P, C), F32).ap()
        y_slots = nc.dram_tensor("y_slots", (NT * P, C), F32).ap()

        ld = {n: sem("ld_" + n) for n in ("x", "const", "kv", "bo", "qk", "ctx", "xqk", "wo", "xwv", "xwo", "ug", "dn", "router", "shared", "sort")}
        stored = sem("stored")
        half_ready = sem("half_ready")
        consts_ready = sem("consts_ready")
        ln1_ready = sem("ln1_ready")
        ln1_rstd = sem("ln1_rstd")
        su_q = sem("su_q")
        su_qc = sem("su_qc")
        su_T = sem("su_T")
        su_Tc = sem("su_Tc")
        su_v = sem("su_v")
        su_vc = sem("su_vc")
        su_x = sem("su_x")
        su_xA = sem("su_xA")
        su_xD = sem("su_xD")
        su_g = sem("su_g")
        su_gA = sem("su_gA")
        su_gD = sem("su_gD")
        su_y = sem("su_y")
        su_yc = sem("su_yc")
        names = dict(
            a_v=1, a_qk0=1, a_k1=1, a_qc=1, a_k0c=4, a_k1c=1, a_sc=2, a_mx=2, a_nm=2, a_ex=8, a_rc=2, a_nr=2,
            b_pT=2, b_pc=2, b_o=1, b_oc=1, b_y=1, b_x1=1,
            v_in=1, v_mm=2, v_c0=1, v_c1=1,
            c_st=1, c_mvd=1, c_ved=1, c_rs=1, c_xnd=1, c_bo=1, c_T=1, c_xTc=1, c_sc=3, c_mx=3, c_sb=3, c_ex=3, c_sm=1, c_rc=1, c_nr=4,
            r_st=1, r_mvd=1, r_ved=1, r_rs=1, r_xnd=1, r_keep=2, r_T=1, r_Tc=1, r_lg=1, r_lgc=1, r_mx=1, r_ix=1, r_pk=1,
            d_pT=4, d_pA=2, d_pD=2, d_o=4, d_oc=4, d_y=1, d_x2=1)
        S = {n: sem(n) for n in names}

        def after(eng, name, j, count=None):
            n = names[name]
            c = n if count is None else count
            if isinstance(j, int):
                if j < 0:
                    return
                j, c = (NB - 1, n) if j >= NB else (j, c)
            eng.wait_ge(S[name], j * n + c)

        zeroed = sem("zeroed")
        zero_src = sem("zero_src")
        sort_c = sem("sort_c")
        sort_d = sem("sort_d")
        ranked = sem("ranked")
        slots_ready = sem("slots_ready")
        owners_ready = sem("owners_ready")
        scattered = sem("scattered")
        s_ug = sem("s_ug")
        s_tanh = sem("s_tanh")
        s_up = sem("s_up")
        s_h = sem("s_h")
        s_dn = sem("s_dn")
        s_add = sem("s_add")
        f_ld = [sem(f"f_ld{n}") for n in range(RING)]
        f_T = sem("f_T")
        f_Tc = sem("f_Tc")
        f_ug = sem("f_ug")
        f_th = sem("f_th")
        f_hu = sem("f_hu")
        f_h = sem("f_h")
        f_hT = sem("f_hT")
        f_hTc = sem("f_hTc")
        f_dn = sem("f_dn")
        f_y = sem("f_y")
        f_st = [sem(f"f_st{n}") for n in range(RING)]
        gathered = [sem(f"gathered{n}") for n in range(NB)]
        final = sem("final")

        block = ctx.enter_context(nc.Block())

        def pipeline(eng, body):
            for i in range(4):
                body(i)
            with eng.Fori(4, NB) as i:
                body(i)
            for i in range(NB, NB + 3):
                body(i)

        def tiles(eng, step, lag=3):
            full_at = RING + 3
            rounds = (NT - full_at) // RING
            for s in range(full_at):
                step(s, s % RING)
            with eng.Fori(0, rounds) as r:
                for n in range(full_at, full_at + RING):
                    step(r * RING + n, n % RING)
            for s in range(full_at + rounds * RING, NT + lag):
                step(s, s % RING)

        def tile(s, ago):
            k = s - ago
            return not isinstance(k, int) or 0 <= k < NT

        def store_count(k):
            return k // RING * 16 + 16

        def reach(eng, semaphore, value):
            if not isinstance(value, int) or value > 0:
                eng.wait_ge(semaphore, value)

        def has(j):
            return not isinstance(j, int) or 0 <= j < NB

        def first(i):
            return isinstance(i, int) and i == 0

        G_BANK = (2, 3, 4, 7)
        PT_BANK = (2, 3, 4, 2)
        SH_BANK = ((0, 1, 3, 4), (1, 2, 5, 3))
        SH_OUT = (6, 7)
        O_BANK = (5, 7, 5, 7)

        @block.sync
        def _(sp):
            sp.dma_start(xs[:, :].rearrange("t (b c) -> t b c", b=NB), x.rearrange("b t c -> t b c")).then_inc(ld["x"], 16)
            sp.dma_start(identity[:, :], ident).then_inc(ld["const"], 16)
            sp.dma_start(causal_in[:, :], mask).then_inc(ld["const"], 16)
            sp.dma_start(xwkT_s[:, :, :], xwkT).then_inc(ld["xqk"], 16)
            sp.dma_start(xwqT_s[:, :, :], xwqT).then_inc(ld["xqk"], 16)
            sp.dma_start(xwv_s[:, :], xwv).then_inc(ld["xwv"], 16)
            sp.dma_start(xwo_s[:, :, :], xwo.rearrange("(k p) c -> p k c", p=P)).then_inc(ld["xwo"], 16)
            sp.dma_start(router_w[:, :], router).then_inc(ld["router"], 16)
            sp.dma_start(tri_in[:, :], tri).then_inc(ld["sort"], 16)
            sp.dma_start(steps_s[:, :], steps.rearrange("(a c) -> a c", a=1).broadcast_to([P, 2 * E + NT])).then_inc(ld["sort"], 16)
            sp.dma_start(ugs_w[:, :], ug_s).then_inc(ld["shared"], 16)
            sp.dma_start(dns_w[:, :, :], dn_s).then_inc(ld["shared"], 16)
            sp.dma_start(ug_w[:, :].rearrange("c (e n) -> c e n", e=E), ug).then_inc(ld["ug"], 16)
            sp.dma_start(dn_w[:, :].rearrange("p (e n) -> p e n", e=E), dn).then_inc(ld["dn"], 16)
            sp.wait_ge(zero_src, 1)
            zero = s_hT[:, :, :].rearrange("p k t -> p (k t)")[:, 0:NT * C]
            sp.dma_start(x_slots.rearrange("(n p) c -> p n c", p=P), zero.rearrange("p (n c) -> p n c", c=C)).then_inc(zeroed, 16)
            sp.wait_ge(scattered, 16 * NB)

            def load(k, n):
                reach(sp, f_T, k - RING + 1)
                sp.dma_start(xg[n][:, :], x_slots[bass.ds(k * P, P), :]).then_inc(f_ld[n], 16)

            def store(k, n):
                sp.wait_ge(f_y, k + 1)
                sp.dma_start(y_slots[bass.ds(k * P, P), :], yg[n][:, :]).then_inc(f_st[n], 16)

            def step(s, n):
                if tile(s, 0):
                    load(s, n)
                if tile(s, RING + 3):
                    store(s - RING - 3, (n + 1) % RING)

            tiles(sp, step, RING + 3)
            for b in range(0, NB, 2):
                sp.wait_ge(final, b + 2)
                sp.dma_start(out[b:b + 2, :, :].rearrange("b t c -> t b c"), yt[:, b:b + 2, :]).then_inc(stored, 16)
            sp.wait_ge(stored, 16 * (NB // 2))

        @block.scalar
        def _(act):
            act.dma_start(wkuT_s[:, :], wkuT).then_inc(ld["qk"], 16)
            act.dma_start(wqT_s[:, :, :], wqT).then_inc(ld["qk"], 16)
            act.dma_start(wkd_s[:, :], wkd).then_inc(ld["kv"], 16)
            act.dma_start(wvd_s[:, :], wvd).then_inc(ld["kv"], 16)
            act.dma_start(ctxT_s[:, :], ctxT).then_inc(ld["ctx"], 16)
            act.dma_start(wvuT_s[:, :], wvuT).then_inc(ld["wo"], 16)
            act.dma_start(wo_s[:, :, :], wo.rearrange("(h p) c -> p h c", p=P)).then_inc(ld["wo"], 16)
            act.dma_start(bo_row[:, :], xbo.rearrange("(a c) -> a c", a=1).broadcast_to([P, C])).then_inc(ld["bo"], 16)

            def g_copy(half, h):
                act.wait_ge(su_g, half * XH + h + 1)
                nc.scalar.copy(G4[:, half * NB // 2:(half + 1) * NB // 2, h, :],
                               bank[G_BANK[h % 4]][:, 0:HALF].rearrange("p (b k) -> p b k", k=NK)).then_inc(su_gA, 1)

            act.wait_ge(su_q, 1)
            nc.scalar.copy(qlat_w[:, :], bank[0][:, 0:H * L]).then_inc(su_qc, 1)
            for n in (0, 1):
                act.wait_ge(su_T, n + 1)
                nc.scalar.copy(a_xnT[:, n * 512:(n + 1) * 512], bank[6 + n][:, :]).then_inc(su_Tc, 1)
            for n in (0, 2):
                act.wait_ge(su_x, n + 1)
                nc.scalar.copy(xqk_w[:, n // 2 * 8:n // 2 * 8 + 7:2, :], bank[2 + n][0:CC, :].rearrange("p (h c) -> p h c", h=4)).then_inc(su_xA, 1)
            for h in range(0, XH, 2):
                g_copy(0, h)

            def body(i):
                a, c, d, e = i, i - 1, i - 2, i - 3
                if has(a):
                    after(act, "a_qk0", a)
                    after(act, "a_sc", a - 1)
                    nc.scalar.copy(q_s[:, :, :], bank[5][:, 0:KV * T].rearrange("p (g t) -> p g t", g=KV)).then_inc(S["a_qc"], 1)
                    for r in range(REP):
                        p = slice(r * L, (r + 1) * L)
                        nc.scalar.copy(k_bd[p, 0, r, :], bank[5][p, 2 * T:3 * T]).then_inc(S["a_k0c"], 1)
                if first(i):
                    for h in range(0, XH, 2):
                        g_copy(1, h)

                def pT_copy(g):
                    after(act, "d_pT", d, g + 1)
                    nc.scalar.copy(c_pT[:, 4 * g:4 * g + 4, :], bank[PT_BANK[g]][0:NK, :].rearrange("p (h t) -> p h t", h=4)).then_inc(S["d_pA"], 1)

                def o_copy(g):
                    after(act, "d_o", d, g + 1)
                    nc.scalar.copy(c_oT[:, 2 * g:2 * g + 2, :], bank[O_BANK[g]][:, 0:2 * T].rearrange("p (h t) -> p h t", h=2)).then_inc(S["d_oc"], 1)

                def exps(g):
                    after(act, "a_nm", a, g + 1)
                    if g == 0:
                        after(act, "b_pT", a - 1)
                    for h in range(g * REP, (g + 1) * REP):
                        nc.scalar.activation(a_p[:, h, :], bank[g][:, h % REP * T:h % REP * T + T], ACT.Exp,
                                             bias=a_nmax[:, h:h + 1], scale=SCALE, accum_out=a_sum[:, h:h + 1]).then_inc(S["a_ex"], 1)

                if has(d):
                    pT_copy(0)
                if has(a):
                    exps(0)
                if has(d):
                    o_copy(0)
                    pT_copy(2)
                    o_copy(1)
                if has(a):
                    exps(1)
                if has(d):
                    o_copy(2)
                    o_copy(3)
                if has(e):
                    after(act, "r_T", e)
                    after(act, "r_lg", e - 1)
                    after(act, "r_keep", e - 1)
                    nc.scalar.copy(r_xnT[:, :], bank[7][:, 0:T]).then_inc(S["r_Tc"], 1)
                if has(c):
                    for n, (h0, h1) in enumerate(CH):
                        after(act, "c_sb", c, n + 1)
                        nc.scalar.activation(c_p[:, h0:h1, :], c_p[:, h0:h1, :], ACT.Exp, scale=XSCALE).then_inc(S["c_ex"], 1)
                if has(a):
                    for g in range(2):
                        after(act, "b_pT", a, g + 1)
                        nc.scalar.copy(a_pT[:, g * REP:(g + 1) * REP, :], bank[g][:, :].rearrange("p (h t) -> p h t", h=REP)).then_inc(S["b_pc"], 1)
                if has(c):
                    after(act, "v_mm", c, 1)
                    nc.scalar.copy(xv_s[:, 0:512], bank[5][0:NK, :]).then_inc(S["v_c0"], 1)
                if has(a):
                    after(act, "b_o", a)
                    nc.scalar.copy(a_oT[:, :, :], bank[6][:, 0:KV * T].rearrange("p (g t) -> p g t", g=KV)).then_inc(S["b_oc"], 1)
                if has(c):
                    after(act, "v_mm", c, 2)
                    nc.scalar.copy(xv_s[:, 512:1024], bank[7][0:NK, :]).then_inc(S["v_c1"], 1)

            def shared_tanh(half):
                for k in range(HK):
                    n = half * HK + k
                    act.wait_ge(s_ug, n + 1)
                    reach(act, s_h, n - 1)
                    nc.scalar.activation(s_th[n % 2][:, :], bank[SH_BANK[half][2 * k + 1]][:, :], ACT.Tanh, scale=0.5).then_inc(s_tanh, 1)

            pipeline(act, body)
            shared_tanh(0)
            shared_tanh(1)

            def step(s, n):
                if tile(s, 3):
                    k = s - 3
                    act.wait_ge(f_dn, k + 1)
                    if tile(s, 3 + RING):
                        act.wait_ge(f_st[(n + 1) % RING], store_count(k - RING))
                    nc.scalar.copy(yg[(n + 1) % RING][:, :], bank[6 + (n + 1) % 2][:, 0:C]).then_inc(f_y, 1)
                if tile(s, 0):
                    act.wait_ge(f_T, s + 1)
                    reach(act, f_ug, s - 1)
                    nc.scalar.copy(xgT[n % 2][:, :], bank[n % 2][:, 0:P]).then_inc(f_Tc, 1)
                if tile(s, 1):
                    act.wait_ge(f_ug, s)
                    reach(act, f_hu, s - 2)
                    nc.scalar.activation(th[(n + 1) % 2][:, :], bank[2 + (n + 1) % 2][:, HID:2 * HID], ACT.Tanh, scale=0.5).then_inc(f_th, 1)

            tiles(act, step)

        @block.gpsimd
        def _(pool):
            nc.gpsimd.memset(minus_half[:, :], -0.5).then_inc(half_ready, 1)
            pool.wait_ge(half_ready, 1)
            pool.wait_ge(ln1_ready, 2 * NB + 1)
            nc.gpsimd.tensor_tensor(a_rstd[:, :], a_ve[:, :], minus_half[:, :].broadcast_to([T, NB]), ALU.pow).then_inc(ln1_rstd, 1)
            pool.wait_ge(ld["ctx"], 16)
            pool.wait_ge(ld["bo"], 16)
            pool.wait_ge(su_vc, 1)

            def body(i):
                a, c, d, e = i, i - 1, i - 2, i - 3
                if has(c):
                    after(pool, "c_ved", c)
                    nc.gpsimd.tensor_tensor(c_rstd[:, :], c_ve[:, :], minus_half[:, :], ALU.pow).then_inc(S["c_rs"], 1)
                if has(a):
                    after(pool, "b_o", a - 1)
                    nc.gpsimd.tensor_copy(v_s[:, :], v_all[:, bass.ds(a * (KV * L), KV * L)]).then_inc(S["a_v"], 1)
                if has(c):
                    after(pool, "v_mm", c - 1)
                    nc.gpsimd.tensor_copy(ctx_b[:, :], ctxT_s[:, bass.ds(c * NK, NK)]).then_inc(S["v_in"], 1)
                    after(pool, "c_xnd", c)
                    rows = xs[:, bass.ds(c * C, C)]
                    nc.gpsimd.tensor_tensor(rows, rows, bo_row[:, :], ALU.add).then_inc(S["c_bo"], 1)
                if has(e):
                    after(pool, "r_ved", e)
                    nc.gpsimd.tensor_tensor(r_rstd[:, :], r_ve[:, :], minus_half[:, :], ALU.pow).then_inc(S["r_rs"], 1)
                if has(a):
                    for g in range(2):
                        after(pool, "a_rc", a, g + 1)
                        h = slice(g * REP, (g + 1) * REP)
                        nc.gpsimd.tensor_tensor(a_p[:, h, :], a_p[:, h, :], a_rec[:, h].rearrange("p (h t) -> p h t", t=1).broadcast_to([T, REP, T]),
                                                ALU.mult).then_inc(S["a_nr"], 1)
                if has(e):
                    after(pool, "r_xnd", e)
                    nc.gpsimd.tensor_copy(xn_all[:, bass.ds(e * C, C)], r_xn[:, :]).then_inc(S["r_keep"], 1)
                    after(pool, "r_Tc", e)
                    nc.gpsimd.tensor_copy(xnT_all[:, bass.ds(e * T, T)], r_xnT[:, :]).then_inc(S["r_keep"], 1)
                if has(c):
                    after(pool, "c_rc", c)
                    for g in range(4):
                        h = slice(g * 4, g * 4 + 4)
                        nc.gpsimd.tensor_tensor(c_p[:, h, :], c_p[:, h, :], c_rec[:, h].rearrange("p (h t) -> p h t", t=1).broadcast_to([T, 4, NK]),
                                                ALU.mult).then_inc(S["c_nr"], 1)

            pipeline(pool, body)

            pool.wait_ge(zeroed, 16)
            pool.wait_ge(slots_ready, 1)
            pool.wait_ge(S["r_keep"], 2 * NB)
            for b in range(NB):
                nc.gpsimd.indirect_dma_start(out=x_slots, out_offset=bass.IndirectOffsetOnAxis(ap=slot[:, b:b + 1], axis=0),
                                             in_=xn_all[:, b * C:(b + 1) * C], in_offset=None).then_inc(scattered, 16)
            for n in range(RING):
                pool.wait_ge(f_st[n], 16 * len(range(n, NT, RING)))
            for b in range(NB):
                nc.gpsimd.indirect_dma_start(out=yt[:, b, :], out_offset=None, in_=y_slots,
                                             in_offset=bass.IndirectOffsetOnAxis(ap=slot[:, b:b + 1], axis=0)).then_inc(gathered[b], 16)

        @block.vector
        def _(dve):
            nc.vector.memset(k_bd[:, :, :, :], 0.0).then_inc(consts_ready, 1)
            nc.vector.memset(s_hT[:, :, :], 0.0).then_inc(zero_src, 1)
            nc.vector.memset(hot_bf[:, NB, :], 0.0).then_inc(sort_c, 1)
            nc.vector.memset(ones_bf[:, :], 1.0).then_inc(sort_c, 1)
            nc.vector.memset(one_row[:, :], 1.0).then_inc(sort_c, 1)
            dve.wait_ge(ld["x"], 16)
            for b in range(NB):
                nc.vector.bn_stats(a_stat[:, b, :], xs[:, b * C:(b + 1) * C]).then_inc(ln1_ready, 1)
            for b in range(NB):
                dve.wait_ge(ln1_ready, NB)
                nc.vector.bn_aggr(a_mv[:, b, :], a_stat[:, b, :]).then_inc(ln1_ready, 1)
            dve.wait_ge(ln1_ready, 2 * NB)
            nc.vector.tensor_scalar(a_ve[:, :], a_mv[:, :, 1], EPS, None, ALU.add).then_inc(ln1_ready, 1)
            dve.wait_ge(ld["const"], 32)
            nc.vector.tensor_copy(identity_bf[:, :], identity[:, :]).then_inc(consts_ready, 1)
            nc.vector.tensor_copy(causal[:, :, :], causal_in[:, :].rearrange("p (a t) -> p a t", a=1).broadcast_to([P, REP, T])).then_inc(consts_ready, 1)
            nc.vector.tensor_reduce(group_rows[:, :], identity[:, :].rearrange("p (r l) -> p r l", l=L), AX_X, ALU.add).then_inc(consts_ready, 1)
            dve.wait_ge(ld["kv"], 32)
            nc.vector.tensor_copy(wkd_rep[:, :, :, :], wkd_s[:, :].rearrange("p (g a l) -> p g a l", g=KV, a=1).broadcast_to([C, KV, REP, L])).then_inc(consts_ready, 1)
            dve.wait_ge(ln1_rstd, 1)
            for b in range(NB):
                nc.vector.tensor_scalar(a_xn[:, b, :], xs[:, b * C:(b + 1) * C], a_mv[:, b, 0:1], a_rstd[:, b:b + 1],
                                        ALU.subtract, ALU.mult).then_inc(ln1_ready, 1)
            dve.wait_ge(consts_ready, 5)

            def plain_wait():
                dve.wait_ge(ld["x"], 16)

            def g_copy(half, h):
                dve.wait_ge(su_g, half * XH + h + 1)
                nc.vector.tensor_copy(G4[:, half * NB // 2:(half + 1) * NB // 2, h, :],
                                      bank[G_BANK[h % 4]][:, 0:HALF].rearrange("p (b k) -> p b k", k=NK)).then_inc(su_gD, 1)

            dve.wait_ge(su_v, 1)
            nc.vector.tensor_copy(v_all[:, :], bank[1][:, 0:NB * KV * L]).then_inc(su_vc, 1)
            for n in (1, 3):
                dve.wait_ge(su_x, n + 1)
                nc.vector.tensor_copy(xqk_w[:, 1 + n // 2 * 8:n // 2 * 8 + 8:2, :], bank[2 + n][0:CC, :].rearrange("p (h c) -> p h c", h=4)).then_inc(su_xD, 1)
            dve.wait_ge(su_y, 1)
            nc.vector.tensor_copy(ylat_w[:, :, :], bank[0][:, 0:KV * C].rearrange("p (g c) -> p g c", g=KV)).then_inc(su_yc, 1)
            for h in range(1, XH, 2):
                g_copy(0, h)

            def body(i):
                a, c, d, e = i, i - 1, i - 2, i - 3
                if has(a):
                    after(dve, "a_k1", a)
                    after(dve, "a_sc", a - 1)
                    nc.vector.tensor_tensor(k_bd[:, 1, :, :], bank[1][:, 0:T].rearrange("p (a t) -> p a t", a=1).broadcast_to([P, REP, T]),
                                            group_rows[:, :].rearrange("p (r a) -> p r a", a=1).broadcast_to([P, REP, T]), ALU.mult).then_inc(S["a_k1c"], 1)
                if has(c):
                    crows = xs[:, bass.ds(c * C, C)]
                    after(dve, "b_x1", c)
                    nc.vector.bn_stats(c_stat[:, :], crows).then_inc(S["c_st"], 1)
                    plain_wait()
                    after(dve, "c_st", c)
                    nc.vector.bn_aggr(c_mv[:, :], c_stat[:, :]).then_inc(S["c_mvd"], 1)
                    after(dve, "c_mvd", c)
                    nc.vector.tensor_scalar(c_ve[:, :], c_mv[:, 1:2], EPS, None, ALU.add).then_inc(S["c_ved"], 1)
                if first(i):
                    for h in range(1, XH, 2):
                        g_copy(1, h)

                def pT_copy(g):
                    after(dve, "d_pT", d, g + 1)
                    nc.vector.tensor_copy(c_pT[:, 4 * g:4 * g + 4, :], bank[PT_BANK[g]][0:NK, :].rearrange("p (h t) -> p h t", h=4)).then_inc(S["d_pD"], 1)

                def row_max(g):
                    after(dve, "a_sc", a, g + 1)
                    hs = slice(g * REP, (g + 1) * REP)
                    nc.vector.reduce_max(a_max[:, hs], bank[g][:, :].rearrange("p (h t) -> p h t", h=REP), AX_X).then_inc(S["a_mx"], 1)
                    after(dve, "a_mx", a, g + 1)
                    nc.vector.tensor_scalar(a_nmax[:, hs], a_max[:, hs], -SCALE, None, ALU.mult).then_inc(S["a_nm"], 1)

                def row_rec(g):
                    hs = slice(g * REP, (g + 1) * REP)
                    after(dve, "a_ex", a, REP * (g + 1))
                    nc.vector.reciprocal(a_rec[:, hs], a_sum[:, hs]).then_inc(S["a_rc"], 1)

                if has(c):
                    after(dve, "c_rs", c)
                    nc.vector.tensor_scalar(c_xn[:, :], crows, c_mv[:, 0:1], c_rstd[:, 0:1], ALU.subtract, ALU.mult).then_inc(S["c_xnd"], 1)
                if has(d):
                    pT_copy(1)
                if has(a):
                    row_max(0)
                if has(e):
                    erows = xs[:, bass.ds(e * C, C)]
                    after(dve, "d_x2", e)
                    nc.vector.bn_stats(r_stat[:, :], erows).then_inc(S["r_st"], 1)
                    plain_wait()
                    after(dve, "r_st", e)
                    nc.vector.bn_aggr(r_mv[:, :], r_stat[:, :]).then_inc(S["r_mvd"], 1)
                    after(dve, "r_mvd", e)
                    nc.vector.tensor_scalar(r_ve[:, :], r_mv[:, 1:2], EPS, None, ALU.add).then_inc(S["r_ved"], 1)
                if has(e):
                    after(dve, "r_rs", e)
                    after(dve, "r_T", e - 1)
                    after(dve, "r_keep", e - 1)
                    nc.vector.tensor_scalar(r_xn[:, :], erows, r_mv[:, 0:1], r_rstd[:, 0:1], ALU.subtract, ALU.mult).then_inc(S["r_xnd"], 1)
                if has(a):
                    row_max(1)
                    row_rec(0)
                if has(d):
                    pT_copy(3)
                if has(c):
                    after(dve, "c_T", c)
                    nc.vector.tensor_copy(c_xnT[:, :], bank[6][:, 0:T]).then_inc(S["c_xTc"], 1)
                if has(a):
                    row_rec(1)
                if has(c):
                    for n, (h0, h1) in enumerate(CH):
                        s = bank[2 + n][:, 0:(h1 - h0) * NK].rearrange("p (h k) -> p h k", k=NK)
                        after(dve, "c_sc", c, n + 1)
                        nc.vector.reduce_max(c_max[:, h0:h1], s, AX_X).then_inc(S["c_mx"], 1)
                        after(dve, "c_mx", c, n + 1)
                        nc.vector.tensor_tensor(c_p[:, h0:h1, :], s, c_max[:, h0:h1].rearrange("p (h k) -> p h k", k=1).broadcast_to([T, h1 - h0, NK]),
                                                ALU.subtract).then_inc(S["c_sb"], 1)
                if has(d):
                    after(dve, "c_bo", d)
                    after(dve, "d_y", d)
                    rows = xs[:, bass.ds(d * C, C)]
                    nc.vector.tensor_tensor(rows, bank[6][:, 0:C], rows, ALU.add).then_inc(S["d_x2"], 1)
                if has(e):
                    after(dve, "r_lg", e)
                    nc.vector.tensor_copy(r_log[:, :], bank[7][:, 0:E]).then_inc(S["r_lgc"], 1)
                if has(c):
                    after(dve, "c_ex", c)
                    nc.vector.reduce_sum(c_sum[:, :], c_p[:, :, :], AX_X).then_inc(S["c_sm"], 1)
                    after(dve, "c_sm", c)
                    nc.vector.reciprocal(c_rec[:, :], c_sum[:, :]).then_inc(S["c_rc"], 1)
                if has(e):
                    plain_wait()
                    after(dve, "r_lgc", e)
                    nc.vector.max(r_top[:, :], r_log[:, :]).then_inc(S["r_mx"], 1)
                    plain_wait()
                    after(dve, "r_mx", e)
                    nc.vector.max_index(r_idx[:, :], r_top[:, :], r_log[:, :]).then_inc(S["r_ix"], 1)
                    after(dve, "r_ix", e)
                    nc.vector.tensor_copy(pick[:, bass.ds(e, 1)], r_idx[:, 0:1]).then_inc(S["r_pk"], 1)
                if has(a):
                    after(dve, "b_y", a)
                    rows = xs[:, bass.ds(a * C, C)]
                    nc.vector.tensor_tensor(rows, bank[6][:, 0:C], rows, ALU.add).then_inc(S["b_x1"], 1)

            def shared_gate(half):
                if half == 0:
                    dve.wait_ge(zeroed, 16)
                for k in range(HK):
                    n = half * HK + k
                    bu, bg = SH_BANK[half][2 * k:2 * k + 2]
                    dve.wait_ge(s_tanh, n + 1)
                    nc.vector.scalar_tensor_tensor(out=s_hu[n % 2][:, :], in0=s_th[n % 2][:, :], scalar=1.0, in1=bank[bu][:, :], op0=ALU.add, op1=ALU.mult).then_inc(s_up, 1)
                    dve.wait_ge(s_up, n + 1)
                    nc.vector.scalar_tensor_tensor(out=s_hT[:, k, half * 512:(half + 1) * 512], in0=s_hu[n % 2][:, :], scalar=0.5, in1=bank[bg][:, :],
                                                   op0=ALU.mult, op1=ALU.mult).then_inc(s_h, 1)

            dve.wait_ge(ld["sort"], 32)
            nc.vector.tensor_copy(tri_bf[:, :], tri_in[:, :]).then_inc(sort_c, 1)
            pipeline(dve, body)

            shared_gate(0)

            dve.wait_ge(sort_c, 4)
            dve.wait_ge(S["r_pk"], NB)
            ids = steps_s[:, 0:E].rearrange("p (b e) -> p b e", b=1)
            nc.vector.tensor_tensor(hot[:, :, :], pick[:, :].rearrange("p (b e) -> p b e", e=1).broadcast_to([T, NB, E]),
                                    ids.broadcast_to([T, NB, E]), ALU.is_equal).then_inc(sort_d, 1)
            dve.wait_ge(sort_d, 1)
            nc.vector.tensor_copy(hot_bf[:, 0:NB, :], hot[:, :, :]).then_inc(sort_d, 1)
            count = bank[0][:, NB * E:(NB + 1) * E]
            dve.wait_ge(ranked, 1)
            nc.vector.tensor_tensor(full[:, :, :], count.rearrange("p (e k) -> p e k", k=1).broadcast_to([T, E, E]),
                                    steps_s[:, E:2 * E].rearrange("p (e k) -> p e k", e=1).broadcast_to([T, E, E]), ALU.is_gt).then_inc(sort_d, 1)
            dve.wait_ge(sort_d, 3)
            nc.vector.reduce_sum(n_tiles[:, :], full[:, :, :], AX_X).then_inc(sort_d, 1)
            dve.wait_ge(sort_d, 4)
            nc.vector.tensor_tensor_scan(tile_end[:, :], one_row[:, :], n_tiles[:, :], 0.0, ALU.mult, ALU.add).then_inc(sort_d, 1)
            dve.wait_ge(sort_d, 5)
            nc.vector.tensor_tensor(start[:, :], tile_end[:, :], n_tiles[:, :], ALU.subtract).then_inc(sort_d, 1)
            dve.wait_ge(sort_d, 6)
            nc.vector.scalar_tensor_tensor(out=place[:, :, :], in0=start[:, :].rearrange("p (b e) -> p b e", b=1).broadcast_to([T, NB, E]), scalar=float(P),
                                           in1=bank[0][:, 0:NB * E].rearrange("p (b e) -> p b e", b=NB), op0=ALU.mult, op1=ALU.add).then_inc(sort_d, 1)
            dve.wait_ge(sort_d, 7)
            nc.vector.tensor_tensor(hot[:, :, :], place[:, :, :], hot[:, :, :], ALU.mult).then_inc(sort_d, 1)
            dve.wait_ge(sort_d, 8)
            nc.vector.reduce_sum(slot_f[:, :], hot[:, :, :], AX_X).then_inc(sort_d, 1)
            dve.wait_ge(sort_d, 9)
            nc.vector.tensor_scalar(slot[:, :], slot_f[:, :], -1.0, None, ALU.add).then_inc(slots_ready, 1)
            nc.vector.tensor_tensor(done_by[:, :, :], steps_s[:, 2 * E:2 * E + NT].rearrange("p (n e) -> p n e", e=1).broadcast_to([T, NT, E]),
                                    tile_end[:, :].rearrange("p (n e) -> p n e", n=1).broadcast_to([T, NT, E]), ALU.is_ge).then_inc(sort_d, 1)
            dve.wait_ge(sort_d, 10)
            nc.vector.reduce_sum(owner_f[:, :], done_by[:, :, :], AX_X).then_inc(sort_d, 1)
            dve.wait_ge(sort_d, 11)
            nc.vector.tensor_scalar(owner[:, :], owner_f[:, :], float(E - 1), None, ALU.min).then_inc(owners_ready, 1)

            shared_gate(1)
            for half in range(2):
                dve.wait_ge(s_dn, half + 1)
                rows = xs[:, half * 512:(half + 1) * 512]
                nc.vector.tensor_tensor(rows, bank[SH_OUT[half]][:, :], rows, ALU.add).then_inc(s_add, 1)

            def step(s, n):
                if tile(s, 3):
                    dve.wait_ge(f_hT, s - 2)
                    reach(dve, f_dn, s - 4)
                    nc.vector.tensor_copy(hT[(n + 1) % 2][:, :, :], bank[4 + (n + 1) % 2][:, 0:HK * P].rearrange("p (k t) -> p k t", k=HK)).then_inc(f_hTc, 1)
                if tile(s, 1):
                    m = (n + 1) % 2
                    dve.wait_ge(f_th, s)
                    nc.vector.scalar_tensor_tensor(out=hu[m][:, :], in0=th[m][:, :], scalar=1.0, in1=bank[2 + m][:, 0:HID], op0=ALU.add, op1=ALU.mult).then_inc(f_hu, 1)
                    dve.wait_ge(f_hu, s)
                    reach(dve, f_hT, s - 2)
                    nc.vector.scalar_tensor_tensor(out=hg[m][:, :], in0=hu[m][:, :], scalar=0.5, in1=bank[2 + m][:, HID:2 * HID], op0=ALU.mult, op1=ALU.mult).then_inc(f_h, 1)

            tiles(dve, step)
            dve.wait_ge(s_add, 2)
            for b in range(NB):
                dve.wait_ge(gathered[b], 16)
                nc.vector.tensor_tensor(yt[:, b, :], yt[:, b, :], xs[:, b * C:(b + 1) * C], ALU.add).then_inc(final, 1)

        @block.tensor
        def _(pe):
            mm = nc.tensor.matmul
            pe.wait_ge(ld["qk"], 32)
            for h in range(H):
                last = mm(bank[0][:, h * L:(h + 1) * L], wqT_s[:, h, :], wkuT_s[:, :], start=True, stop=True)
            last.then_inc(su_q, 1)
            pe.wait_ge(ld["const"], 32)
            for b in range(NB):
                pe.wait_ge(ln1_ready, 2 * NB + 2 + b)
                last = nc.tensor.transpose(bank[6 + b // 4][:, b % 4 * T:(b % 4 + 1) * T], a_xn[:, b, :], identity[:, :])
                if b % 4 == 3:
                    last.then_inc(su_T, 1)
            pe.wait_ge(ld["xqk"], 32)
            for n in range(4):
                half, odd = n // 2, n % 2
                for k in range(4):
                    p = slice(odd * XD, odd * XD + XD)
                    last = mm(bank[2 + n][0:CC, k * C:(k + 1) * C], xwkT_s[p, half * 4 + k, :], xwqT_s[p, half * 4 + k, :], start=True, stop=True)
                last.then_inc(su_x, 1)
            pe.wait_ge(su_Tc, 2)
            pe.wait_ge(ld["kv"], 32)
            for b in range(NB):
                last = mm(bank[1][:, b * KV * L:(b + 1) * KV * L], a_xnT[:, b * T:(b + 1) * T], wvd_s[:, :], start=True, stop=True)
            last.then_inc(su_v, 1)
            pe.wait_ge(su_qc, 1)
            pe.wait_ge(ld["wo"], 32)
            for h in range(H):
                g, r = h // REP, h % REP
                last = mm(bank[0][r * L:(r + 1) * L, g * C:(g + 1) * C], wvuT_s[:, :], wo_s[:, h, :], start=True, stop=True)
            last.then_inc(su_y, 1)

            def g_mm(half):
                for h in range(XH):
                    n = half * XH + h
                    if n >= 4:
                        pe.wait_ge((su_gA, su_gD)[h % 2], (n - 4) // 2 + 1)
                    mm(bank[G_BANK[h % 4]][:, 0:HALF], xqk_w[:, h, :], ctxT_s[:, half * HALF:(half + 1) * HALF], start=True, stop=True).then_inc(su_g, 1)

            pe.wait_ge(su_xA, 2)
            pe.wait_ge(su_xD, 2)
            pe.wait_ge(ld["ctx"], 16)
            g_mm(0)
            pe.wait_ge(consts_ready, 5)
            pe.wait_ge(su_vc, 1)
            pe.wait_ge(su_yc, 1)
            pe.wait_ge(su_gA, XH // 2)
            pe.wait_ge(su_gD, XH // 2)

            def body(i):
                a, c, d, e = i, i - 1, i - 2, i - 3

                def pT(g):
                    after(pe, "c_nr", d, g + 1)
                    if g == 3:
                        after(pe, "d_pA", d, 1)
                    for k in range(4):
                        last = nc.tensor.transpose(bank[PT_BANK[g]][0:NK, k * T:(k + 1) * T], c_p[:, 4 * g + k, :], identity[:, :])
                    last.then_inc(S["d_pT"], 1)

                def pv(g):
                    after(pe, ("d_pA", "d_pD")[g % 2], d, g // 2 + 1)
                    if g == 0:
                        after(pe, "v_c0", d)
                        after(pe, "v_c1", d)
                    if g >= 2:
                        after(pe, "d_oc", d, g - 1)
                    if g == 1:
                        after(pe, "v_c1", d)
                    for k in range(4):
                        h = 4 * g + k
                        o = k % 2 * XD
                        last = mm(bank[O_BANK[g]][o:o + XD, k // 2 * T:(k // 2 + 1) * T], xv_s[:, h * XD:(h + 1) * XD], c_pT[:, h, :], start=True, stop=True)
                    last.then_inc(S["d_o"], 1)

                def scores(g):
                    if g == 0:
                        after(pe, "a_qc", a)
                        after(pe, "a_k0c", a)
                        after(pe, "b_pc", a - 1)
                    else:
                        after(pe, "a_k1c", a)
                    mm(bank[g][:, :], identity_bf[:, :], causal[:, :, :].rearrange("p r t -> p (r t)"), start=True, stop=False)
                    mm(bank[g][:, :], q_s[:, g, :], k_bd[:, g, :, :].rearrange("p r t -> p (r t)"), start=False, stop=True).then_inc(S["a_sc"], 1)

                if has(a):
                    after(pe, "v_c0", a - 2)
                    xnT = a_xnT[:, bass.ds(a * T, T)]
                    for g in range(KV):
                        mm(bank[5][:, g * T:(g + 1) * T], qlat_w[:, g * P:(g + 1) * P], xnT, start=True, stop=True)
                    mm(bank[5][:, 2 * T:3 * T], wkd_rep[:, 0, :, :].rearrange("c r l -> c (r l)"), xnT, start=True, stop=True).then_inc(S["a_qk0"], 1)
                    after(pe, "b_pc", a - 1)
                    mm(bank[1][:, 0:T], wkd_rep[:, 1, :, :].rearrange("c r l -> c (r l)"), xnT, start=True, stop=True).then_inc(S["a_k1"], 1)
                if first(i):
                    g_mm(1)
                if has(d):
                    pT(0)
                    pT(1)
                if has(a):
                    scores(0)
                if has(d):
                    if has(a):
                        after(pe, "a_qc", a)
                        after(pe, "a_k0c", a)
                    pv(0)
                if has(a):
                    scores(1)
                if has(d):
                    pT(2)
                    pv(1)
                    pT(3)
                    pv(2)
                if has(c):
                    after(pe, "c_xnd", c)
                    after(pe, "b_x1", c)
                    nc.tensor.transpose(bank[6][:, 0:T], c_xn[:, :], identity[:, :]).then_inc(S["c_T"], 1)
                if has(d):
                    pv(3)
                if has(c):
                    after(pe, "c_xTc", c)
                    for n, (h0, h1) in enumerate(CH):
                        if n == 0 or n == 1:
                            after(pe, "d_pD", c - 1, 2 - n)
                        else:
                            after(pe, "d_pA", c - 1, 2)
                        if first(i - 1):
                            pe.wait_ge(su_gA, XH)
                            pe.wait_ge(su_gD, XH)
                        mm(bank[2 + n][:, 0:(h1 - h0) * NK], c_xnT[:, :], G[:, bass.ds((c * XH + h0) * NK, (h1 - h0) * NK)],
                           start=True, stop=True).then_inc(S["c_sc"], 1)
                if has(e):
                    after(pe, "r_xnd", e)
                    after(pe, "d_oc", e + 1)
                    nc.tensor.transpose(bank[7][:, 0:T], r_xn[:, :], identity[:, :]).then_inc(S["r_T"], 1)
                if has(d):
                    after(pe, "c_xTc", d + 1)
                    for k in range(XP):
                        if k % 2 == 0:
                            after(pe, "d_oc", d, k // 2 + 1)
                        last = mm(bank[6][:, 0:C], c_oT[:, k, :], xwo_s[:, k, :], start=(k == 0), stop=(k == XP - 1))
                    last.then_inc(S["d_y"], 1)
                if has(e):
                    after(pe, "r_Tc", e)
                    mm(bank[7][:, 0:E], r_xnT[:, :], router_w[:, :], start=True, stop=True).then_inc(S["r_lg"], 1)
                if isinstance(i, int) and i == NB + 1:
                    shared_up(0)
                if has(a):
                    for g in range(2):
                        after(pe, "a_nr", a, g + 1)
                        for k in range(REP):
                            last = nc.tensor.transpose(bank[g][:, k * T:(k + 1) * T], a_p[:, g * REP + k, :], identity[:, :])
                        last.then_inc(S["b_pT"], 1)
                if has(c):
                    after(pe, "v_in", c)
                    after(pe, "d_oc", c - 1)
                    mm(bank[5][0:NK, :], ctx_b[:, :], xwv_s[:, 0:512], start=True, stop=True).then_inc(S["v_mm"], 1)
                if has(a):
                    after(pe, "d_x2", a - 2)
                    after(pe, "a_v", a)
                    for g in range(2):
                        after(pe, "b_pc", a, g + 1)
                        for k in range(REP):
                            last = mm(bank[6][k * L:(k + 1) * L, g * T:(g + 1) * T], v_s[:, g * L:(g + 1) * L], a_pT[:, g * REP + k, :], start=True, stop=True)
                    last.then_inc(S["b_o"], 1)
                if has(c):
                    after(pe, "r_lgc", c - 2)
                    mm(bank[7][0:NK, :], ctx_b[:, :], xwv_s[:, 512:1024], start=True, stop=True).then_inc(S["v_mm"], 1)
                if has(a):
                    after(pe, "b_oc", a)
                    for g in range(KV):
                        last = mm(bank[6][:, 0:C], a_oT[:, g, :], ylat_w[:, g, :], start=(g == 0), stop=(g == KV - 1))
                    last.then_inc(S["b_y"], 1)

            def shared_up(half):
                if half == 0:
                    pe.wait_ge(ld["shared"], 32)
                pe.wait_ge(S["r_keep"], NB * (half + 1))
                tokens = xnT_all[:, half * 512:(half + 1) * 512]
                for k in range(HK):
                    bu, bg = SH_BANK[half][2 * k:2 * k + 2]
                    mm(bank[bu][:, :], ugs_w[:, k * P:(k + 1) * P], tokens, start=True, stop=True)
                    mm(bank[bg][:, :], ugs_w[:, HID + k * P:HID + (k + 1) * P], tokens, start=True, stop=True).then_inc(s_ug, 1)

            def shared_down():
                for b in range(NB):
                    half = b // 4
                    if b % 4 == 0:
                        pe.wait_ge(s_h, HK * (half + 1))
                    for k in range(HK):
                        last = mm(bank[SH_OUT[half]][:, b % 4 * C:(b % 4 + 1) * C], s_hT[:, k, b * T:(b + 1) * T], dns_w[:, k, :],
                                  start=(k == 0), stop=(k == HK - 1))
                    if b % 4 == 3:
                        last.then_inc(s_dn, 1)

            pe.wait_ge(ld["xwv"], 16)
            pe.wait_ge(ld["xwo"], 16)
            pe.wait_ge(ld["router"], 16)
            pipeline(pe, body)

            pe.wait_ge(sort_c, 4)
            pe.wait_ge(sort_d, 2)
            mm(bank[0][:, 0:(NB + 1) * E], tri_bf[:, :], hot_bf[:, :, :].rearrange("p b e -> p (b e)"), start=True, stop=False)
            for b in range(NB):
                left = NB - b
                last = mm(bank[0][:, (b + 1) * E:(NB + 1) * E], ones_bf[:, :], hot_bf[:, b:b + 1, :].broadcast_to([T, left, E]),
                          start=False, stop=(b == NB - 1))
            last.then_inc(ranked, 1)

            shared_up(1)
            shared_down()

            pe.wait_ge(owners_ready, 1)
            pe.wait_ge(s_add, 2)
            pe.wait_ge(ld["ug"], 16)
            pe.wait_ge(ld["dn"], 16)

            def expert_of(k):
                return pe.value_load(owner[0:1, bass.ds(k, 1)], min_val=0, max_val=E - 1)

            def step(s, n):
                m = (n + 1) % 2
                if tile(s, 1):
                    up_expert = expert_of(s - 1)
                if tile(s, 3):
                    down_expert = expert_of(s - 3)
                    pe.wait_ge(f_h, s - 2)
                    reach(pe, f_hTc, s - 4)
                    for k in range(HK):
                        last = nc.tensor.transpose(bank[4 + m][:, k * P:(k + 1) * P], hg[m][:, k * P:(k + 1) * P], identity[:, :])
                    last.then_inc(f_hT, 1)
                if tile(s, 0):
                    pe.wait_ge(f_ld[n], store_count(s))
                    nc.tensor.transpose(bank[n % 2][:, 0:P], xg[n][:, :], identity[:, :]).then_inc(f_T, 1)
                if tile(s, 1):
                    pe.wait_ge(f_Tc, s)
                    reach(pe, f_h, s - 2)
                    mm(bank[2 + m][:, :], xgT[m][:, :], ug_w[:, bass.ds(up_expert * (2 * HID), 2 * HID)], start=True, stop=True).then_inc(f_ug, 1)
                if tile(s, 3):
                    pe.wait_ge(f_hTc, s - 2)
                    reach(pe, f_y, s - 4)
                    for k in range(HK):
                        last = mm(bank[6 + m][:, 0:C], hT[m][:, k, :], dn_w[:, bass.ds(down_expert * (HK * C) + k * C, C)], start=(k == 0), stop=(k == HK - 1))
                    last.then_inc(f_dn, 1)

            tiles(pe, step)


def kernel(**inputs):
    import numpy as np
    import concourse.bacc as bacc
    from concourse.bass_utils import run_bass_kernel_spmd as run

    nc = bacc.Bacc("TRN2", target_bir_lowering=False, num_devices=1)
    a = {k: np.asarray(v) for k, v in inputs.items()}
    flat = np.ascontiguousarray
    T = a["x"].shape[1]
    CC = a["ctx_768"].shape[2]
    P = 128
    sent = {
        "x": flat(a["x"]),
        "ctxT": flat(a["ctx_768"].reshape(-1, CC).T),
        "wqT": flat(a["L0_attn_wq"].reshape(-1, 8, 128).transpose(2, 1, 0)),
        "wkd": flat(a["L0_attn_wk_down"]), "wvd": flat(a["L0_attn_wv_down"]),
        "wkuT": flat(a["L0_attn_wk_up"].T), "wvuT": flat(a["L0_attn_wv_up"].T), "wo": flat(a["L0_attn_wo"]),
        "xwqT": flat(a["L0_xattn_Wq"].T.reshape(8, P, -1).transpose(1, 0, 2)),
        "xwkT": flat(a["L0_xattn_Wk"].T.reshape(8, P, -1).transpose(1, 0, 2)),
        "xwv": flat(a["L0_xattn_Wv"]), "xwo": flat(a["L0_xattn_Wo"]), "xbo": flat(a["L0_xattn_bo"]),
        "ug": flat(np.concatenate([a["L0_ffn_up"], a["L0_ffn_gate"]], axis=1).transpose(2, 0, 1)),
        "dn": flat(a["L0_ffn_down"].transpose(2, 0, 1).reshape(2, P, 8, P).transpose(1, 2, 0, 3).reshape(P, 8, 2 * P)),
        "router": flat(a["L0_ffn_router"].T),
        "ug_s": flat(np.concatenate([a["L0_ffn_w_up_s"], a["L0_ffn_w_gate_s"]]).T),
        "dn_s": flat(a["L0_ffn_w_down_s"].T.reshape(2, P, P).transpose(1, 0, 2)),
        "ident": np.eye(P, dtype=np.float32),
        "mask": np.where(np.tril(np.ones((T, T), bool)), 0.0, -3.0e38).astype(np.float32),
        "tri": np.triu(np.ones((P, P), np.float32)),
        "steps": np.concatenate([np.arange(8), np.arange(8) * P, np.arange((1024 - 8) // P + 8)]).astype(np.float32),
    }
    aps = {k: nc.dram_tensor("in_" + k, v.shape, mybir.dt.from_np(v.dtype), kind="ExternalInput").ap() for k, v in sent.items()}
    out = nc.dram_tensor("out", a["x"].shape, F32, kind="ExternalOutput").ap()
    build_layer(nc, *aps.values(), out)
    r = run(nc, [{"in_" + k: v for k, v in sent.items()}], core_ids=[0])
    return r.results[0]["out"]
```

```python
from contextlib import ExitStack

import concourse.bass as bass
from concourse import mybir

F32 = mybir.dt.float32
F32R = mybir.dt.float32r
BF16 = mybir.dt.bfloat16
I32 = mybir.dt.int32
U32 = mybir.dt.uint32
ALU = mybir.AluOpType
ACT = mybir.ActivationFunctionType
AX_X = mybir.AxisListType.X


def build_layer(nc, x, ctxT, wqT, wkd, wvd, wkuT, wvuT, wo, xwqT, xwkT, xwv, xwo, xbo, ug, dn, router, ug_s, dn_s, ident, mask, tri, steps, tokens, out):
    P = 128
    NB, T, C = x.shape
    CC, NK = ctxT.shape[0], ctxT.shape[1] // NB
    H = wqT.shape[1]
    L = wkuT.shape[1]
    KV = wkd.shape[1] // L
    REP = H // KV
    XH = 16
    XD = xwv.shape[1] // XH
    XP = XH // 2
    SCALE = float(wqT.shape[0]) ** -0.5
    XSCALE = float(XD) ** -0.5
    EPS = 1e-5
    HALF = NB // 2 * NK
    E = router.shape[1]
    HID = ug.shape[2] // 2
    HK = HID // P
    NT = (NB * T - E) // P + E
    PAIR = NB * T // P + 1
    BLOCKS = 1 + E // 2 * PAIR
    RW = 2 * C + 1
    NO_TOKEN = 4.0 * NB * T
    PACK = 8
    NTP = -(-NT // PACK) * PACK
    NCONST = 5 * E + NTP + NTP * E + NTP
    CH = [(0, 5), (5, 10), (10, XH)]

    with ExitStack() as ctx:
        def sb(name, shape, dt=F32):
            return ctx.enter_context(nc.sbuf_tensor(name, shape, dt))

        def sem(name):
            return ctx.enter_context(nc.semaphore(name))

        bank = [ctx.enter_context(nc.psum_tensor(f"bank{n}", [P, 512], F32)) for n in range(8)]

        identity = sb("identity", [P, P])
        identity_bf = sb("identity_bf", [P, P], BF16)
        causal = sb("causal", [P, REP, T], BF16)
        causal_in = sb("causal_in", [P, T])
        group_rows = sb("group_rows", [P, REP])
        minus_half = sb("minus_half", [P, 1])
        ctxT_s = sb("ctxT_s", [CC, NB * NK])
        wqT_s = sb("wqT_s", [P, H, C])
        wkuT_s = sb("wkuT_s", [P, L])
        wvuT_s = sb("wvuT_s", [P, L])
        wo_s = sb("wo_s", [P, H, C])
        wkd_s = sb("wkd_s", [C, KV * L])
        wkd_rep = sb("wkd_rep", [C, KV, REP, L])
        wvd_s = sb("wvd_s", [C, KV * L])
        xwqT_s = sb("xwqT_s", [P, XP, C])
        xwkT_s = sb("xwkT_s", [P, XP, CC])
        xwv_s = sb("xwv_s", [CC, XH * XD])
        xwo_s = sb("xwo_s", [P, XP, C])
        ug_w = sb("ug_w", [C, E * 2 * HID])
        dn_w = sb("dn_w", [P, E * HK * C])
        router_w = sb("router_w", [C, E])
        ugs_w = sb("ugs_w", [C, 2 * HID])
        dns_w = sb("dns_w", [P, HK, C])
        tri_in = sb("tri_in", [P, P])
        tri_bf = sb("tri_bf", [P, P], BF16)
        ones_bf = sb("ones_bf", [P, P], BF16)
        fill_row = sb("fill_row", [P, RW])
        token_ids = sb("token_ids", [T, NB])
        sort_s = sb("sort_s", [P, NCONST])
        ids_c = sort_s[:, 0:E]
        fills_c = sort_s[:, E:2 * E]
        row_c = sort_s[:, 2 * E:3 * E]
        sign_c = sort_s[:, 3 * E:4 * E]
        block_c = sort_s[:, 4 * E:5 * E]
        tile_c = sort_s[:, 5 * E:5 * E + NTP]
        tile_sign_c = sort_s[:, 5 * E + NTP:5 * E + NTP + NTP * E]
        pow_c = sort_s[:, 5 * E + NTP + NTP * E:NCONST]
        bo_row = sb("bo_row", [P, C])
        qlat_w = sb("qlat_w", [C, H * L])
        ylat_w = sb("ylat_w", [P, KV, C])
        xqk_w = [sb("xqk_" + n, [CC, XH, C], F32R) for n in ("hi", "lo")]
        ctx_w = [sb("ctx_" + n, [CC, NB * NK], F32R) for n in ("hi", "lo")]
        xwv_w = [sb("xwv_" + n, [CC, XH * XD], F32R) for n in ("hi", "lo")]
        G = sb("G", [C, NB * XH * NK])
        G4 = G[:, :].rearrange("c (b h k) -> c b h k", b=NB, h=XH)

        xs = sb("xs", [T, NB * C])
        a_stat = sb("a_stat", [T, NB, 6])
        a_mv = sb("a_mv", [T, NB, 2])
        a_ve = sb("a_ve", [T, NB])
        a_rstd = sb("a_rstd", [T, NB])
        a_xn = sb("a_xn", [T, NB, C])
        a_xnT = sb("a_xnT", [C, NB * T])
        v_all = sb("v_all", [T, NB * KV * L])
        c_stat = sb("c_stat", [T, 6])
        c_mv = sb("c_mv", [T, 2])
        c_ve = sb("c_ve", [T, 1])
        c_rstd = sb("c_rstd", [T, 1])
        q_s = sb("q_s", [P, KV, T])
        k_bd = sb("k_bd", [P, KV, REP, T])
        v_s = sb("v_s", [T, KV * L])
        a_max = sb("a_max", [T, H])
        a_nmax = sb("a_nmax", [T, H])
        a_sum = sb("a_sum", [T, H])
        a_rec = sb("a_rec", [T, H])
        a_p = sb("a_p", [T, H, T])
        a_pT = sb("a_pT", [T, H, T])
        a_oT = sb("a_oT", [P, KV, T])
        c_xn = sb("c_xn", [T, C])
        c_xnT = sb("c_xnT", [C, T])
        c_max = sb("c_max", [T, XH])
        c_sum = sb("c_sum", [T, XH])
        c_rec = sb("c_rec", [T, XH])
        c_p = sb("c_p", [T, XH, NK])
        c_pT = sb("c_pT", [NK, XH, T])
        ctx_b = [sb("ctx_b_" + n, [CC, NK], F32R) for n in ("hi", "lo")]
        xv_s = sb("xv_s", [NK, XH * XD])
        c_oT = sb("c_oT", [P, XP, T])

        r_stat = sb("r_stat", [T, 6])
        r_mv = sb("r_mv", [T, 2])
        r_ve = sb("r_ve", [T, 1])
        r_rstd = sb("r_rstd", [T, 1])
        r_xn = sb("r_xn", [T, C])
        rows_s = [sb(f"rows_s{n}", [T, RW]) for n in range(2)]
        r_xnT = sb("r_xnT", [C, T])
        r_log = sb("r_log", [T, E])
        r_top = sb("r_top", [T, 8])
        r_idx = sb("r_idx", [T, 8], U32)
        pick = sb("pick", [T, 1])
        hot = sb("hot", [T, E], BF16)
        seen = sb("seen", [T, E], BF16)
        s_th = sb("s_th", [P, HID])
        s_hu = sb("s_hu", [P, HID])
        s_hT = sb("s_hT", [P, HK, T])
        place = sb("place", [T, 3, E])
        slot_f = sb("slot_f", [T, 1])
        slots_s = [sb(f"slots_s{n}", [T, 1], U32) for n in range(2)]
        full = sb("full", [T, E, E])
        n_tiles = sb("n_tiles", [T, E])
        tile_end = sb("tile_end", [T, E])
        one_row = sb("one_row", [T, E])
        start = sb("start", [T, E])
        base = sb("base", [T, E])
        signed = sb("signed", [T, E])
        done_by = sb("done_by", [T, NTP, E])
        begun_by = sb("begun_by", [T, NTP, E])
        block_f = sb("block_f", [T, NTP, E])
        block_sum = sb("block_sum", [T, NTP])
        block_of = sb("block_of", [T, NTP], I32)
        owner_f = sb("owner_f", [T, NTP])
        owner_c = sb("owner_c", [T, NTP])
        packed_f = sb("packed_f", [T, NTP // PACK])
        packed = sb("packed", [T, NTP // PACK], I32)
        RING = 4
        xg_all = G[:, 0:NT * RW]
        ids = [sb(f"ids{n}", [P, 1], U32) for n in range(RING)]
        xgT = [sb(f"xgT{n}", [C, P]) for n in range(2)]
        th = [sb(f"th{n}", [P, HID]) for n in range(2)]
        hu = [sb(f"hu{n}", [P, HID]) for n in range(2)]
        hg = [sb(f"hg{n}", [P, HID]) for n in range(2)]
        hT = [sb(f"hT{n}", [P, HK, P]) for n in range(2)]
        yg = [sb(f"yg{n}", [P, C]) for n in range(RING)]
        x_slots = nc.dram_tensor("x_slots", (BLOCKS * P, RW), F32).ap()

        ld = {n: sem("ld_" + n) for n in ("x", "const", "kv", "bo", "qk", "ctx", "xqk", "wo", "xwv", "xwo", "ug", "dn", "router", "shared", "sort")}
        half_ready = sem("half_ready")
        consts_ready = sem("consts_ready")
        ln1_ready = sem("ln1_ready")
        ln1_rstd = sem("ln1_rstd")
        su_q = sem("su_q")
        su_qc = sem("su_qc")
        su_T = sem("su_T")
        su_Tc = sem("su_Tc")
        su_v = sem("su_v")
        su_vc = sem("su_vc")
        su_x = sem("su_x")
        su_xA = sem("su_xA")
        su_xD = sem("su_xD")
        ctx_split = sem("ctx_split")
        xwv_split = sem("xwv_split")
        su_g = sem("su_g")
        su_gA = sem("su_gA")
        su_gD = sem("su_gD")
        su_y = sem("su_y")
        su_yc = sem("su_yc")
        names = dict(
            a_v=1, a_qk0=1, a_k1=1, a_qc=1, a_k0c=4, a_k1c=1, a_sc=2, a_mx=2, a_nm=2, a_ex=8, a_rc=2, a_nr=2,
            b_pT=2, b_pc=2, b_o=1, b_oc=1, b_y=1, b_x1=1,
            v_in=2, v_mm=2, v_c0=1, v_c1=1,
            c_st=1, c_mvd=1, c_ved=1, c_rs=1, c_xnd=1, c_bo=1, c_T=1, c_xTc=1, c_sc=3, c_mx=3, c_sb=3, c_ex=3, c_sm=1, c_rc=1, c_nr=4,
            r_st=1, r_mvd=1, r_ved=1, r_rs=1, r_xnd=1, r_T=1, r_Tc=1, r_lg=1, r_lgc=1, r_mx=1, r_ix=1, r_pk=1, r_hot=1,
            s_ug=1, s_tanh=1, s_up=1, s_h=1,
            g_xn=1, g_rk=1, g_dn=1, g_res=1, g_pl=4, g_slot=1, g_seen=1, g_id=1, g_sc=16,
            d_pT=4, d_pA=2, d_pD=2, d_o=4, d_oc=4, d_y=1, d_x2=1)
        S = {n: sem(n) for n in names}

        def after(eng, name, j, count=None):
            n = names[name]
            c = n if count is None else count
            if isinstance(j, int):
                if j < 0:
                    return
                j, c = (NB - 1, n) if j >= NB else (j, c)
            eng.wait_ge(S[name], j * n + c)

        zeroed = sem("zeroed")
        zero_src = sem("zero_src")
        ones_ready = sem("ones_ready")
        sort_c = sem("sort_c")
        sort_d = sem("sort_d")
        blocks_ready = sem("blocks_ready")
        owners_ready = sem("owners_ready")
        f_ld = [sem(f"f_ld{n}") for n in range(RING)]
        f_T = sem("f_T")
        f_Tc = sem("f_Tc")
        f_ug = sem("f_ug")
        f_th = sem("f_th")
        f_hu = sem("f_hu")
        f_h = sem("f_h")
        f_hT = sem("f_hT")
        f_hTc = sem("f_hTc")
        f_dn = sem("f_dn")
        f_y = sem("f_y")
        f_st = [sem(f"f_st{n}") for n in range(RING)]
        f_id = sem("f_id")

        block = ctx.enter_context(nc.Block())

        def pipeline(eng, body):
            for i in range(4):
                body(i)
            with eng.Fori(4, NB) as i:
                body(i)
            for i in range(NB, NB + 4):
                body(i)

        def tiles(eng, step, lag=3):
            full_at = RING + 3
            rounds = (NT - full_at) // RING
            for s in range(full_at):
                step(s, s % RING)
            with eng.Fori(0, rounds) as r:
                for n in range(full_at, full_at + RING):
                    step(r * RING + n, n % RING)
            for s in range(full_at + rounds * RING, NT + lag):
                step(s, s % RING)

        def tile(s, ago):
            k = s - ago
            return not isinstance(k, int) or 0 <= k < NT

        def store_count(k):
            return k // RING * 16 + 16

        def reach(eng, semaphore, value):
            if not isinstance(value, int) or value > 0:
                eng.wait_ge(semaphore, value)

        def has(j):
            return not isinstance(j, int) or 0 <= j < NB

        def first(i):
            return isinstance(i, int) and i == 0

        G_BANK = (2, 3, 4, 7)
        PT_BANK = (2, 3, 4, 2)
        O_BANK = (5, 7, 5, 7)

        def qk_heads(rows, n):
            h0 = n // 2 * XP + n % 2
            return rows[:, h0:h0 + 7:2, :]

        def last_batch(j):
            return int(isinstance(j, int) and j == NB - 1)

        def draining(i):
            return isinstance(i, int) and i > NB

        def shared_out(i):
            return bank[1 if draining(i - 1) else 6][:, T:2 * T]

        @block.sync
        def _(sp):
            sp.dma_start(xs[:, :].rearrange("t (b c) -> t b c", b=NB), x.rearrange("b t c -> t b c")).then_inc(ld["x"], 16)
            sp.dma_start(identity[:, :], ident).then_inc(ld["const"], 16)
            sp.dma_start(causal_in[:, :], mask).then_inc(ld["const"], 16)
            sp.dma_start(xwkT_s[:, :, :], xwkT).then_inc(ld["xqk"], 16)
            sp.dma_start(xwqT_s[:, :, :], xwqT).then_inc(ld["xqk"], 16)
            sp.dma_start(xwv_s[:, :], xwv).then_inc(ld["xwv"], 16)
            sp.dma_start(xwo_s[:, :, :], xwo.rearrange("(k p) c -> p k c", p=P)).then_inc(ld["xwo"], 16)
            sp.dma_start(router_w[:, :], router).then_inc(ld["router"], 16)
            sp.dma_start(tri_in[:, :], tri).then_inc(ld["sort"], 16)
            sp.dma_start(sort_s[:, :], steps.rearrange("(a c) -> a c", a=1).broadcast_to([P, NCONST])).then_inc(ld["sort"], 16)
            sp.dma_start(token_ids[:, :], tokens).then_inc(ld["sort"], 16)
            sp.dma_start(ugs_w[:, :], ug_s).then_inc(ld["shared"], 16)
            sp.dma_start(dns_w[:, :, :], dn_s).then_inc(ld["shared"], 16)
            sp.dma_start(ug_w[:, :].rearrange("c (e n) -> c e n", e=E), ug).then_inc(ld["ug"], 16)
            sp.dma_start(dn_w[:, :].rearrange("p (e n) -> p e n", e=E), dn).then_inc(ld["dn"], 16)
            sp.wait_ge(zero_src, 2)
            sp.dma_start(x_slots.rearrange("(n p) c -> p n c", p=P),
                         fill_row[:, :].rearrange("p (n c) -> p n c", n=1).broadcast_to([P, BLOCKS, RW])).then_inc(zeroed, 16)
            sp.wait_ge(blocks_ready, 1)
            first_blocks = [sp.value_load(block_of[0:1, k:k + 1], min_val=0, max_val=BLOCKS - 1) for k in range(RING)]
            sp.wait_ge(S["g_sc"], 16 * NB)

            def step(s, n):
                reach(sp, f_T, s - RING + 1)
                if isinstance(s, int) and s < RING:
                    at = first_blocks[s]
                else:
                    at = sp.value_load(block_of[0:1, bass.ds(s, 1)], min_val=0, max_val=BLOCKS - 1)
                sp.dma_start(xg_all[:, bass.ds(s * RW, RW)], x_slots[bass.ds(at * P, P), :]).then_inc(f_ld[n], 16)

            tiles(sp, step, 0)

        @block.scalar
        def _(act):
            act.dma_start(wkuT_s[:, :], wkuT).then_inc(ld["qk"], 16)
            act.dma_start(wqT_s[:, :, :], wqT).then_inc(ld["qk"], 16)
            act.dma_start(wkd_s[:, :], wkd).then_inc(ld["kv"], 16)
            act.dma_start(wvd_s[:, :], wvd).then_inc(ld["kv"], 16)
            act.dma_start(ctxT_s[:, :], ctxT).then_inc(ld["ctx"], 16)
            act.dma_start(wvuT_s[:, :], wvuT).then_inc(ld["wo"], 16)
            act.dma_start(wo_s[:, :, :], wo.rearrange("(h p) c -> p h c", p=P)).then_inc(ld["wo"], 16)
            act.dma_start(bo_row[:, :], xbo.rearrange("(a c) -> a c", a=1).broadcast_to([P, C])).then_inc(ld["bo"], 16)

            def g_copy(half, h):
                act.wait_ge(su_g, half * XH + h + 1)
                nc.scalar.copy(G4[:, half * NB // 2:(half + 1) * NB // 2, h, :],
                               bank[G_BANK[h % 4]][:, 0:HALF].rearrange("p (b k) -> p b k", k=NK)).then_inc(su_gA, 1)

            act.wait_ge(su_q, 1)
            nc.scalar.copy(qlat_w[:, :], bank[0][:, 0:H * L]).then_inc(su_qc, 1)
            for n in (0, 1):
                act.wait_ge(su_T, n + 1)
                nc.scalar.copy(a_xnT[:, n * 512:(n + 1) * 512], bank[6 + n][:, :]).then_inc(su_Tc, 1)
            for n in range(4):
                act.wait_ge(su_x, n + 1)
                nc.scalar.copy(qk_heads(xqk_w[0], n), bank[2 + n][0:CC, :].rearrange("p (h c) -> p h c", h=4)).then_inc(su_xA, 1)
            for h in range(0, XH, 2):
                g_copy(0, h)

            def body(i):
                a, c, d, e, f = i, i - 1, i - 2, i - 3, i - 4
                if has(a):
                    after(act, "a_qk0", a)
                    after(act, "a_sc", a - 1)
                    nc.scalar.copy(q_s[:, :, :], bank[5][:, 0:KV * T].rearrange("p (g t) -> p g t", g=KV)).then_inc(S["a_qc"], 1)
                    for r in range(REP):
                        p = slice(r * L, (r + 1) * L)
                        nc.scalar.copy(k_bd[p, 0, r, :], bank[5][p, 2 * T:3 * T]).then_inc(S["a_k0c"], 1)

                if first(i):
                    g_copy(1, 0)

                def pT_copy(g):
                    after(act, "d_pT", d, g + 1)
                    nc.scalar.copy(c_pT[:, 4 * g:4 * g + 4, :], bank[PT_BANK[g]][0:NK, :].rearrange("p (h t) -> p h t", h=4)).then_inc(S["d_pA"], 1)

                def o_copy(g):
                    after(act, "d_o", d, g + 1)
                    nc.scalar.copy(c_oT[:, 2 * g:2 * g + 2, :], bank[O_BANK[g]][:, 0:2 * T].rearrange("p (h t) -> p h t", h=2)).then_inc(S["d_oc"], 1)

                def exps(h0, h1):
                    if not has(a):
                        return
                    g = h0 // REP
                    after(act, "a_nm", a, g + 1)
                    if h0 == 0:
                        after(act, "b_pT", a - 1)
                    for h in range(h0, h1):
                        nc.scalar.activation(a_p[:, h, :], bank[g][:, h % REP * T:h % REP * T + T], ACT.Exp,
                                             bias=a_nmax[:, h:h + 1], scale=SCALE, accum_out=a_sum[:, h:h + 1]).then_inc(S["a_ex"], 1)

                if has(d):
                    pT_copy(0)
                    o_copy(0)
                    pT_copy(2)
                exps(0, 2)
                if has(d):
                    o_copy(1)
                exps(2, 4)
                if first(i):
                    g_copy(1, 2)
                exps(4, 5)
                if has(d):
                    o_copy(2)
                exps(5, 6)
                if has(d):
                    o_copy(3)
                exps(6, 8)
                if first(i):
                    for h in range(4, 12, 2):
                        g_copy(1, h)
                if has(e):
                    after(act, "r_T", e)
                    after(act, "s_ug", e - 1)
                    nc.scalar.copy(r_xnT[:, :], bank[7][:, 0:T]).then_inc(S["r_Tc"], 1)
                def c_exp(n):
                    if has(c):
                        h0, h1 = CH[n]
                        after(act, "c_sb", c, n + 1)
                        nc.scalar.activation(c_p[:, h0:h1, :], c_p[:, h0:h1, :], ACT.Exp, scale=XSCALE).then_inc(S["c_ex"], 1)

                def a_pT_copy(g):
                    if has(a):
                        after(act, "b_pT", a, g + 1)
                        nc.scalar.copy(a_pT[:, g * REP:(g + 1) * REP, :], bank[g][:, :].rearrange("p (h t) -> p h t", h=REP)).then_inc(S["b_pc"], 1)

                c_exp(0)
                c_exp(1)
                a_pT_copy(0)
                a_pT_copy(1)
                c_exp(2)
                if first(i):
                    g_copy(1, 12)
                if has(c):
                    after(act, "v_mm", c, 1)
                    nc.scalar.copy(xv_s[:, 0:512], bank[5][0:NK, :]).then_inc(S["v_c0"], 1)
                if has(a):
                    after(act, "b_o", a)
                    nc.scalar.copy(a_oT[:, :, :], bank[6][:, 0:KV * T].rearrange("p (g t) -> p g t", g=KV)).then_inc(S["b_oc"], 1)
                if first(i):
                    g_copy(1, 14)
                if has(c):
                    after(act, "v_mm", c, 2)
                    nc.scalar.copy(xv_s[:, 512:1024], bank[7][0:NK, :]).then_inc(S["v_c1"], 1)
                if has(e):
                    after(act, "s_ug", e)
                    after(act, "s_up", e - 1)
                    nc.scalar.activation(s_th[:, :], bank[4][:, HK * T:2 * HK * T], ACT.Tanh, scale=0.5).then_inc(S["s_tanh"], 1)
                    after(act, "r_xnd", e)
                    if not last_batch(e):
                        after(act, "g_sc", e - 1)
                    nc.scalar.copy(rows_s[last_batch(e)][:, 0:C], r_xn[:, :]).then_inc(S["g_xn"], 1)

            pipeline(act, body)

            def step(s, n):
                if tile(s, 3):
                    act.wait_ge(f_hT, s - 2)
                    reach(act, f_dn, s - 4)
                    nc.scalar.copy(hT[(n + 1) % 2][:, :, :], bank[4 + (n + 1) % 2][:, 0:HK * P].rearrange("p (k t) -> p k t", k=HK)).then_inc(f_hTc, 1)
                if tile(s, 0):
                    act.wait_ge(f_T, s + 1)
                    reach(act, f_ug, s - 1)
                    nc.scalar.copy(xgT[n % 2][:, :], bank[n % 2][:, 0:P]).then_inc(f_Tc, 1)
                if tile(s, 1):
                    act.wait_ge(f_ug, s)
                    reach(act, f_hu, s - 2)
                    nc.scalar.activation(th[(n + 1) % 2][:, :], bank[2 + (n + 1) % 2][:, HID:2 * HID], ACT.Tanh, scale=0.5).then_inc(f_th, 1)

            tiles(act, step)

        @block.gpsimd
        def _(pool):
            nc.gpsimd.memset(minus_half[:, :], -0.5).then_inc(half_ready, 1)
            pool.wait_ge(half_ready, 1)
            pool.wait_ge(ln1_ready, 2 * NB + 1)
            nc.gpsimd.tensor_tensor(a_rstd[:, :], a_ve[:, :], minus_half[:, :].broadcast_to([T, NB]), ALU.pow).then_inc(ln1_rstd, 1)
            pool.wait_ge(ld["xwv"], 16)
            nc.gpsimd.tensor_copy(xwv_w[0][:, :], xwv_s[:, :]).then_inc(xwv_split, 1)
            pool.wait_ge(xwv_split, 1)
            nc.gpsimd.tensor_tensor(xwv_w[1][:, :], xwv_s[:, :], xwv_w[0][:, :], ALU.subtract).then_inc(xwv_split, 1)
            pool.wait_ge(ld["ctx"], 16)
            pool.wait_ge(ld["bo"], 16)
            pool.wait_ge(su_vc, 1)
            pool.wait_ge(ld["sort"], 48)

            pool.wait_ge(ctx_split, 2)

            def plain_wait():
                pool.wait_ge(ld["ctx"], 16)

            def body(i):
                a, c, d, e, f = i, i - 1, i - 2, i - 3, i - 4
                if has(c):
                    after(pool, "c_ved", c)
                    nc.gpsimd.tensor_tensor(c_rstd[:, :], c_ve[:, :], minus_half[:, :], ALU.pow).then_inc(S["c_rs"], 1)
                if has(a):
                    after(pool, "b_o", a - 1)
                    nc.gpsimd.tensor_copy(v_s[:, :], v_all[:, bass.ds(a * (KV * L), KV * L)]).then_inc(S["a_v"], 1)
                if has(c):
                    after(pool, "v_mm", c - 1)
                    for n in range(2):
                        nc.gpsimd.tensor_copy(ctx_b[n][:, :], ctx_w[n][:, bass.ds(c * NK, NK)]).then_inc(S["v_in"], 1)
                    after(pool, "c_xnd", c)
                    rows = xs[:, bass.ds(c * C, C)]
                    nc.gpsimd.tensor_tensor(rows, rows, bo_row[:, :], ALU.add).then_inc(S["c_bo"], 1)
                if has(e):
                    after(pool, "r_ved", e)
                    nc.gpsimd.tensor_tensor(r_rstd[:, :], r_ve[:, :], minus_half[:, :], ALU.pow).then_inc(S["r_rs"], 1)
                if has(a):
                    for g in range(2):
                        after(pool, "a_rc", a, g + 1)
                        h = slice(g * REP, (g + 1) * REP)
                        nc.gpsimd.tensor_tensor(a_p[:, h, :], a_p[:, h, :], a_rec[:, h].rearrange("p (h t) -> p h t", t=1).broadcast_to([T, REP, T]),
                                                ALU.mult).then_inc(S["a_nr"], 1)
                if isinstance(i, int) and i == 3:
                    pool.wait_ge(zeroed, 16)
                if has(f):
                    nc_id = token_ids[:, bass.ds(f, 1)]
                    plain_wait()
                    after(pool, "g_xn", f)
                    nc.gpsimd.tensor_copy(rows_s[last_batch(f)][:, 2 * C:RW], nc_id).then_inc(S["g_id"], 1)
                    plain_wait()
                    after(pool, "g_id", f)
                    after(pool, "g_res", f)
                    after(pool, "g_slot", f)
                    nc.gpsimd.indirect_dma_start(out=x_slots, out_offset=bass.IndirectOffsetOnAxis(ap=slots_s[last_batch(f)][:, :], axis=0),
                                                 in_=rows_s[last_batch(f)][:, :], in_offset=None).then_inc(S["g_sc"], 16)
                if has(c):
                    after(pool, "c_rc", c)
                    for g in range(4):
                        h = slice(g * 4, g * 4 + 4)
                        nc.gpsimd.tensor_tensor(c_p[:, h, :], c_p[:, h, :], c_rec[:, h].rearrange("p (h t) -> p h t", t=1).broadcast_to([T, 4, NK]),
                                                ALU.mult).then_inc(S["c_nr"], 1)

            pipeline(pool, body)

            out_rows = out.rearrange("b t c -> (b t) c")
            last_token = pool.to_reg(NB * T - 1)

            def step(s, n):
                plain_wait()
                pool.wait_ge(f_T, s + 1)
                if tile(s, RING):
                    pool.wait_ge(f_st[n], store_count(s - RING))
                nc.gpsimd.tensor_copy(ids[n][:, :], xg_all[:, bass.ds(s * RW + 2 * C, 1)]).then_inc(f_id, 1)
                plain_wait()
                pool.wait_ge(f_id, s + 1)
                pool.wait_ge(f_y, s + 1)
                nc.gpsimd.indirect_dma_start(out=out_rows, out_offset=bass.IndirectOffsetOnAxis(ap=ids[n][:, :], axis=0),
                                             in_=yg[n][:, :], in_offset=None, bounds_check=last_token, oob_is_err=False).then_inc(f_st[n], 16)

            tiles(pool, step, 0)
            for n in range(RING):
                pool.wait_ge(f_st[n], 16 * len(range(n, NT, RING)))

        @block.vector
        def _(dve):
            nc.vector.memset(ones_bf[:, :], 1.0).then_inc(ones_ready, 1)
            nc.vector.memset(k_bd[:, :, :, :], 0.0).then_inc(consts_ready, 1)
            nc.vector.memset(fill_row[:, 0:2 * C], 0.0).then_inc(zero_src, 1)
            nc.vector.memset(fill_row[:, 2 * C:RW], NO_TOKEN).then_inc(zero_src, 1)
            nc.vector.memset(seen[:, :], 0.0).then_inc(sort_c, 1)
            nc.vector.memset(one_row[:, :], 1.0).then_inc(sort_c, 1)
            dve.wait_ge(ld["x"], 16)
            for b in range(NB):
                nc.vector.bn_stats(a_stat[:, b, :], xs[:, b * C:(b + 1) * C]).then_inc(ln1_ready, 1)
            for b in range(NB):
                dve.wait_ge(ln1_ready, NB)
                nc.vector.bn_aggr(a_mv[:, b, :], a_stat[:, b, :]).then_inc(ln1_ready, 1)
            dve.wait_ge(ln1_ready, 2 * NB)
            nc.vector.tensor_scalar(a_ve[:, :], a_mv[:, :, 1], EPS, None, ALU.add).then_inc(ln1_ready, 1)
            dve.wait_ge(ld["const"], 32)
            nc.vector.tensor_copy(identity_bf[:, :], identity[:, :]).then_inc(consts_ready, 1)
            nc.vector.tensor_copy(causal[:, :, :], causal_in[:, :].rearrange("p (a t) -> p a t", a=1).broadcast_to([P, REP, T])).then_inc(consts_ready, 1)
            nc.vector.tensor_reduce(group_rows[:, :], identity[:, :].rearrange("p (r l) -> p r l", l=L), AX_X, ALU.add).then_inc(consts_ready, 1)
            dve.wait_ge(ld["kv"], 32)
            nc.vector.tensor_copy(wkd_rep[:, :, :, :], wkd_s[:, :].rearrange("p (g a l) -> p g a l", g=KV, a=1).broadcast_to([C, KV, REP, L])).then_inc(consts_ready, 1)
            dve.wait_ge(ln1_rstd, 1)
            for b in range(NB):
                nc.vector.tensor_scalar(a_xn[:, b, :], xs[:, b * C:(b + 1) * C], a_mv[:, b, 0:1], a_rstd[:, b:b + 1],
                                        ALU.subtract, ALU.mult).then_inc(ln1_ready, 1)
            dve.wait_ge(consts_ready, 5)

            def plain_wait():
                dve.wait_ge(ld["x"], 16)

            def g_copy(half, h):
                dve.wait_ge(su_g, half * XH + h + 1)
                nc.vector.tensor_copy(G4[:, half * NB // 2:(half + 1) * NB // 2, h, :],
                                      bank[G_BANK[h % 4]][:, 0:HALF].rearrange("p (b k) -> p b k", k=NK)).then_inc(su_gD, 1)

            dve.wait_ge(ld["ctx"], 16)
            nc.vector.tensor_copy(ctx_w[0][:, :], ctxT_s[:, :]).then_inc(ctx_split, 1)
            dve.wait_ge(ctx_split, 1)
            nc.vector.tensor_tensor(ctx_w[1][:, :], ctxT_s[:, :], ctx_w[0][:, :], ALU.subtract).then_inc(ctx_split, 1)
            for n in range(4):
                dve.wait_ge(su_xA, n + 1)
                nc.vector.tensor_tensor(qk_heads(xqk_w[1], n), bank[2 + n][0:CC, :].rearrange("p (h c) -> p h c", h=4), qk_heads(xqk_w[0], n),
                                        ALU.subtract).then_inc(su_xD, 1)
            dve.wait_ge(ld["sort"], 48)
            nc.vector.tensor_copy(tri_bf[:, :], tri_in[:, :]).then_inc(sort_c, 1)
            dve.wait_ge(su_v, 1)
            nc.vector.tensor_copy(v_all[:, :], bank[1][:, 0:NB * KV * L]).then_inc(su_vc, 1)
            dve.wait_ge(su_y, 1)
            nc.vector.tensor_copy(ylat_w[:, :, :], bank[0][:, 0:KV * C].rearrange("p (g c) -> p g c", g=KV)).then_inc(su_yc, 1)
            for h in range(1, XH, 2):
                g_copy(0, h)

            def body(i):
                a, c, d, e, f = i, i - 1, i - 2, i - 3, i - 4
                if has(c):
                    crows = xs[:, bass.ds(c * C, C)]
                    after(dve, "b_x1", c)
                    nc.vector.bn_stats(c_stat[:, :], crows).then_inc(S["c_st"], 1)
                    plain_wait()
                    after(dve, "c_st", c)
                    nc.vector.bn_aggr(c_mv[:, :], c_stat[:, :]).then_inc(S["c_mvd"], 1)
                    after(dve, "c_mvd", c)
                    nc.vector.tensor_scalar(c_ve[:, :], c_mv[:, 1:2], EPS, None, ALU.add).then_inc(S["c_ved"], 1)
                erows = xs[:, bass.ds(e * C, C)] if has(e) else None

                def choose(j):
                    plain_wait()
                    after(dve, "r_lgc", j)
                    nc.vector.max(r_top[:, :], r_log[:, :]).then_inc(S["r_mx"], 1)
                    plain_wait()
                    after(dve, "r_mx", j)
                    nc.vector.max_index(r_idx[:, :], r_top[:, :], r_log[:, :]).then_inc(S["r_ix"], 1)
                    after(dve, "r_ix", j)
                    nc.vector.tensor_copy(pick[:, :], r_idx[:, 0:1]).then_inc(S["r_pk"], 1)
                    after(dve, "r_pk", j)
                    nc.vector.tensor_scalar(hot[:, :], ids_c, pick[:, 0:1], None, ALU.is_equal).then_inc(S["r_hot"], 1)

                def third_statistics():
                    after(dve, "d_x2", e)
                    nc.vector.bn_stats(r_stat[:, :], erows).then_inc(S["r_st"], 1)
                    plain_wait()
                    after(dve, "r_st", e)
                    nc.vector.bn_aggr(r_mv[:, :], r_stat[:, :]).then_inc(S["r_mvd"], 1)
                    after(dve, "r_mvd", e)
                    nc.vector.tensor_scalar(r_ve[:, :], r_mv[:, 1:2], EPS, None, ALU.add).then_inc(S["r_ved"], 1)

                def gate():
                    after(dve, "s_tanh", f)
                    nc.vector.scalar_tensor_tensor(out=s_hu[:, :], in0=s_th[:, :], scalar=1.0, in1=bank[4][:, 0:HK * T], op0=ALU.add, op1=ALU.mult).then_inc(S["s_up"], 1)
                    after(dve, "s_up", f)
                    nc.vector.scalar_tensor_tensor(out=s_hT[:, :, :].rearrange("p k t -> p (k t)"), in0=s_hu[:, :], scalar=0.5, in1=bank[4][:, HK * T:2 * HK * T],
                                                   op0=ALU.mult, op1=ALU.mult).then_inc(S["s_h"], 1)

                def signed_rank():
                    after(dve, "g_rk", f)
                    nc.vector.tensor_tensor(place[:, 0, :], bank[6][:, 2 * T:2 * T + E], sign_c, ALU.mult).then_inc(S["g_pl"], 1)

                def residual():
                    after(dve, "g_dn", f)
                    nc.vector.tensor_tensor(rows_s[last_batch(f)][:, C:2 * C], shared_out(i), xs[:, bass.ds(f * C, C)], ALU.add).then_inc(S["g_res"], 1)

                def slots():
                    after(dve, "g_pl", f, 1)
                    nc.vector.tensor_tensor(place[:, 1, :], place[:, 0, :], row_c, ALU.add).then_inc(S["g_pl"], 1)
                    after(dve, "g_pl", f, 2)
                    nc.vector.tensor_tensor(place[:, 2, :], place[:, 1, :], hot[:, :], ALU.mult).then_inc(S["g_pl"], 1)
                    after(dve, "g_pl", f, 3)
                    nc.vector.reduce_sum(slot_f[:, :], place[:, 2, :], AX_X).then_inc(S["g_pl"], 1)
                    after(dve, "g_pl", f, 4)
                    if not last_batch(f):
                        after(dve, "g_xn", f)
                    nc.vector.tensor_copy(slots_s[last_batch(f)][:, :], slot_f[:, :]).then_inc(S["g_slot"], 1)
                    nc.vector.tensor_tensor(seen[:, :], seen[:, :], hot[:, :], ALU.add).then_inc(S["g_seen"], 1)

                if isinstance(i, int) and i == NB + 3:
                    choose(f)
                    signed_rank()
                    gate()
                    slots()
                    residual()
                    tile_counts()
                    tile_blocks()
                    return
                if has(e) and not has(c):
                    third_statistics()
                if has(a):
                    after(dve, "a_k1", a)
                    after(dve, "a_sc", a - 1)
                    nc.vector.tensor_tensor(k_bd[:, 1, :, :], bank[1][:, 0:T].rearrange("p (a t) -> p a t", a=1).broadcast_to([P, REP, T]),
                                            group_rows[:, :].rearrange("p (r a) -> p r a", a=1).broadcast_to([P, REP, T]), ALU.mult).then_inc(S["a_k1c"], 1)
                if first(i):
                    g_copy(1, 1)

                def pT_copy(g):
                    after(dve, "d_pT", d, g + 1)
                    nc.vector.tensor_copy(c_pT[:, 4 * g:4 * g + 4, :], bank[PT_BANK[g]][0:NK, :].rearrange("p (h t) -> p h t", h=4)).then_inc(S["d_pD"], 1)

                def row_max(g):
                    after(dve, "a_sc", a, g + 1)
                    hs = slice(g * REP, (g + 1) * REP)
                    nc.vector.reduce_max(a_max[:, hs], bank[g][:, :].rearrange("p (h t) -> p h t", h=REP), AX_X).then_inc(S["a_mx"], 1)
                    after(dve, "a_mx", a, g + 1)
                    nc.vector.tensor_scalar(a_nmax[:, hs], a_max[:, hs], -SCALE, None, ALU.mult).then_inc(S["a_nm"], 1)

                def row_rec(g):
                    hs = slice(g * REP, (g + 1) * REP)
                    after(dve, "a_ex", a, REP * (g + 1))
                    nc.vector.reciprocal(a_rec[:, hs], a_sum[:, hs]).then_inc(S["a_rc"], 1)

                if has(f):
                    gate()
                if has(c):
                    after(dve, "c_rs", c)
                    nc.vector.tensor_scalar(c_xn[:, :], crows, c_mv[:, 0:1], c_rstd[:, 0:1], ALU.subtract, ALU.mult).then_inc(S["c_xnd"], 1)
                if has(d):
                    pT_copy(1)
                if has(a):
                    row_max(0)
                if has(e) and has(c):
                    third_statistics()
                if has(a):
                    row_max(1)
                if has(d):
                    pT_copy(3)
                if has(e):
                    after(dve, "r_rs", e)
                    after(dve, "g_xn", e - 1)
                    nc.vector.tensor_scalar(r_xn[:, :], erows, r_mv[:, 0:1], r_rstd[:, 0:1], ALU.subtract, ALU.mult).then_inc(S["r_xnd"], 1)
                if has(f) and draining(i - 1):
                    choose(f)
                if has(c):
                    after(dve, "c_T", c)
                    nc.vector.tensor_copy(c_xnT[:, :], bank[6][:, 0:T]).then_inc(S["c_xTc"], 1)
                if has(f) and draining(i - 1):
                    signed_rank()
                    slots()
                    residual()
                elif has(f):
                    residual()
                    signed_rank()
                    slots()
                if first(i):
                    for h in range(3, 12, 2):
                        g_copy(1, h)
                        if h in (5, 9):
                            row_rec(h // 8)
                    g_copy(1, 13)
                    g_copy(1, 15)
                elif has(a):
                    row_rec(0)
                if has(a) and not first(i):
                    row_rec(1)
                if has(c):
                    for n, (h0, h1) in enumerate(CH):
                        s = bank[2 + n][:, 0:(h1 - h0) * NK].rearrange("p (h k) -> p h k", k=NK)
                        after(dve, "c_sc", c, n + 1)
                        nc.vector.reduce_max(c_max[:, h0:h1], s, AX_X).then_inc(S["c_mx"], 1)
                        after(dve, "c_mx", c, n + 1)
                        nc.vector.tensor_tensor(c_p[:, h0:h1, :], s, c_max[:, h0:h1].rearrange("p (h k) -> p h k", k=1).broadcast_to([T, h1 - h0, NK]),
                                                ALU.subtract).then_inc(S["c_sb"], 1)
                if has(d):
                    after(dve, "c_bo", d)
                    after(dve, "d_y", d)
                    rows = xs[:, bass.ds(d * C, C)]
                    nc.vector.tensor_tensor(rows, bank[6][:, 0:C], rows, ALU.add).then_inc(S["d_x2"], 1)
                if has(e):
                    after(dve, "r_lg", e)
                    nc.vector.tensor_copy(r_log[:, :], bank[7][:, 0:E]).then_inc(S["r_lgc"], 1)
                if has(c):
                    after(dve, "c_ex", c)
                    nc.vector.reduce_sum(c_sum[:, :], c_p[:, :, :], AX_X).then_inc(S["c_sm"], 1)
                    after(dve, "c_sm", c)
                    nc.vector.reciprocal(c_rec[:, :], c_sum[:, :]).then_inc(S["c_rc"], 1)
                if has(e) and not draining(i):
                    choose(e)
                if has(a):
                    after(dve, "b_y", a)
                    rows = xs[:, bass.ds(a * C, C)]
                    nc.vector.tensor_tensor(rows, bank[6][:, 0:C], rows, ALU.add).then_inc(S["b_x1"], 1)

            def tile_counts():
                count = bank[6][:, 2 * T + E:2 * T + 2 * E]
                nc.vector.tensor_tensor(full[:, :, :], count.rearrange("p (e k) -> p e k", k=1).broadcast_to([T, E, E]),
                                        fills_c.rearrange("p (e k) -> p e k", e=1).broadcast_to([T, E, E]), ALU.is_gt).then_inc(sort_d, 1)
                dve.wait_ge(sort_d, 1)
                nc.vector.reduce_sum(n_tiles[:, :], full[:, :, :], AX_X).then_inc(sort_d, 1)
                dve.wait_ge(sort_d, 2)
                nc.vector.tensor_tensor_scan(tile_end[:, :], one_row[:, :], n_tiles[:, :], 0.0, ALU.mult, ALU.add).then_inc(sort_d, 1)
                dve.wait_ge(sort_d, 3)
                nc.vector.tensor_tensor(start[:, :], tile_end[:, :], n_tiles[:, :], ALU.subtract).then_inc(sort_d, 1)
                dve.wait_ge(sort_d, 4)

            def tile_blocks():
                nc.vector.tensor_tensor(signed[:, :], start[:, :], sign_c, ALU.mult).then_inc(sort_d, 1)

                def per_tile(row):
                    return row.rearrange("p (n e) -> p n e", n=1).broadcast_to([T, NTP, E])

                tile_n = tile_c.rearrange("p (n e) -> p n e", e=1).broadcast_to([T, NTP, E])
                nc.vector.tensor_tensor(done_by[:, :, :], tile_n, per_tile(tile_end[:, :]), ALU.is_ge).then_inc(sort_d, 1)
                nc.vector.tensor_tensor(begun_by[:, :, :], tile_n, per_tile(start[:, :]), ALU.is_ge).then_inc(sort_d, 1)
                dve.wait_ge(sort_d, 7)
                nc.vector.tensor_tensor(base[:, :], block_c, signed[:, :], ALU.subtract).then_inc(sort_d, 1)
                nc.vector.tensor_tensor(begun_by[:, :, :], begun_by[:, :, :], done_by[:, :, :], ALU.subtract).then_inc(sort_d, 1)
                dve.wait_ge(sort_d, 9)
                nc.vector.tensor_tensor(block_f[:, :, :], tile_sign_c.rearrange("p (n e) -> p n e", n=NTP), per_tile(base[:, :]), ALU.add).then_inc(sort_d, 1)
                dve.wait_ge(sort_d, 10)
                nc.vector.tensor_tensor(block_f[:, :, :], block_f[:, :, :], begun_by[:, :, :], ALU.mult).then_inc(sort_d, 1)
                dve.wait_ge(sort_d, 11)
                nc.vector.reduce_sum(block_sum[:, :], block_f[:, :, :], AX_X).then_inc(sort_d, 1)
                dve.wait_ge(sort_d, 12)
                nc.vector.tensor_copy(block_of[:, :], block_sum[:, :]).then_inc(blocks_ready, 1)
                nc.vector.reduce_sum(owner_f[:, :], done_by[:, :, :], AX_X).then_inc(sort_d, 1)
                dve.wait_ge(sort_d, 13)
                nc.vector.tensor_scalar(owner_c[:, :], owner_f[:, :], float(E - 1), None, ALU.min).then_inc(sort_d, 1)
                dve.wait_ge(sort_d, 14)
                nc.vector.tensor_tensor(owner_c[:, :], owner_c[:, :], pow_c, ALU.mult).then_inc(sort_d, 1)
                dve.wait_ge(sort_d, 15)
                nc.vector.reduce_sum(packed_f[:, :], owner_c[:, :].rearrange("p (w n) -> p w n", n=PACK), AX_X).then_inc(sort_d, 1)
                dve.wait_ge(sort_d, 16)
                nc.vector.tensor_copy(packed[:, :], packed_f[:, :]).then_inc(owners_ready, 1)

            pipeline(dve, body)

            def step(s, n):
                m = (n + 1) % 2
                if tile(s, 1):
                    dve.wait_ge(f_th, s)
                    nc.vector.scalar_tensor_tensor(out=hu[m][:, :], in0=th[m][:, :], scalar=1.0, in1=bank[2 + m][:, 0:HID], op0=ALU.add, op1=ALU.mult).then_inc(f_hu, 1)
                    dve.wait_ge(f_hu, s)
                    reach(dve, f_hT, s - 2)
                    nc.vector.scalar_tensor_tensor(out=hg[m][:, :], in0=hu[m][:, :], scalar=0.5, in1=bank[2 + m][:, HID:2 * HID], op0=ALU.mult, op1=ALU.mult).then_inc(f_h, 1)
                if tile(s, 3):
                    k, r = s - 3, (n + 1) % RING
                    dve.wait_ge(f_dn, k + 1)
                    if tile(s, 3 + RING):
                        dve.wait_ge(f_st[r], store_count(k - RING))
                    nc.vector.tensor_tensor(yg[r][:, :], bank[6 + m][:, 0:C], xg_all[:, bass.ds(k * RW + C, C)], ALU.add).then_inc(f_y, 1)

            tiles(dve, step)

        @block.tensor
        def _(pe):
            mm = nc.tensor.matmul

            def mm_split(result, a, b):
                mm(result, a[0], b[0], start=True, stop=False)
                mm(result, a[0], b[1], start=False, stop=False)
                return mm(result, a[1], b[0], start=False, stop=True)


            def warm_up(products):
                for _ in range(products):
                    mm(bank[7][:, :].rearrange("p (a t) -> p a t", t=P), ones_bf[:, :],
                       ones_bf[:, :].rearrange("p (a t) -> p a t", a=1).broadcast_to([P, 4, P]), start=True, stop=True)

            pe.wait_ge(ones_ready, 1)
            warm_up(16)
            pe.wait_ge(ld["qk"], 32)
            for h in range(H):
                last = mm(bank[0][:, h * L:(h + 1) * L], wqT_s[:, h, :], wkuT_s[:, :], start=True, stop=True)
            last.then_inc(su_q, 1)
            pe.wait_ge(ld["const"], 32)
            for b in range(NB):
                pe.wait_ge(ln1_ready, 2 * NB + 2 + b)
                last = nc.tensor.transpose(bank[6 + b // 4][:, b % 4 * T:(b % 4 + 1) * T], a_xn[:, b, :], identity[:, :])
                if b % 4 == 3:
                    last.then_inc(su_T, 1)
            pe.wait_ge(ld["xqk"], 32)
            for n in range(4):
                half, odd = n // 2, n % 2
                for k in range(4):
                    p = slice(odd * XD, odd * XD + XD)
                    last = mm(bank[2 + n][0:CC, k * C:(k + 1) * C], xwkT_s[p, half * 4 + k, :], xwqT_s[p, half * 4 + k, :], start=True, stop=True)
                last.then_inc(su_x, 1)
            pe.wait_ge(su_Tc, 2)
            pe.wait_ge(ld["kv"], 32)
            for b in range(NB):
                last = mm(bank[1][:, b * KV * L:(b + 1) * KV * L], a_xnT[:, b * T:(b + 1) * T], wvd_s[:, :], start=True, stop=True)
            last.then_inc(su_v, 1)
            pe.wait_ge(su_qc, 1)
            pe.wait_ge(ld["wo"], 32)
            for h in range(H):
                g, r = h // REP, h % REP
                last = mm(bank[0][r * L:(r + 1) * L, g * C:(g + 1) * C], wvuT_s[:, :], wo_s[:, h, :], start=True, stop=True)
            last.then_inc(su_y, 1)

            def g_mm(half, h0=0, h1=XH):
                for h in range(h0, h1):
                    n = half * XH + h
                    if n >= 4:
                        pe.wait_ge((su_gA, su_gD)[h % 2], (n - 4) // 2 + 1)
                    mm_split(bank[G_BANK[h % 4]][:, 0:HALF], [w[:, h, :] for w in xqk_w], [w[:, half * HALF:(half + 1) * HALF] for w in ctx_w]).then_inc(su_g, 1)

            pe.wait_ge(su_xA, 4)
            pe.wait_ge(su_xD, 4)
            pe.wait_ge(ctx_split, 2)
            g_mm(0)
            pe.wait_ge(consts_ready, 5)
            pe.wait_ge(su_vc, 1)
            pe.wait_ge(su_yc, 1)

            def body(i):
                a, c, d, e, f = i, i - 1, i - 2, i - 3, i - 4

                def pT(g):
                    after(pe, "c_nr", d, g + 1)
                    if g == 2:
                        after(pe, "s_h", d - 2)
                    if g == 3:
                        after(pe, "d_pA", d, 1)
                    for k in range(4):
                        last = nc.tensor.transpose(bank[PT_BANK[g]][0:NK, k * T:(k + 1) * T], c_p[:, 4 * g + k, :], identity[:, :])
                    last.then_inc(S["d_pT"], 1)

                def pv(g):
                    after(pe, ("d_pA", "d_pD")[g % 2], d, g // 2 + 1)
                    if g == 0:
                        after(pe, "v_c0", d)
                        after(pe, "v_c1", d)
                    if g >= 2:
                        after(pe, "d_oc", d, g - 1)
                    if g == 1:
                        after(pe, "v_c1", d)
                    for k in range(4):
                        h = 4 * g + k
                        o = k % 2 * XD
                        last = mm(bank[O_BANK[g]][o:o + XD, k // 2 * T:(k // 2 + 1) * T], xv_s[:, h * XD:(h + 1) * XD], c_pT[:, h, :], start=True, stop=True)
                    last.then_inc(S["d_o"], 1)

                def scores(g):
                    if g == 0:
                        after(pe, "a_qc", a)
                        after(pe, "a_k0c", a)
                        after(pe, "b_pc", a - 1)
                    else:
                        after(pe, "a_k1c", a)
                    mm(bank[g][:, :], identity_bf[:, :], causal[:, :, :].rearrange("p r t -> p (r t)"), start=True, stop=False)
                    mm(bank[g][:, :], q_s[:, g, :], k_bd[:, g, :, :].rearrange("p r t -> p (r t)"), start=False, stop=True).then_inc(S["a_sc"], 1)

                if has(a):
                    after(pe, "v_c0", a - 2)
                    xnT = a_xnT[:, bass.ds(a * T, T)]
                    for g in range(KV):
                        mm(bank[5][:, g * T:(g + 1) * T], qlat_w[:, g * P:(g + 1) * P], xnT, start=True, stop=True)
                    mm(bank[5][:, 2 * T:3 * T], wkd_rep[:, 0, :, :].rearrange("c r l -> c (r l)"), xnT, start=True, stop=True).then_inc(S["a_qk0"], 1)
                if has(a):
                    after(pe, "b_pc", a - 1)
                    mm(bank[1][:, 0:T], wkd_rep[:, 1, :, :].rearrange("c r l -> c (r l)"), xnT, start=True, stop=True).then_inc(S["a_k1"], 1)
                if first(i):
                    g_mm(1, 0, 2)
                if has(d):
                    pT(0)
                    pT(1)
                if has(a):
                    scores(0)
                if has(d):
                    if has(a):
                        after(pe, "a_qc", a)
                        after(pe, "a_k0c", a)
                    pv(0)
                if has(a):
                    scores(1)
                if first(i):
                    g_mm(1, 2, 12)
                if has(d):
                    pT(2)
                    pv(1)
                    pT(3)
                    pv(2)
                def transpose_third():
                    after(pe, "r_xnd", e)
                    after(pe, "d_oc", e + 1)
                    nc.tensor.transpose(bank[7][:, 0:T], r_xn[:, :], identity[:, :]).then_inc(S["r_T"], 1)

                if has(e) and not has(d):
                    transpose_third()
                if has(f):
                    after(pe, "r_hot", f)
                    after(pe, "b_x1", f + 3)
                    mm(bank[6][:, 2 * T:2 * T + E], tri_bf[:, :], hot[:, :], start=True, stop=False)
                    last = mm(bank[6][:, 2 * T:2 * T + E], ones_bf[:, :], seen[:, :], start=False, stop=True)
                    if isinstance(i, int) and i == NB + 3:
                        mm(bank[6][:, 2 * T + E:2 * T + 2 * E], ones_bf[:, :], hot[:, :], start=True, stop=False)
                        last = mm(bank[6][:, 2 * T + E:2 * T + 2 * E], ones_bf[:, :], seen[:, :], start=False, stop=True)
                    last.then_inc(S["g_rk"], 1)
                    after(pe, "s_h", f)
                    for k in range(HK):
                        last = mm(shared_out(i), s_hT[:, k, :], dns_w[:, k, :], start=(k == 0), stop=(k == HK - 1))
                    last.then_inc(S["g_dn"], 1)
                if has(c):
                    after(pe, "c_xnd", c)
                    after(pe, "b_x1", c)
                    nc.tensor.transpose(bank[6][:, 0:T], c_xn[:, :], identity[:, :]).then_inc(S["c_T"], 1)
                if has(d):
                    pv(3)
                if has(c):
                    after(pe, "c_xTc", c)
                    for n, (h0, h1) in enumerate(CH):
                        if n == 0 or n == 1:
                            after(pe, "d_pD", c - 1, 2 - n)
                        else:
                            after(pe, "d_pA", c - 1, 2)
                        if first(i - 1):
                            pe.wait_ge(su_gA, XH)
                            pe.wait_ge(su_gD, XH)
                        mm(bank[2 + n][:, 0:(h1 - h0) * NK], c_xnT[:, :], G[:, bass.ds((c * XH + h0) * NK, (h1 - h0) * NK)],
                           start=True, stop=True).then_inc(S["c_sc"], 1)
                if has(e) and has(d):
                    transpose_third()
                if has(d):
                    after(pe, "c_xTc", d + 1)
                    after(pe, "g_pl", d - 2, 1)
                    for k in range(XP):
                        if k % 2 == 0:
                            after(pe, "d_oc", d, k // 2 + 1)
                        last = mm(bank[6][:, 0:C], c_oT[:, k, :], xwo_s[:, k, :], start=(k == 0), stop=(k == XP - 1))
                    last.then_inc(S["d_y"], 1)
                if has(e):
                    after(pe, "r_Tc", e)
                    mm(bank[7][:, 0:E], r_xnT[:, :], router_w[:, :], start=True, stop=True).then_inc(S["r_lg"], 1)
                if has(a):
                    for g in range(2):
                        after(pe, "a_nr", a, g + 1)
                        for k in range(REP):
                            last = nc.tensor.transpose(bank[g][:, k * T:(k + 1) * T], a_p[:, g * REP + k, :], identity[:, :])
                        last.then_inc(S["b_pT"], 1)
                if first(i):
                    g_mm(1, 12, 14)
                if has(c):
                    after(pe, "v_in", c)
                    after(pe, "d_oc", c - 1)
                    mm_split(bank[5][0:NK, :], [w[:, :] for w in ctx_b], [w[:, 0:512] for w in xwv_w]).then_inc(S["v_mm"], 1)
                if has(a):
                    after(pe, "d_x2", a - 2)
                    after(pe, "a_v", a)
                    for g in range(2):
                        after(pe, "b_pc", a, g + 1)
                        for k in range(REP):
                            last = mm(bank[6][k * L:(k + 1) * L, g * T:(g + 1) * T], v_s[:, g * L:(g + 1) * L], a_pT[:, g * REP + k, :], start=True, stop=True)
                    last.then_inc(S["b_o"], 1)
                if first(i):
                    g_mm(1, 14, 16)
                if has(c):
                    after(pe, "r_lgc", c - 2)
                    mm_split(bank[7][0:NK, :], [w[:, :] for w in ctx_b], [w[:, 512:1024] for w in xwv_w]).then_inc(S["v_mm"], 1)
                if has(e):
                    after(pe, "c_sb", e + 2)
                    for k in range(2 * HK):
                        last = mm(bank[4][:, k * T:(k + 1) * T], ugs_w[:, k * P:(k + 1) * P], r_xnT[:, :], start=True, stop=True)
                    last.then_inc(S["s_ug"], 1)
                if has(a):
                    after(pe, "b_oc", a)
                    for g in range(KV):
                        last = mm(bank[6][:, 0:C], a_oT[:, g, :], ylat_w[:, g, :], start=(g == 0), stop=(g == KV - 1))
                    last.then_inc(S["b_y"], 1)

            pe.wait_ge(xwv_split, 2)
            pe.wait_ge(ld["xwo"], 16)
            pe.wait_ge(ld["router"], 16)
            pe.wait_ge(ld["shared"], 32)
            pe.wait_ge(sort_c, 3)
            pipeline(pe, body)

            pe.wait_ge(ld["ug"], 16)
            pe.wait_ge(ld["dn"], 16)
            warm_up(14)
            pe.wait_ge(blocks_ready, 1)
            pe.wait_ge(owners_ready, 1)
            words = [pe.value_load(packed[0:1, w:w + 1], min_val=0, max_val=E ** PACK - 1) for w in range(NTP // PACK)]
            warm_up(10)
            bits = E.bit_length() - 1
            expert = [(words[k // PACK] >> (bits * (k % PACK))) & (E - 1) for k in range(NT)]

            def step(s, n):
                m = (n + 1) % 2
                if tile(s, 1):
                    up_expert = expert[s - 1]
                if tile(s, 3):
                    down_expert = expert[s - 3]
                    pe.wait_ge(f_h, s - 2)
                    reach(pe, f_hTc, s - 4)
                    for k in range(HK):
                        last = nc.tensor.transpose(bank[4 + m][:, k * P:(k + 1) * P], hg[m][:, k * P:(k + 1) * P], identity[:, :])
                    last.then_inc(f_hT, 1)
                if tile(s, 0):
                    pe.wait_ge(f_ld[n], store_count(s))
                    nc.tensor.transpose(bank[n % 2][:, 0:P], xg_all[:, s * RW:s * RW + C], identity[:, :]).then_inc(f_T, 1)
                if tile(s, 1):
                    pe.wait_ge(f_Tc, s)
                    reach(pe, f_h, s - 2)
                    mm(bank[2 + m][:, :], xgT[m][:, :], ug_w[:, bass.ds(up_expert * (2 * HID), 2 * HID)], start=True, stop=True).then_inc(f_ug, 1)
                if tile(s, 3):
                    pe.wait_ge(f_hTc, s - 2)
                    reach(pe, f_y, s - 4)
                    for k in range(HK):
                        last = mm(bank[6 + m][:, 0:C], hT[m][:, k, :], dn_w[:, bass.ds(down_expert * (HK * C) + k * C, C)], start=(k == 0), stop=(k == HK - 1))
                    last.then_inc(f_dn, 1)

            for s in range(NT + 3):
                step(s, s % RING)


def sort_constants(P, tokens, E=8, pack=8):
    import numpy as np

    pair = tokens // P + 1
    tiles = (tokens - E) // P + E
    tiles = -(-tiles // pack) * pack
    e, k = np.arange(E), np.arange(tiles)
    sign = 1 - 2 * (e % 2)
    first_block = 1 + e // 2 * pair
    row = np.where(sign > 0, first_block * P - 1, (first_block + pair) * P)
    block = np.where(sign > 0, first_block, first_block + pair - 1)
    parts = [e, e * P, row, sign, block, k, (k[:, None] * sign[None, :]).ravel(), E ** (k % pack)]
    return np.concatenate(parts).astype(np.float32)


def kernel(**inputs):
    import numpy as np
    import concourse.bacc as bacc
    from concourse.bass_utils import run_bass_kernel_spmd as run

    nc = bacc.Bacc("TRN2", target_bir_lowering=False, num_devices=1)
    a = {k: np.asarray(v) for k, v in inputs.items()}
    flat = np.ascontiguousarray
    T = a["x"].shape[1]
    CC = a["ctx_768"].shape[2]
    P = 128
    sent = {
        "x": flat(a["x"]),
        "ctxT": flat(a["ctx_768"].reshape(-1, CC).T),
        "wqT": flat(a["L0_attn_wq"].reshape(-1, 8, 128).transpose(2, 1, 0)),
        "wkd": flat(a["L0_attn_wk_down"]), "wvd": flat(a["L0_attn_wv_down"]),
        "wkuT": flat(a["L0_attn_wk_up"].T), "wvuT": flat(a["L0_attn_wv_up"].T), "wo": flat(a["L0_attn_wo"]),
        "xwqT": flat(a["L0_xattn_Wq"].T.reshape(8, P, -1).transpose(1, 0, 2)),
        "xwkT": flat(a["L0_xattn_Wk"].T.reshape(8, P, -1).transpose(1, 0, 2)),
        "xwv": flat(a["L0_xattn_Wv"]), "xwo": flat(a["L0_xattn_Wo"]), "xbo": flat(a["L0_xattn_bo"]),
        "ug": flat(np.concatenate([a["L0_ffn_up"], a["L0_ffn_gate"]], axis=1).transpose(2, 0, 1)),
        "dn": flat(a["L0_ffn_down"].transpose(2, 0, 1).reshape(2, P, 8, P).transpose(1, 2, 0, 3).reshape(P, 8, 2 * P)),
        "router": flat(a["L0_ffn_router"].T),
        "ug_s": flat(np.concatenate([a["L0_ffn_w_up_s"], a["L0_ffn_w_gate_s"]]).T),
        "dn_s": flat(a["L0_ffn_w_down_s"].T.reshape(2, P, P).transpose(1, 0, 2)),
        "ident": np.eye(P, dtype=np.float32),
        "mask": np.where(np.tril(np.ones((T, T), bool)), 0.0, -3.0e38).astype(np.float32),
        "tri": np.triu(np.ones((P, P), np.float32)),
        "steps": sort_constants(P, a["x"].shape[0] * T),
        "tokens": flat(np.arange(a["x"].shape[0] * T).reshape(-1, T).T.astype(np.float32)),
    }
    aps = {k: nc.dram_tensor("in_" + k, v.shape, mybir.dt.from_np(v.dtype), kind="ExternalInput").ap() for k, v in sent.items()}
    out = nc.dram_tensor("out", a["x"].shape, F32, kind="ExternalOutput").ap()
    build_layer(nc, *aps.values(), out)
    r = run(nc, [{"in_" + k: v for k, v in sent.items()}], core_ids=[0])
    return r.results[0]["out"]
```

```python
from contextlib import ExitStack

import concourse.bass as bass
from concourse import mybir

F32 = mybir.dt.float32
F32R = mybir.dt.float32r
BF16 = mybir.dt.bfloat16
I32 = mybir.dt.int32
U32 = mybir.dt.uint32
ALU = mybir.AluOpType
ACT = mybir.ActivationFunctionType
AX_X = mybir.AxisListType.X


def build_layer(nc, x, ctxT, wqT, wkd, wvd, wkuT, wvuT, wo, xwqT, xwkT, xwv, xwo, xbo, ug, dn, router, ug_s, dn_s, ident, mask, tri, steps, tokens, out):
    P = 128
    NB, T, C = x.shape
    CC, NK = ctxT.shape[0], ctxT.shape[1] // NB
    H = wqT.shape[1]
    L = wkuT.shape[1]
    KV = wkd.shape[1] // L
    REP = H // KV
    XH = 16
    XD = xwv.shape[1] // XH
    XP = XH // 2
    SCALE = float(wqT.shape[0]) ** -0.5
    XSCALE = float(XD) ** -0.5
    EPS = 1e-5
    HALF = NB // 2 * NK
    E = router.shape[1]
    HID = ug.shape[2] // 2
    HK = HID // P
    NT = (NB * T - E) // P + E
    PAIR = NB * T // P + 1
    BLOCKS = 1 + E // 2 * PAIR
    RW = 2 * C + 1
    NO_TOKEN = 4.0 * NB * T
    PACK = 8
    NTP = -(-NT // PACK) * PACK
    NCONST = 5 * E + NTP + NTP * E + NTP
    CH = [(0, 5), (5, 10), (10, XH)]

    with ExitStack() as ctx:
        def sb(name, shape, dt=F32):
            return ctx.enter_context(nc.sbuf_tensor(name, shape, dt))

        def sem(name):
            return ctx.enter_context(nc.semaphore(name))

        bank = [ctx.enter_context(nc.psum_tensor(f"bank{n}", [P, 512], F32)) for n in range(8)]

        identity = sb("identity", [P, P])
        identity_bf = sb("identity_bf", [P, P], BF16)
        causal = sb("causal", [P, REP, T], BF16)
        causal_in = sb("causal_in", [P, T])
        group_rows = sb("group_rows", [P, REP])
        minus_half = sb("minus_half", [P, 1])
        ctxT_s = sb("ctxT_s", [CC, NB * NK])
        wqT_s = sb("wqT_s", [P, H, C])
        wkuT_s = sb("wkuT_s", [P, L])
        wvuT_s = sb("wvuT_s", [P, L])
        wo_s = sb("wo_s", [P, H, C])
        wkd_s = sb("wkd_s", [C, KV * L])
        wkd_rep = sb("wkd_rep", [C, KV, REP, L])
        wvd_s = sb("wvd_s", [C, KV * L])
        xwqT_s = sb("xwqT_s", [P, XP, C])
        xwkT_s = sb("xwkT_s", [P, XP, CC])
        xwv_s = sb("xwv_s", [CC, XH * XD])
        xwo_s = sb("xwo_s", [P, XP, C])
        ug_w = sb("ug_w", [C, E * 2 * HID])
        dn_w = sb("dn_w", [P, E * HK * C])
        router_w = sb("router_w", [C, E])
        ugs_w = sb("ugs_w", [C, 2 * HID])
        dns_w = sb("dns_w", [P, HK, C])
        tri_in = sb("tri_in", [P, P])
        tri_bf = sb("tri_bf", [P, P], BF16)
        ones_bf = sb("ones_bf", [P, P], BF16)
        fill_row = sb("fill_row", [P, RW])
        token_ids = sb("token_ids", [T, NB])
        sort_s = sb("sort_s", [P, NCONST])
        ids_c = sort_s[:, 0:E]
        fills_c = sort_s[:, E:2 * E]
        row_c = sort_s[:, 2 * E:3 * E]
        sign_c = sort_s[:, 3 * E:4 * E]
        block_c = sort_s[:, 4 * E:5 * E]
        tile_c = sort_s[:, 5 * E:5 * E + NTP]
        tile_sign_c = sort_s[:, 5 * E + NTP:5 * E + NTP + NTP * E]
        pow_c = sort_s[:, 5 * E + NTP + NTP * E:NCONST]
        bo_row = sb("bo_row", [P, C])
        qlat_w = sb("qlat_w", [C, H * L])
        ylat_w = sb("ylat_w", [P, KV, C])
        xqk_w = [sb("xqk_" + n, [CC, XH, C], F32R) for n in ("hi", "lo")]
        ctx_w = [sb("ctx_" + n, [CC, NB * NK], F32R) for n in ("hi", "lo")]
        xwv_w = [sb("xwv_" + n, [CC, XH * XD], F32R) for n in ("hi", "lo")]
        G = sb("G", [C, NB * XH * NK])
        G4 = G[:, :].rearrange("c (b h k) -> c b h k", b=NB, h=XH)

        xs = sb("xs", [T, NB * C])
        a_stat = sb("a_stat", [T, NB, 6])
        a_mv = sb("a_mv", [T, NB, 2])
        a_ve = sb("a_ve", [T, NB])
        a_rstd = sb("a_rstd", [T, NB])
        a_xn = sb("a_xn", [T, NB, C])
        a_xnT = sb("a_xnT", [C, NB * T])
        v_all = sb("v_all", [T, NB * KV * L])
        c_stat = sb("c_stat", [T, 6])
        c_mv = sb("c_mv", [T, 2])
        c_ve = sb("c_ve", [T, 1])
        c_rstd = sb("c_rstd", [T, 1])
        q_s = sb("q_s", [P, KV, T])
        k_bd = sb("k_bd", [P, KV, REP, T])
        v_s = sb("v_s", [T, KV * L])
        a_max = sb("a_max", [T, H])
        a_nmax = sb("a_nmax", [T, H])
        a_sum = sb("a_sum", [T, H])
        a_rec = sb("a_rec", [T, H])
        a_p = sb("a_p", [T, H, T])
        a_pT = sb("a_pT", [T, H, T])
        a_oT = sb("a_oT", [P, KV, T])
        c_xn = sb("c_xn", [T, C])
        c_xnT = sb("c_xnT", [C, T])
        c_max = sb("c_max", [T, XH])
        c_sum = sb("c_sum", [T, XH])
        c_rec = sb("c_rec", [T, XH])
        c_p = sb("c_p", [T, XH, NK])
        c_pT = sb("c_pT", [NK, XH, T])
        ctx_b = [sb("ctx_b_" + n, [CC, NK], F32R) for n in ("hi", "lo")]
        xv_s = sb("xv_s", [NK, XH * XD])
        c_oT = sb("c_oT", [P, XP, T])

        r_stat = sb("r_stat", [T, 6])
        r_mv = sb("r_mv", [T, 2])
        r_ve = sb("r_ve", [T, 1])
        r_rstd = sb("r_rstd", [T, 1])
        r_xn = sb("r_xn", [T, C])
        rows_s = [sb(f"rows_s{n}", [T, RW]) for n in range(2)]
        r_xnT = sb("r_xnT", [C, T])
        r_log = sb("r_log", [T, E])
        r_top = sb("r_top", [T, 8])
        r_idx = sb("r_idx", [T, 8], U32)
        pick = sb("pick", [T, 1])
        hot = sb("hot", [T, E], BF16)
        seen = sb("seen", [T, E], BF16)
        s_th = sb("s_th", [P, HID])
        s_hu = sb("s_hu", [P, HID])
        s_hT = sb("s_hT", [P, HK, T])
        place = sb("place", [T, 3, E])
        slot_f = sb("slot_f", [T, 1])
        slots_s = [sb(f"slots_s{n}", [T, 1], U32) for n in range(2)]
        full = sb("full", [T, E, E])
        n_tiles = sb("n_tiles", [T, E])
        tile_end = sb("tile_end", [T, E])
        one_row = sb("one_row", [T, E])
        start = sb("start", [T, E])
        base = sb("base", [T, E])
        signed = sb("signed", [T, E])
        done_by = sb("done_by", [T, NTP, E])
        begun_by = sb("begun_by", [T, NTP, E])
        block_f = sb("block_f", [T, NTP, E])
        block_sum = sb("block_sum", [T, NTP])
        block_of = sb("block_of", [T, NTP], I32)
        owner_f = sb("owner_f", [T, NTP])
        owner_c = sb("owner_c", [T, NTP])
        packed_f = sb("packed_f", [T, NTP // PACK])
        packed = sb("packed", [T, NTP // PACK], I32)
        RING = 4
        xg_all = G[:, 0:NT * RW]
        ids = [sb(f"ids{n}", [P, 1], U32) for n in range(RING)]
        ug_hi = G[:, NT * RW + 1:NT * RW + 1 + E * 2 * HID].bitcast(F32R)
        ug_lo = ug_w[:, :].bitcast(F32R)
        xgT = [[sb(f"xgT_{part}{n}", [C, P], F32R) for n in range(2)] for part in ("hi", "lo")]
        th = [sb(f"th{n}", [P, HID]) for n in range(2)]
        hu = [sb(f"hu{n}", [P, HID]) for n in range(2)]
        hg = [sb(f"hg{n}", [P, HID]) for n in range(2)]
        hT = [sb(f"hT{n}", [P, HK, P]) for n in range(2)]
        yg = [sb(f"yg{n}", [P, C]) for n in range(RING)]
        x_slots = nc.dram_tensor("x_slots", (BLOCKS * P, RW), F32).ap()

        ld = {n: sem("ld_" + n) for n in ("x", "const", "kv", "bo", "qk", "ctx", "xqk", "wo", "xwv", "xwo", "ug", "dn", "router", "shared", "sort")}
        half_ready = sem("half_ready")
        consts_ready = sem("consts_ready")
        ln1_ready = sem("ln1_ready")
        ln1_rstd = sem("ln1_rstd")
        su_q = sem("su_q")
        su_qc = sem("su_qc")
        su_T = sem("su_T")
        su_Tc = sem("su_Tc")
        su_v = sem("su_v")
        su_vc = sem("su_vc")
        su_x = sem("su_x")
        su_xA = sem("su_xA")
        su_xD = sem("su_xD")
        ctx_split = sem("ctx_split")
        xwv_split = sem("xwv_split")
        su_g = sem("su_g")
        su_gA = sem("su_gA")
        su_gD = sem("su_gD")
        su_y = sem("su_y")
        su_yc = sem("su_yc")
        names = dict(
            a_v=1, a_qk0=1, a_k1=1, a_qc=1, a_k0c=4, a_k1c=1, a_sc=2, a_mx=2, a_nm=2, a_ex=8, a_rc=2, a_nr=2,
            b_pT=2, b_pc=2, b_o=1, b_oc=1, b_y=1, b_x1=1,
            v_in=2, v_mm=2, v_c0=1, v_c1=1,
            c_st=1, c_mvd=1, c_ved=1, c_rs=1, c_xnd=1, c_bo=1, c_T=1, c_xTc=1, c_sc=3, c_mx=3, c_sb=3, c_ex=3, c_sm=3, c_rc=3, c_nr=3,
            r_st=1, r_mvd=1, r_ved=1, r_rs=1, r_xnd=1, r_T=1, r_Tc=1, r_lg=1, r_lgc=1, r_mx=1, r_ix=1, r_pk=1, r_hot=1,
            s_ug=1, s_tanh=1, s_up=1, s_h=1,
            g_xn=1, g_rk=1, g_dn=1, g_res=1, g_pl=4, g_slot=1, g_seen=1, g_id=1, g_sc=16,
            d_pT=4, d_pA=2, d_pD=2, d_o=4, d_oc=4, d_y=1, d_x2=1)
        S = {n: sem(n) for n in names}

        def after(eng, name, j, count=None):
            n = names[name]
            c = n if count is None else count
            if isinstance(j, int):
                if j < 0:
                    return
                j, c = (NB - 1, n) if j >= NB else (j, c)
            eng.wait_ge(S[name], j * n + c)

        zeroed = sem("zeroed")
        zero_src = sem("zero_src")
        ones_ready = sem("ones_ready")
        sort_c = sem("sort_c")
        sort_d = sem("sort_d")
        blocks_ready = sem("blocks_ready")
        owners_ready = sem("owners_ready")
        f_ld = [sem(f"f_ld{n}") for n in range(RING)]
        ug_his = sem("ug_his")
        ug_losP = sem("ug_losP")
        ug_losD = sem("ug_losD")
        f_T = sem("f_T")
        f_Tlo = sem("f_Tlo")
        f_Tc = sem("f_Tc")
        f_ug = sem("f_ug")
        f_th = sem("f_th")
        f_hu = sem("f_hu")
        f_h = sem("f_h")
        f_hT = sem("f_hT")
        f_hTc = sem("f_hTc")
        f_dn = sem("f_dn")
        f_y = sem("f_y")
        f_st = [sem(f"f_st{n}") for n in range(RING)]
        f_id = sem("f_id")

        block = ctx.enter_context(nc.Block())

        def pipeline(eng, body):
            for i in range(4):
                body(i)
            with eng.Fori(4, NB) as i:
                body(i)
            for i in range(NB, NB + 4):
                body(i)

        def tiles(eng, step, lag=3):
            full_at = RING + 3
            rounds = (NT - full_at) // RING
            for s in range(full_at):
                step(s, s % RING)
            with eng.Fori(0, rounds) as r:
                for n in range(full_at, full_at + RING):
                    step(r * RING + n, n % RING)
            for s in range(full_at + rounds * RING, NT + lag):
                step(s, s % RING)

        def tile(s, ago):
            k = s - ago
            return not isinstance(k, int) or 0 <= k < NT

        def store_count(k):
            return k // RING * 16 + 16

        def reach(eng, semaphore, value):
            if not isinstance(value, int) or value > 0:
                eng.wait_ge(semaphore, value)

        def has(j):
            return not isinstance(j, int) or 0 <= j < NB

        def first(i):
            return isinstance(i, int) and i == 0

        G_BANK = (2, 3, 4, 7)
        PT_BANK = (2, 3, 4, 2)
        O_BANK = (5, 7, 5, 7)

        def qk_heads(rows, n):
            h0 = n // 2 * XP + n % 2
            return rows[:, h0:h0 + 7:2, :]

        def turn(i):
            return isinstance(i, int) and i == NB

        def scores_bank(i, n):
            return bank[(0, 1, 4)[n] if turn(i) else 2 + n]

        def head_scale(h0, h1):
            return c_rec[:, h0:h1].rearrange("p (h t) -> p h t", t=1).broadcast_to([T, h1 - h0, NK])

        def last_batch(j):
            return int(isinstance(j, int) and j == NB - 1)

        def draining(i):
            return isinstance(i, int) and i > NB

        def of_expert(rows, x):
            return rows[:, x * 2 * HID:(x + 1) * 2 * HID]

        DVE_LOS, POOL_LOS = range(0, 2), range(2, E)

        def at_step(i, n):
            return isinstance(i, int) and i == NB + n

        def shared_out(i):
            return bank[1 if draining(i - 1) else 6][:, T:2 * T]

        @block.sync
        def _(sp):
            sp.dma_start(xs[:, :].rearrange("t (b c) -> t b c", b=NB), x.rearrange("b t c -> t b c")).then_inc(ld["x"], 16)
            sp.dma_start(identity[:, :], ident).then_inc(ld["const"], 16)
            sp.dma_start(causal_in[:, :], mask).then_inc(ld["const"], 16)
            sp.dma_start(xwkT_s[:, :, :], xwkT).then_inc(ld["xqk"], 16)
            sp.dma_start(xwqT_s[:, :, :], xwqT).then_inc(ld["xqk"], 16)
            sp.dma_start(xwv_s[:, :], xwv).then_inc(ld["xwv"], 16)
            sp.dma_start(xwo_s[:, :, :], xwo.rearrange("(k p) c -> p k c", p=P)).then_inc(ld["xwo"], 16)
            sp.dma_start(router_w[:, :], router).then_inc(ld["router"], 16)
            sp.dma_start(tri_in[:, :], tri).then_inc(ld["sort"], 16)
            sp.dma_start(sort_s[:, :], steps.rearrange("(a c) -> a c", a=1).broadcast_to([P, NCONST])).then_inc(ld["sort"], 16)
            sp.dma_start(token_ids[:, :], tokens).then_inc(ld["sort"], 16)
            sp.dma_start(ugs_w[:, :], ug_s).then_inc(ld["shared"], 16)
            sp.dma_start(dns_w[:, :, :], dn_s).then_inc(ld["shared"], 16)
            sp.dma_start(ug_w[:, :].rearrange("c (e n) -> c e n", e=E), ug).then_inc(ld["ug"], 16)
            sp.dma_start(dn_w[:, :].rearrange("p (e n) -> p e n", e=E), dn).then_inc(ld["dn"], 16)
            sp.wait_ge(zero_src, 2)
            sp.dma_start(x_slots.rearrange("(n p) c -> p n c", p=P),
                         fill_row[:, :].rearrange("p (n c) -> p n c", n=1).broadcast_to([P, BLOCKS, RW])).then_inc(zeroed, 16)
            sp.wait_ge(blocks_ready, 1)
            first_blocks = [sp.value_load(block_of[0:1, k:k + 1], min_val=0, max_val=BLOCKS - 1) for k in range(2)]
            sp.wait_ge(S["g_sc"], 16 * NB)

            def step(s, n):
                reach(sp, f_T, s - RING + 1)
                if isinstance(s, int) and s < 2:
                    at = first_blocks[s]
                else:
                    at = sp.value_load(block_of[0:1, bass.ds(s, 1)], min_val=0, max_val=BLOCKS - 1)
                sp.dma_start(xg_all[:, bass.ds(s * RW, RW)], x_slots[bass.ds(at * P, P), :]).then_inc(f_ld[n], 16)

            tiles(sp, step, 0)

        @block.scalar
        def _(act):
            act.dma_start(wkuT_s[:, :], wkuT).then_inc(ld["qk"], 16)
            act.dma_start(wqT_s[:, :, :], wqT).then_inc(ld["qk"], 16)
            act.dma_start(wkd_s[:, :], wkd).then_inc(ld["kv"], 16)
            act.dma_start(wvd_s[:, :], wvd).then_inc(ld["kv"], 16)
            act.dma_start(ctxT_s[:, :], ctxT).then_inc(ld["ctx"], 16)
            act.dma_start(wvuT_s[:, :], wvuT).then_inc(ld["wo"], 16)
            act.dma_start(wo_s[:, :, :], wo.rearrange("(h p) c -> p h c", p=P)).then_inc(ld["wo"], 16)
            act.dma_start(bo_row[:, :], xbo.rearrange("(a c) -> a c", a=1).broadcast_to([P, C])).then_inc(ld["bo"], 16)

            def g_copy(half, h):
                act.wait_ge(su_g, half * XH + h + 1)
                nc.scalar.copy(G4[:, half * NB // 2:(half + 1) * NB // 2, h, :],
                               bank[G_BANK[h % 4]][:, 0:HALF].rearrange("p (b k) -> p b k", k=NK)).then_inc(su_gA, 1)

            act.wait_ge(su_q, 1)
            nc.scalar.copy(qlat_w[:, :], bank[0][:, 0:H * L]).then_inc(su_qc, 1)
            for n in (0, 1):
                act.wait_ge(su_T, n + 1)
                nc.scalar.copy(a_xnT[:, n * 512:(n + 1) * 512], bank[6 + n][:, :]).then_inc(su_Tc, 1)
            for n in range(4):
                act.wait_ge(su_x, n + 1)
                nc.scalar.copy(qk_heads(xqk_w[0], n), bank[2 + n][0:CC, :].rearrange("p (h c) -> p h c", h=4)).then_inc(su_xA, 1)
            for h in range(0, XH, 2):
                g_copy(0, h)

            def split_experts(x0, x1):
                act.wait_ge(ld["ug"], 16)
                after(act, "c_sc", NB - 1)
                for x in range(x0, x1):
                    nc.scalar.copy(of_expert(ug_hi, x), of_expert(ug_w, x)).then_inc(ug_his, 1)

            def body(i):
                a, c, d, e, f = i, i - 1, i - 2, i - 3, i - 4
                if has(a):
                    after(act, "a_qk0", a)
                    after(act, "a_sc", a - 1)
                    nc.scalar.copy(q_s[:, :, :], bank[5][:, 0:KV * T].rearrange("p (g t) -> p g t", g=KV)).then_inc(S["a_qc"], 1)
                    for r in range(REP):
                        p = slice(r * L, (r + 1) * L)
                        nc.scalar.copy(k_bd[p, 0, r, :], bank[5][p, 2 * T:3 * T]).then_inc(S["a_k0c"], 1)

                if first(i):
                    g_copy(1, 0)

                def pT_copy(g):
                    after(act, "d_pT", d, g + 1)
                    nc.scalar.copy(c_pT[:, 4 * g:4 * g + 4, :], bank[PT_BANK[g]][0:NK, :].rearrange("p (h t) -> p h t", h=4)).then_inc(S["d_pA"], 1)

                def o_copy(g):
                    after(act, "d_o", d, g + 1)
                    nc.scalar.copy(c_oT[:, 2 * g:2 * g + 2, :], bank[O_BANK[g]][:, 0:2 * T].rearrange("p (h t) -> p h t", h=2)).then_inc(S["d_oc"], 1)

                def exps(h0, h1):
                    if not has(a):
                        return
                    g = h0 // REP
                    after(act, "a_nm", a, g + 1)
                    if h0 == 0:
                        after(act, "b_pT", a - 1)
                    for h in range(h0, h1):
                        nc.scalar.activation(a_p[:, h, :], bank[g][:, h % REP * T:h % REP * T + T], ACT.Exp,
                                             bias=a_nmax[:, h:h + 1], scale=SCALE, accum_out=a_sum[:, h:h + 1]).then_inc(S["a_ex"], 1)

                def c_exp(n):
                    if has(c):
                        h0, h1 = CH[n]
                        after(act, "c_sb", c, n + 1)
                        nc.scalar.activation(c_p[:, h0:h1, :], c_p[:, h0:h1, :], ACT.Exp, scale=XSCALE).then_inc(S["c_ex"], 1)

                if has(d):
                    pT_copy(0)
                    o_copy(0)
                    pT_copy(2)
                exps(0, 2)
                if turn(i):
                    c_exp(0)
                if has(d):
                    o_copy(1)
                if turn(i):
                    c_exp(1)
                exps(2, 4)
                if first(i):
                    g_copy(1, 2)
                exps(4, 5)
                if has(d):
                    o_copy(2)
                exps(5, 6)
                if has(d):
                    o_copy(3)
                if turn(i):
                    c_exp(2)
                exps(6, 8)
                if first(i):
                    for h in range(4, 12, 2):
                        g_copy(1, h)
                if has(e):
                    after(act, "r_T", e)
                    after(act, "s_ug", e - 1)
                    nc.scalar.copy(r_xnT[:, :], bank[7][:, 0:T]).then_inc(S["r_Tc"], 1)
                if at_step(i, 1):
                    split_experts(0, E // 2)
                if at_step(i, 2):
                    split_experts(3 * E // 4, E)

                def a_pT_copy(g):
                    if has(a):
                        after(act, "b_pT", a, g + 1)
                        nc.scalar.copy(a_pT[:, g * REP:(g + 1) * REP, :], bank[g][:, :].rearrange("p (h t) -> p h t", h=REP)).then_inc(S["b_pc"], 1)

                if not turn(i):
                    c_exp(0)
                    c_exp(1)
                a_pT_copy(0)
                a_pT_copy(1)
                if not turn(i):
                    c_exp(2)
                if first(i):
                    g_copy(1, 12)
                if has(c):
                    after(act, "v_mm", c, 1)
                    nc.scalar.copy(xv_s[:, 0:512], bank[5][0:NK, :]).then_inc(S["v_c0"], 1)
                if has(a):
                    after(act, "b_o", a)
                    nc.scalar.copy(a_oT[:, :, :], bank[6][:, 0:KV * T].rearrange("p (g t) -> p g t", g=KV)).then_inc(S["b_oc"], 1)
                if first(i):
                    g_copy(1, 14)
                if has(c):
                    after(act, "v_mm", c, 2)
                    nc.scalar.copy(xv_s[:, 512:1024], bank[7][0:NK, :]).then_inc(S["v_c1"], 1)
                if has(e):
                    after(act, "s_ug", e)
                    after(act, "s_up", e - 1)
                    nc.scalar.activation(s_th[:, :], bank[4][:, HK * T:2 * HK * T], ACT.Tanh, scale=0.5).then_inc(S["s_tanh"], 1)
                    after(act, "r_xnd", e)
                    if not last_batch(e):
                        after(act, "g_sc", e - 1)
                    nc.scalar.copy(rows_s[last_batch(e)][:, 0:C], r_xn[:, :]).then_inc(S["g_xn"], 1)
                if at_step(i, 1):
                    split_experts(E // 2, 3 * E // 4)

            pipeline(act, body)

            def step(s, n):
                if tile(s, 3):
                    act.wait_ge(f_hT, s - 2)
                    reach(act, f_dn, s - 4)
                    nc.scalar.copy(hT[(n + 1) % 2][:, :, :], bank[4 + (n + 1) % 2][:, 0:HK * P].rearrange("p (k t) -> p k t", k=HK)).then_inc(f_hTc, 1)
                if tile(s, 0):
                    act.wait_ge(f_T, s + 1)
                    reach(act, f_ug, s - 1)
                    nc.scalar.copy(xgT[0][n % 2][:, :], bank[n % 2][:, 0:P]).then_inc(f_Tc, 1)
                if tile(s, 1):
                    act.wait_ge(f_ug, s)
                    reach(act, f_hu, s - 2)
                    nc.scalar.activation(th[(n + 1) % 2][:, :], bank[2 + (n + 1) % 2][:, HID:2 * HID], ACT.Tanh, scale=0.5).then_inc(f_th, 1)

            tiles(act, step)

        @block.gpsimd
        def _(pool):
            nc.gpsimd.memset(minus_half[:, :], -0.5).then_inc(half_ready, 1)
            pool.wait_ge(half_ready, 1)
            pool.wait_ge(ln1_ready, 2 * NB + 1)
            nc.gpsimd.tensor_tensor(a_rstd[:, :], a_ve[:, :], minus_half[:, :].broadcast_to([T, NB]), ALU.pow).then_inc(ln1_rstd, 1)
            pool.wait_ge(ld["xwv"], 16)
            nc.gpsimd.tensor_copy(xwv_w[0][:, :], xwv_s[:, :]).then_inc(xwv_split, 1)
            pool.wait_ge(xwv_split, 1)
            nc.gpsimd.tensor_tensor(xwv_w[1][:, :], xwv_s[:, :], xwv_w[0][:, :], ALU.subtract).then_inc(xwv_split, 1)
            pool.wait_ge(ld["ctx"], 16)
            pool.wait_ge(ld["bo"], 16)
            pool.wait_ge(su_vc, 1)
            pool.wait_ge(ld["sort"], 48)

            pool.wait_ge(ctx_split, 2)

            def plain_wait():
                pool.wait_ge(ld["ctx"], 16)

            def split_experts(experts):
                for x in experts:
                    pool.wait_ge(ug_his, x + 1)
                    nc.gpsimd.tensor_tensor(of_expert(ug_lo, x), of_expert(ug_w, x), of_expert(ug_hi, x), ALU.subtract).then_inc(ug_losP, 1)

            def body(i):
                a, c, d, e, f = i, i - 1, i - 2, i - 3, i - 4
                if has(c):
                    after(pool, "c_ved", c)
                    nc.gpsimd.tensor_tensor(c_rstd[:, :], c_ve[:, :], minus_half[:, :], ALU.pow).then_inc(S["c_rs"], 1)
                if has(a):
                    after(pool, "b_o", a - 1)
                    nc.gpsimd.tensor_copy(v_s[:, :], v_all[:, bass.ds(a * (KV * L), KV * L)]).then_inc(S["a_v"], 1)
                if has(c):
                    after(pool, "v_mm", c - 1)
                    for n in range(2):
                        nc.gpsimd.tensor_copy(ctx_b[n][:, :], ctx_w[n][:, bass.ds(c * NK, NK)]).then_inc(S["v_in"], 1)
                    after(pool, "c_xnd", c)
                    rows = xs[:, bass.ds(c * C, C)]
                    nc.gpsimd.tensor_tensor(rows, rows, bo_row[:, :], ALU.add).then_inc(S["c_bo"], 1)
                if has(e):
                    after(pool, "r_ved", e)
                    nc.gpsimd.tensor_tensor(r_rstd[:, :], r_ve[:, :], minus_half[:, :], ALU.pow).then_inc(S["r_rs"], 1)
                if has(a):
                    for g in range(2):
                        after(pool, "a_rc", a, g + 1)
                        h = slice(g * REP, (g + 1) * REP)
                        nc.gpsimd.tensor_tensor(a_p[:, h, :], a_p[:, h, :], a_rec[:, h].rearrange("p (h t) -> p h t", t=1).broadcast_to([T, REP, T]),
                                                ALU.mult).then_inc(S["a_nr"], 1)
                if isinstance(i, int) and i == 3:
                    pool.wait_ge(zeroed, 16)
                if has(f):
                    plain_wait()
                    after(pool, "g_xn", f)
                    nc.gpsimd.tensor_copy(rows_s[last_batch(f)][:, 2 * C:RW], token_ids[:, bass.ds(f, 1)]).then_inc(S["g_id"], 1)
                    if at_step(i, 2):
                        split_experts(POOL_LOS[:4])
                    plain_wait()
                    after(pool, "g_id", f)
                    after(pool, "g_res", f)
                    after(pool, "g_slot", f)
                    nc.gpsimd.indirect_dma_start(out=x_slots, out_offset=bass.IndirectOffsetOnAxis(ap=slots_s[last_batch(f)][:, :], axis=0),
                                                 in_=rows_s[last_batch(f)][:, :], in_offset=None).then_inc(S["g_sc"], 16)
                if has(c) and not turn(i):
                    for n, (h0, h1) in enumerate(CH):
                        after(pool, "c_rc", c, n + 1)
                        nc.gpsimd.tensor_tensor(c_p[:, h0:h1, :], c_p[:, h0:h1, :], head_scale(h0, h1), ALU.mult).then_inc(S["c_nr"], 1)

            pipeline(pool, body)
            split_experts(POOL_LOS[4:])

            out_rows = out.rearrange("b t c -> (b t) c")
            last_token = pool.to_reg(NB * T - 1)

            def step(s, n):
                if tile(s, 0):
                    plain_wait()
                    pool.wait_ge(f_T, s + 1)
                    if tile(s, RING):
                        pool.wait_ge(f_st[n], store_count(s - RING))
                    reach(pool, f_id, s)
                    nc.gpsimd.tensor_copy(ids[n][:, :], xg_all[:, bass.ds(s * RW + 2 * C, 1)]).then_inc(f_id, 1)
                if tile(s, 1):
                    k = (n + RING - 1) % RING
                    plain_wait()
                    pool.wait_ge(f_id, s)
                    pool.wait_ge(f_y, s)
                    nc.gpsimd.indirect_dma_start(out=out_rows, out_offset=bass.IndirectOffsetOnAxis(ap=ids[k][:, :], axis=0),
                                                 in_=yg[k][:, :], in_offset=None, bounds_check=last_token, oob_is_err=False).then_inc(f_st[k], 16)

            tiles(pool, step, 1)
            for n in range(RING):
                pool.wait_ge(f_st[n], 16 * len(range(n, NT, RING)))

        @block.vector
        def _(dve):
            nc.vector.memset(ones_bf[:, :], 1.0).then_inc(ones_ready, 1)
            nc.vector.memset(k_bd[:, :, :, :], 0.0).then_inc(consts_ready, 1)
            nc.vector.memset(fill_row[:, 0:2 * C], 0.0).then_inc(zero_src, 1)
            nc.vector.memset(fill_row[:, 2 * C:RW], NO_TOKEN).then_inc(zero_src, 1)
            nc.vector.memset(seen[:, :], 0.0).then_inc(sort_c, 1)
            nc.vector.memset(one_row[:, :], 1.0).then_inc(sort_c, 1)
            dve.wait_ge(ld["x"], 16)
            for b in range(NB):
                nc.vector.bn_stats(a_stat[:, b, :], xs[:, b * C:(b + 1) * C]).then_inc(ln1_ready, 1)
            for b in range(NB):
                dve.wait_ge(ln1_ready, NB)
                nc.vector.bn_aggr(a_mv[:, b, :], a_stat[:, b, :]).then_inc(ln1_ready, 1)
            dve.wait_ge(ln1_ready, 2 * NB)
            nc.vector.tensor_scalar(a_ve[:, :], a_mv[:, :, 1], EPS, None, ALU.add).then_inc(ln1_ready, 1)
            dve.wait_ge(ld["const"], 32)
            nc.vector.tensor_copy(identity_bf[:, :], identity[:, :]).then_inc(consts_ready, 1)
            nc.vector.tensor_copy(causal[:, :, :], causal_in[:, :].rearrange("p (a t) -> p a t", a=1).broadcast_to([P, REP, T])).then_inc(consts_ready, 1)
            nc.vector.tensor_reduce(group_rows[:, :], identity[:, :].rearrange("p (r l) -> p r l", l=L), AX_X, ALU.add).then_inc(consts_ready, 1)
            dve.wait_ge(ld["kv"], 32)
            nc.vector.tensor_copy(wkd_rep[:, :, :, :], wkd_s[:, :].rearrange("p (g a l) -> p g a l", g=KV, a=1).broadcast_to([C, KV, REP, L])).then_inc(consts_ready, 1)
            dve.wait_ge(ln1_rstd, 1)
            for b in range(NB):
                nc.vector.tensor_scalar(a_xn[:, b, :], xs[:, b * C:(b + 1) * C], a_mv[:, b, 0:1], a_rstd[:, b:b + 1],
                                        ALU.subtract, ALU.mult).then_inc(ln1_ready, 1)
            dve.wait_ge(consts_ready, 5)

            def plain_wait():
                dve.wait_ge(ld["x"], 16)

            def split_experts(experts):
                for x in experts:
                    dve.wait_ge(ug_his, x + 1)
                    nc.vector.tensor_tensor(of_expert(ug_lo, x), of_expert(ug_w, x), of_expert(ug_hi, x), ALU.subtract).then_inc(ug_losD, 1)

            def g_copy(half, h):
                dve.wait_ge(su_g, half * XH + h + 1)
                nc.vector.tensor_copy(G4[:, half * NB // 2:(half + 1) * NB // 2, h, :],
                                      bank[G_BANK[h % 4]][:, 0:HALF].rearrange("p (b k) -> p b k", k=NK)).then_inc(su_gD, 1)

            dve.wait_ge(ld["ctx"], 16)
            nc.vector.tensor_copy(ctx_w[0][:, :], ctxT_s[:, :]).then_inc(ctx_split, 1)
            dve.wait_ge(ctx_split, 1)
            nc.vector.tensor_tensor(ctx_w[1][:, :], ctxT_s[:, :], ctx_w[0][:, :], ALU.subtract).then_inc(ctx_split, 1)
            for n in range(4):
                dve.wait_ge(su_xA, n + 1)
                nc.vector.tensor_tensor(qk_heads(xqk_w[1], n), bank[2 + n][0:CC, :].rearrange("p (h c) -> p h c", h=4), qk_heads(xqk_w[0], n),
                                        ALU.subtract).then_inc(su_xD, 1)
            dve.wait_ge(ld["sort"], 48)
            nc.vector.tensor_copy(tri_bf[:, :], tri_in[:, :]).then_inc(sort_c, 1)
            dve.wait_ge(su_v, 1)
            nc.vector.tensor_copy(v_all[:, :], bank[1][:, 0:NB * KV * L]).then_inc(su_vc, 1)
            dve.wait_ge(su_y, 1)
            nc.vector.tensor_copy(ylat_w[:, :, :], bank[0][:, 0:KV * C].rearrange("p (g c) -> p g c", g=KV)).then_inc(su_yc, 1)
            for h in range(1, XH, 2):
                g_copy(0, h)

            def body(i):
                a, c, d, e, f = i, i - 1, i - 2, i - 3, i - 4
                if has(c):
                    crows = xs[:, bass.ds(c * C, C)]
                    after(dve, "b_x1", c)
                    nc.vector.bn_stats(c_stat[:, :], crows).then_inc(S["c_st"], 1)
                    plain_wait()
                    after(dve, "c_st", c)
                    nc.vector.bn_aggr(c_mv[:, :], c_stat[:, :]).then_inc(S["c_mvd"], 1)
                    after(dve, "c_mvd", c)
                    nc.vector.tensor_scalar(c_ve[:, :], c_mv[:, 1:2], EPS, None, ALU.add).then_inc(S["c_ved"], 1)
                erows = xs[:, bass.ds(e * C, C)] if has(e) else None

                def choose(j):
                    plain_wait()
                    after(dve, "r_lgc", j)
                    nc.vector.max(r_top[:, :], r_log[:, :]).then_inc(S["r_mx"], 1)
                    plain_wait()
                    after(dve, "r_mx", j)
                    nc.vector.max_index(r_idx[:, :], r_top[:, :], r_log[:, :]).then_inc(S["r_ix"], 1)
                    after(dve, "r_ix", j)
                    nc.vector.tensor_copy(pick[:, :], r_idx[:, 0:1]).then_inc(S["r_pk"], 1)
                    after(dve, "r_pk", j)
                    nc.vector.tensor_scalar(hot[:, :], ids_c, pick[:, 0:1], None, ALU.is_equal).then_inc(S["r_hot"], 1)

                def third_statistics():
                    after(dve, "d_x2", e)
                    nc.vector.bn_stats(r_stat[:, :], erows).then_inc(S["r_st"], 1)
                    plain_wait()
                    after(dve, "r_st", e)
                    nc.vector.bn_aggr(r_mv[:, :], r_stat[:, :]).then_inc(S["r_mvd"], 1)
                    after(dve, "r_mvd", e)
                    nc.vector.tensor_scalar(r_ve[:, :], r_mv[:, 1:2], EPS, None, ALU.add).then_inc(S["r_ved"], 1)

                def gate():
                    after(dve, "s_tanh", f)
                    nc.vector.scalar_tensor_tensor(out=s_hu[:, :], in0=s_th[:, :], scalar=1.0, in1=bank[4][:, 0:HK * T], op0=ALU.add, op1=ALU.mult).then_inc(S["s_up"], 1)
                    after(dve, "s_up", f)
                    nc.vector.scalar_tensor_tensor(out=s_hT[:, :, :].rearrange("p k t -> p (k t)"), in0=s_hu[:, :], scalar=0.5, in1=bank[4][:, HK * T:2 * HK * T],
                                                   op0=ALU.mult, op1=ALU.mult).then_inc(S["s_h"], 1)

                def signed_rank():
                    after(dve, "g_rk", f)
                    nc.vector.tensor_tensor(place[:, 0, :], bank[6][:, 2 * T:2 * T + E], sign_c, ALU.mult).then_inc(S["g_pl"], 1)

                def residual(j):
                    after(dve, "g_dn", j)
                    nc.vector.tensor_tensor(rows_s[last_batch(j)][:, C:2 * C], shared_out(j + 4), xs[:, bass.ds(j * C, C)], ALU.add).then_inc(S["g_res"], 1)

                def place_of_rank():
                    after(dve, "g_pl", f, 1)
                    nc.vector.tensor_tensor(place[:, 1, :], place[:, 0, :], row_c, ALU.add).then_inc(S["g_pl"], 1)

                def own_place():
                    after(dve, "g_pl", f, 2)
                    nc.vector.tensor_tensor(place[:, 2, :], place[:, 1, :], hot[:, :], ALU.mult).then_inc(S["g_pl"], 1)

                def slot_sum():
                    after(dve, "g_pl", f, 3)
                    nc.vector.reduce_sum(slot_f[:, :], place[:, 2, :], AX_X).then_inc(S["g_pl"], 1)

                def slot_number():
                    after(dve, "g_pl", f, 4)
                    if not last_batch(f):
                        after(dve, "g_xn", f)
                    nc.vector.tensor_copy(slots_s[last_batch(f)][:, :], slot_f[:, :]).then_inc(S["g_slot"], 1)
                    nc.vector.tensor_tensor(seen[:, :], seen[:, :], hot[:, :], ALU.add).then_inc(S["g_seen"], 1)

                def slots():
                    place_of_rank()
                    own_place()
                    slot_sum()
                    slot_number()

                def pT_copy(g):
                    after(dve, "d_pT", d, g + 1)
                    nc.vector.tensor_copy(c_pT[:, 4 * g:4 * g + 4, :], bank[PT_BANK[g]][0:NK, :].rearrange("p (h t) -> p h t", h=4)).then_inc(S["d_pD"], 1)

                if at_step(i, 3):
                    choose(f)
                    residual(f - 1)
                    signed_rank()
                    gate()
                    place_of_rank()
                    compare_counts()
                    own_place()
                    tiles_of_experts()
                    slot_sum()
                    tile_ends()
                    slot_number()
                    residual(f)
                    tile_starts()
                    tile_blocks()
                    return
                if at_step(i, 1):
                    pT_copy(1)
                    gate()
                if has(e) and not has(c):
                    third_statistics()
                if has(a):
                    after(dve, "a_k1", a)
                    after(dve, "a_sc", a - 1)
                    nc.vector.tensor_tensor(k_bd[:, 1, :, :], bank[1][:, 0:T].rearrange("p (a t) -> p a t", a=1).broadcast_to([P, REP, T]),
                                            group_rows[:, :].rearrange("p (r a) -> p r a", a=1).broadcast_to([P, REP, T]), ALU.mult).then_inc(S["a_k1c"], 1)
                if first(i):
                    g_copy(1, 1)

                def row_max(g):
                    after(dve, "a_sc", a, g + 1)
                    hs = slice(g * REP, (g + 1) * REP)
                    nc.vector.reduce_max(a_max[:, hs], bank[g][:, :].rearrange("p (h t) -> p h t", h=REP), AX_X).then_inc(S["a_mx"], 1)
                    after(dve, "a_mx", a, g + 1)
                    nc.vector.tensor_scalar(a_nmax[:, hs], a_max[:, hs], -SCALE, None, ALU.mult).then_inc(S["a_nm"], 1)

                def row_rec(g):
                    hs = slice(g * REP, (g + 1) * REP)
                    after(dve, "a_ex", a, REP * (g + 1))
                    nc.vector.reciprocal(a_rec[:, hs], a_sum[:, hs]).then_inc(S["a_rc"], 1)

                def c_T_copy():
                    after(dve, "c_T", c)
                    nc.vector.tensor_copy(c_xnT[:, :], bank[6][:, 0:T]).then_inc(S["c_xTc"], 1)

                if has(f) and not at_step(i, 1):
                    gate()
                if has(c):
                    after(dve, "c_rs", c)
                    nc.vector.tensor_scalar(c_xn[:, :], crows, c_mv[:, 0:1], c_rstd[:, 0:1], ALU.subtract, ALU.mult).then_inc(S["c_xnd"], 1)
                if has(d) and not at_step(i, 1):
                    pT_copy(1)
                if turn(i):
                    c_T_copy()
                if has(a):
                    row_max(0)
                if has(e) and has(c):
                    third_statistics()
                if has(a):
                    row_max(1)
                if at_step(i, 1):
                    choose(f)
                if has(d):
                    pT_copy(3)
                if has(e):
                    after(dve, "r_rs", e)
                    after(dve, "g_xn", e - 1)
                    nc.vector.tensor_scalar(r_xn[:, :], erows, r_mv[:, 0:1], r_rstd[:, 0:1], ALU.subtract, ALU.mult).then_inc(S["r_xnd"], 1)
                if has(f) and draining(i - 1):
                    choose(f)
                if has(c) and not turn(i):
                    c_T_copy()
                if at_step(i, 2):
                    signed_rank()
                    slots()
                elif has(f) and not turn(i):
                    residual(f)
                    signed_rank()
                    slots()
                if first(i):
                    for h in range(3, 12, 2):
                        g_copy(1, h)
                        if h in (5, 9):
                            row_rec(h // 8)
                    g_copy(1, 13)
                    g_copy(1, 15)
                elif has(a):
                    row_rec(0)
                if has(a) and not first(i):
                    row_rec(1)
                if has(c):
                    for n, (h0, h1) in enumerate(CH):
                        s = scores_bank(i, n)[:, 0:(h1 - h0) * NK].rearrange("p (h k) -> p h k", k=NK)
                        after(dve, "c_sc", c, n + 1)
                        nc.vector.reduce_max(c_max[:, h0:h1], s, AX_X).then_inc(S["c_mx"], 1)
                        after(dve, "c_mx", c, n + 1)
                        nc.vector.tensor_tensor(c_p[:, h0:h1, :], s, c_max[:, h0:h1].rearrange("p (h k) -> p h k", k=1).broadcast_to([T, h1 - h0, NK]),
                                                ALU.subtract).then_inc(S["c_sb"], 1)

                def c_scale(n):
                    h0, h1 = CH[n]
                    after(dve, "c_ex", c, n + 1)
                    nc.vector.reduce_sum(c_sum[:, h0:h1], c_p[:, h0:h1, :], AX_X).then_inc(S["c_sm"], 1)
                    after(dve, "c_sm", c, n + 1)
                    nc.vector.reciprocal(c_rec[:, h0:h1], c_sum[:, h0:h1]).then_inc(S["c_rc"], 1)
                    if turn(i):
                        after(dve, "c_rc", c, n + 1)
                        nc.vector.tensor_tensor(c_p[:, h0:h1, :], c_p[:, h0:h1, :], head_scale(h0, h1), ALU.mult).then_inc(S["c_nr"], 1)

                if turn(i):
                    residual(f)
                    signed_rank()
                    slots()
                    c_scale(0)
                if at_step(i, 1):
                    split_experts(DVE_LOS)
                if has(d):
                    after(dve, "c_bo", d)
                    after(dve, "d_y", d)
                    rows = xs[:, bass.ds(d * C, C)]
                    nc.vector.tensor_tensor(rows, bank[6][:, 0:C], rows, ALU.add).then_inc(S["d_x2"], 1)
                if has(e):
                    after(dve, "r_lg", e)
                    nc.vector.tensor_copy(r_log[:, :], bank[7][:, 0:E]).then_inc(S["r_lgc"], 1)
                if has(c):
                    for n in range(1 if turn(i) else 0, 3):
                        c_scale(n)
                if has(e) and not draining(i + 1):
                    choose(e)
                if has(a):
                    after(dve, "b_y", a)
                    rows = xs[:, bass.ds(a * C, C)]
                    nc.vector.tensor_tensor(rows, bank[6][:, 0:C], rows, ALU.add).then_inc(S["b_x1"], 1)

            def compare_counts():
                count = bank[6][:, 2 * T + E:2 * T + 2 * E]
                nc.vector.tensor_tensor(full[:, :, :], count.rearrange("p (e k) -> p e k", k=1).broadcast_to([T, E, E]),
                                        fills_c.rearrange("p (e k) -> p e k", e=1).broadcast_to([T, E, E]), ALU.is_gt).then_inc(sort_d, 1)

            def tiles_of_experts():
                dve.wait_ge(sort_d, 1)
                nc.vector.reduce_sum(n_tiles[:, :], full[:, :, :], AX_X).then_inc(sort_d, 1)

            def tile_ends():
                dve.wait_ge(sort_d, 2)
                nc.vector.tensor_tensor_scan(tile_end[:, :], one_row[:, :], n_tiles[:, :], 0.0, ALU.mult, ALU.add).then_inc(sort_d, 1)

            def tile_starts():
                dve.wait_ge(sort_d, 3)
                nc.vector.tensor_tensor(start[:, :], tile_end[:, :], n_tiles[:, :], ALU.subtract).then_inc(sort_d, 1)
                dve.wait_ge(sort_d, 4)

            def tile_blocks():
                nc.vector.tensor_tensor(signed[:, :], start[:, :], sign_c, ALU.mult).then_inc(sort_d, 1)

                def per_tile(row):
                    return row.rearrange("p (n e) -> p n e", n=1).broadcast_to([T, NTP, E])

                tile_n = tile_c.rearrange("p (n e) -> p n e", e=1).broadcast_to([T, NTP, E])
                nc.vector.tensor_tensor(done_by[:, :, :], tile_n, per_tile(tile_end[:, :]), ALU.is_ge).then_inc(sort_d, 1)
                nc.vector.tensor_tensor(begun_by[:, :, :], tile_n, per_tile(start[:, :]), ALU.is_ge).then_inc(sort_d, 1)
                dve.wait_ge(sort_d, 7)
                nc.vector.tensor_tensor(base[:, :], block_c, signed[:, :], ALU.subtract).then_inc(sort_d, 1)
                nc.vector.tensor_tensor(begun_by[:, :, :], begun_by[:, :, :], done_by[:, :, :], ALU.subtract).then_inc(sort_d, 1)
                dve.wait_ge(sort_d, 9)
                nc.vector.tensor_tensor(block_f[:, :, :], tile_sign_c.rearrange("p (n e) -> p n e", n=NTP), per_tile(base[:, :]), ALU.add).then_inc(sort_d, 1)
                dve.wait_ge(sort_d, 10)
                nc.vector.tensor_tensor(block_f[:, :, :], block_f[:, :, :], begun_by[:, :, :], ALU.mult).then_inc(sort_d, 1)
                dve.wait_ge(sort_d, 11)
                nc.vector.reduce_sum(block_sum[:, :], block_f[:, :, :], AX_X).then_inc(sort_d, 1)
                dve.wait_ge(sort_d, 12)
                nc.vector.tensor_copy(block_of[:, :], block_sum[:, :]).then_inc(blocks_ready, 1)
                nc.vector.reduce_sum(owner_f[:, :], done_by[:, :, :], AX_X).then_inc(sort_d, 1)
                dve.wait_ge(sort_d, 13)
                nc.vector.tensor_scalar(owner_c[:, :], owner_f[:, :], float(E - 1), None, ALU.min).then_inc(sort_d, 1)
                dve.wait_ge(sort_d, 14)
                nc.vector.tensor_tensor(owner_c[:, :], owner_c[:, :], pow_c, ALU.mult).then_inc(sort_d, 1)
                dve.wait_ge(sort_d, 15)
                nc.vector.reduce_sum(packed_f[:, :], owner_c[:, :].rearrange("p (w n) -> p w n", n=PACK), AX_X).then_inc(sort_d, 1)
                dve.wait_ge(sort_d, 16)
                nc.vector.tensor_copy(packed[:, :], packed_f[:, :]).then_inc(owners_ready, 1)

            pipeline(dve, body)

            def step(s, n):
                m = (n + 1) % 2
                if tile(s, 0):
                    dve.wait_ge(f_Tc, s + 1)
                    nc.vector.tensor_tensor(xgT[1][n % 2][:, :], bank[n % 2][:, 0:P], xgT[0][n % 2][:, :], ALU.subtract).then_inc(f_Tlo, 1)
                if tile(s, 1):
                    dve.wait_ge(f_th, s)
                    nc.vector.scalar_tensor_tensor(out=hu[m][:, :], in0=th[m][:, :], scalar=1.0, in1=bank[2 + m][:, 0:HID], op0=ALU.add, op1=ALU.mult).then_inc(f_hu, 1)
                    dve.wait_ge(f_hu, s)
                    reach(dve, f_hT, s - 2)
                    nc.vector.scalar_tensor_tensor(out=hg[m][:, :], in0=hu[m][:, :], scalar=0.5, in1=bank[2 + m][:, HID:2 * HID], op0=ALU.mult, op1=ALU.mult).then_inc(f_h, 1)
                if tile(s, 3):
                    k, r = s - 3, (n + 1) % RING
                    dve.wait_ge(f_dn, k + 1)
                    if tile(s, 3 + RING):
                        dve.wait_ge(f_st[r], store_count(k - RING))
                    nc.vector.tensor_tensor(yg[r][:, :], bank[6 + m][:, 0:C], xg_all[:, bass.ds(k * RW + C, C)], ALU.add).then_inc(f_y, 1)

            tiles(dve, step)

        @block.tensor
        def _(pe):
            mm = nc.tensor.matmul

            def mm_split(result, a, b):
                mm(result, a[0], b[0], start=True, stop=False)
                mm(result, a[0], b[1], start=False, stop=False)
                return mm(result, a[1], b[0], start=False, stop=True)


            def warm_up(products):
                for _ in range(products):
                    mm(bank[0][:, :].rearrange("p (a t) -> p a t", t=P), ones_bf[:, :],
                       ones_bf[:, :].rearrange("p (a t) -> p a t", a=1).broadcast_to([P, 4, P]), start=True, stop=True)

            pe.wait_ge(ones_ready, 1)
            warm_up(16)
            pe.wait_ge(ld["qk"], 32)
            for h in range(H):
                last = mm(bank[0][:, h * L:(h + 1) * L], wqT_s[:, h, :], wkuT_s[:, :], start=True, stop=True)
            last.then_inc(su_q, 1)
            pe.wait_ge(ld["const"], 32)
            for b in range(NB):
                pe.wait_ge(ln1_ready, 2 * NB + 2 + b)
                last = nc.tensor.transpose(bank[6 + b // 4][:, b % 4 * T:(b % 4 + 1) * T], a_xn[:, b, :], identity[:, :])
                if b % 4 == 3:
                    last.then_inc(su_T, 1)
            pe.wait_ge(ld["xqk"], 32)
            for n in range(4):
                half, odd = n // 2, n % 2
                for k in range(4):
                    p = slice(odd * XD, odd * XD + XD)
                    last = mm(bank[2 + n][0:CC, k * C:(k + 1) * C], xwkT_s[p, half * 4 + k, :], xwqT_s[p, half * 4 + k, :], start=True, stop=True)
                last.then_inc(su_x, 1)
            pe.wait_ge(su_Tc, 2)
            pe.wait_ge(ld["kv"], 32)
            for b in range(NB):
                last = mm(bank[1][:, b * KV * L:(b + 1) * KV * L], a_xnT[:, b * T:(b + 1) * T], wvd_s[:, :], start=True, stop=True)
            last.then_inc(su_v, 1)
            pe.wait_ge(su_qc, 1)
            pe.wait_ge(ld["wo"], 32)
            for h in range(H):
                g, r = h // REP, h % REP
                last = mm(bank[0][r * L:(r + 1) * L, g * C:(g + 1) * C], wvuT_s[:, :], wo_s[:, h, :], start=True, stop=True)
            last.then_inc(su_y, 1)

            def g_mm(half, h0=0, h1=XH):
                for h in range(h0, h1):
                    n = half * XH + h
                    if n >= 4:
                        pe.wait_ge((su_gA, su_gD)[h % 2], (n - 4) // 2 + 1)
                    mm_split(bank[G_BANK[h % 4]][:, 0:HALF], [w[:, h, :] for w in xqk_w], [w[:, half * HALF:(half + 1) * HALF] for w in ctx_w]).then_inc(su_g, 1)

            pe.wait_ge(su_xA, 4)
            pe.wait_ge(su_xD, 4)
            pe.wait_ge(ctx_split, 2)
            g_mm(0)
            pe.wait_ge(consts_ready, 5)
            pe.wait_ge(su_vc, 1)
            pe.wait_ge(su_yc, 1)

            def body(i):
                a, c, d, e, f = i, i - 1, i - 2, i - 3, i - 4

                def pT(g):
                    after(pe, "c_nr", d, min(g + 1, 3))
                    if g == 2:
                        after(pe, "s_h", d - 2)
                    if g == 3:
                        after(pe, "d_pA", d, 1)
                    for k in range(4):
                        last = nc.tensor.transpose(bank[PT_BANK[g]][0:NK, k * T:(k + 1) * T], c_p[:, 4 * g + k, :], identity[:, :])
                    last.then_inc(S["d_pT"], 1)

                def pv(g):
                    after(pe, ("d_pA", "d_pD")[g % 2], d, g // 2 + 1)
                    if g == 0:
                        after(pe, "v_c0", d)
                        after(pe, "v_c1", d)
                    if g >= 2:
                        after(pe, "d_oc", d, g - 1)
                    if g == 1:
                        after(pe, "v_c1", d)
                    for k in range(4):
                        h = 4 * g + k
                        o = k % 2 * XD
                        last = mm(bank[O_BANK[g]][o:o + XD, k // 2 * T:(k // 2 + 1) * T], xv_s[:, h * XD:(h + 1) * XD], c_pT[:, h, :], start=True, stop=True)
                    last.then_inc(S["d_o"], 1)

                def scores(g):
                    if g == 0:
                        after(pe, "a_qc", a)
                        after(pe, "a_k0c", a)
                        after(pe, "b_pc", a - 1)
                    else:
                        after(pe, "a_k1c", a)
                    mm(bank[g][:, :], identity_bf[:, :], causal[:, :, :].rearrange("p r t -> p (r t)"), start=True, stop=False)
                    mm(bank[g][:, :], q_s[:, g, :], k_bd[:, g, :, :].rearrange("p r t -> p (r t)"), start=False, stop=True).then_inc(S["a_sc"], 1)

                def transpose_third():
                    after(pe, "r_xnd", e)
                    after(pe, "d_oc", e + 1)
                    nc.tensor.transpose(bank[7][:, 0:T], r_xn[:, :], identity[:, :]).then_inc(S["r_T"], 1)

                def transpose_second():
                    after(pe, "c_xnd", c)
                    after(pe, "b_x1", c)
                    nc.tensor.transpose(bank[6][:, 0:T], c_xn[:, :], identity[:, :]).then_inc(S["c_T"], 1)

                def rank():
                    after(pe, "r_hot", f)
                    after(pe, "b_x1", f + 3)
                    mm(bank[6][:, 2 * T:2 * T + E], tri_bf[:, :], hot[:, :], start=True, stop=False)
                    last = mm(bank[6][:, 2 * T:2 * T + E], ones_bf[:, :], seen[:, :], start=False, stop=True)
                    if isinstance(i, int) and i == NB + 3:
                        mm(bank[6][:, 2 * T + E:2 * T + 2 * E], ones_bf[:, :], hot[:, :], start=True, stop=False)
                        last = mm(bank[6][:, 2 * T + E:2 * T + 2 * E], ones_bf[:, :], seen[:, :], start=False, stop=True)
                    last.then_inc(S["g_rk"], 1)

                def shared_down():
                    after(pe, "s_h", f)
                    for k in range(HK):
                        last = mm(shared_out(i), s_hT[:, k, :], dns_w[:, k, :], start=(k == 0), stop=(k == HK - 1))
                    last.then_inc(S["g_dn"], 1)

                if has(a):
                    after(pe, "v_c0", a - 2)
                    xnT = a_xnT[:, bass.ds(a * T, T)]
                    for g in range(KV):
                        mm(bank[5][:, g * T:(g + 1) * T], qlat_w[:, g * P:(g + 1) * P], xnT, start=True, stop=True)
                    mm(bank[5][:, 2 * T:3 * T], wkd_rep[:, 0, :, :].rearrange("c r l -> c (r l)"), xnT, start=True, stop=True).then_inc(S["a_qk0"], 1)
                if has(a):
                    after(pe, "b_pc", a - 1)
                    mm(bank[1][:, 0:T], wkd_rep[:, 1, :, :].rearrange("c r l -> c (r l)"), xnT, start=True, stop=True).then_inc(S["a_k1"], 1)
                if first(i):
                    g_mm(1, 0, 2)
                if has(d):
                    pT(0)
                    pT(1)
                if has(a):
                    scores(0)
                if has(d):
                    if has(a):
                        after(pe, "a_qc", a)
                        after(pe, "a_k0c", a)
                    pv(0)
                if has(a):
                    scores(1)
                if first(i):
                    g_mm(1, 2, 12)
                if turn(i):
                    transpose_second()
                if has(d):
                    pT(2)
                    if not turn(i):
                        pv(1)
                    pT(3)
                    if not turn(i):
                        pv(2)
                if has(e) and not has(d):
                    if at_step(i, 2):
                        warm_up(8)
                    transpose_third()
                if has(f) and not turn(i):
                    rank()
                    if not at_step(i, 2):
                        shared_down()
                if has(c) and not turn(i):
                    transpose_second()
                if has(d) and not turn(i):
                    pv(3)
                if has(c):
                    after(pe, "c_xTc", c)
                    if turn(i):
                        after(pe, "b_pc", c)
                    for n, (h0, h1) in enumerate(CH):
                        if n < 2 and not turn(i):
                            after(pe, "d_pD", c - 1, 2 - n)
                        elif n == 2:
                            after(pe, "d_pA", c - 1, 2)
                        if first(i - 1):
                            pe.wait_ge(su_gA, XH)
                            pe.wait_ge(su_gD, XH)
                        mm(scores_bank(i, n)[:, 0:(h1 - h0) * NK], c_xnT[:, :], G[:, bass.ds((c * XH + h0) * NK, (h1 - h0) * NK)],
                           start=True, stop=True).then_inc(S["c_sc"], 1)
                if turn(i):
                    rank()
                    shared_down()
                    for g in range(1, 4):
                        pv(g)
                if has(e) and has(d):
                    transpose_third()
                if has(d):
                    after(pe, "c_xTc", d + 1)
                    after(pe, "g_pl", d - 2, 1)
                    for k in range(XP):
                        if k % 2 == 0:
                            after(pe, "d_oc", d, k // 2 + 1)
                        last = mm(bank[6][:, 0:C], c_oT[:, k, :], xwo_s[:, k, :], start=(k == 0), stop=(k == XP - 1))
                    last.then_inc(S["d_y"], 1)
                if has(e):
                    after(pe, "r_Tc", e)
                    mm(bank[7][:, 0:E], r_xnT[:, :], router_w[:, :], start=True, stop=True).then_inc(S["r_lg"], 1)
                if has(a):
                    for g in range(2):
                        after(pe, "a_nr", a, g + 1)
                        for k in range(REP):
                            last = nc.tensor.transpose(bank[g][:, k * T:(k + 1) * T], a_p[:, g * REP + k, :], identity[:, :])
                        last.then_inc(S["b_pT"], 1)
                if first(i):
                    g_mm(1, 12, 14)
                if has(c):
                    after(pe, "v_in", c)
                    after(pe, "d_oc", c - 1)
                    mm_split(bank[5][0:NK, :], [w[:, :] for w in ctx_b], [w[:, 0:512] for w in xwv_w]).then_inc(S["v_mm"], 1)
                if has(a):
                    after(pe, "d_x2", a - 2)
                    after(pe, "a_v", a)
                    for g in range(2):
                        after(pe, "b_pc", a, g + 1)
                        for k in range(REP):
                            last = mm(bank[6][k * L:(k + 1) * L, g * T:(g + 1) * T], v_s[:, g * L:(g + 1) * L], a_pT[:, g * REP + k, :], start=True, stop=True)
                    last.then_inc(S["b_o"], 1)
                if first(i):
                    g_mm(1, 14, 16)
                if has(c):
                    after(pe, "r_lgc", c - 2)
                    mm_split(bank[7][0:NK, :], [w[:, :] for w in ctx_b], [w[:, 512:1024] for w in xwv_w]).then_inc(S["v_mm"], 1)
                if has(e):
                    after(pe, "c_sb", e + 2)
                    if at_step(i, 2):
                        after(pe, "s_h", f)
                    for k in range(2 * HK):
                        last = mm(bank[4][:, k * T:(k + 1) * T], ugs_w[:, k * P:(k + 1) * P], r_xnT[:, :], start=True, stop=True)
                    last.then_inc(S["s_ug"], 1)
                if at_step(i, 2):
                    shared_down()
                if has(a):
                    after(pe, "b_oc", a)
                    for g in range(KV):
                        last = mm(bank[6][:, 0:C], a_oT[:, g, :], ylat_w[:, g, :], start=(g == 0), stop=(g == KV - 1))
                    last.then_inc(S["b_y"], 1)

            pe.wait_ge(xwv_split, 2)
            pe.wait_ge(ld["xwo"], 16)
            pe.wait_ge(ld["router"], 16)
            pe.wait_ge(ld["shared"], 32)
            pe.wait_ge(sort_c, 3)
            pipeline(pe, body)

            pe.wait_ge(ld["dn"], 16)
            warm_up(18)
            pe.wait_ge(blocks_ready, 1)
            pe.wait_ge(owners_ready, 1)
            words = [pe.value_load(packed[0:1, w:w + 1], min_val=0, max_val=E ** PACK - 1) for w in range(NTP // PACK)]
            bits = E.bit_length() - 1
            pe.wait_ge(ug_losP, len(POOL_LOS))
            pe.wait_ge(ug_losD, len(DVE_LOS))
            expert = [(words[k // PACK] >> (bits * (k % PACK))) & (E - 1) for k in range(NT)]

            def step(s, n):
                m = (n + 1) % 2
                if tile(s, 1):
                    up_expert = expert[s - 1]

                def transpose_hidden(k):
                    pe.wait_ge(f_h, k + 1)
                    reach(pe, f_hTc, k - 1)
                    for c in range(HK):
                        last = nc.tensor.transpose(bank[4 + k % 2][:, c * P:(c + 1) * P], hg[k % 2][:, c * P:(c + 1) * P], identity[:, :])
                    last.then_inc(f_hT, 1)

                if tile(s, 3):
                    down_expert = expert[s - 3]
                    if s < NT + 2:
                        transpose_hidden(s - 3)
                    if s == NT + 1:
                        transpose_hidden(s - 2)
                if tile(s, 0):
                    pe.wait_ge(f_ld[n], store_count(s))
                    nc.tensor.transpose(bank[n % 2][:, 0:P], xg_all[:, s * RW:s * RW + C], identity[:, :]).then_inc(f_T, 1)
                if tile(s, 1):
                    pe.wait_ge(f_Tlo, s)
                    reach(pe, f_h, s - 2)
                    mm_split(bank[2 + m][:, :], [part[m][:, :] for part in xgT], [w[:, bass.ds(up_expert * (2 * HID), 2 * HID)] for w in (ug_hi, ug_lo)]).then_inc(f_ug, 1)
                if tile(s, 3):
                    pe.wait_ge(f_hTc, s - 2)
                    reach(pe, f_y, s - 4)
                    for k in range(HK):
                        last = mm(bank[6 + m][:, 0:C], hT[m][:, k, :], dn_w[:, bass.ds(down_expert * (HK * C) + k * C, C)], start=(k == 0), stop=(k == HK - 1))
                    last.then_inc(f_dn, 1)

            for s in range(NT + 3):
                step(s, s % RING)


def sort_constants(P, tokens, E=8, pack=8):
    import numpy as np

    pair = tokens // P + 1
    tiles = (tokens - E) // P + E
    tiles = -(-tiles // pack) * pack
    e, k = np.arange(E), np.arange(tiles)
    sign = 1 - 2 * (e % 2)
    first_block = 1 + e // 2 * pair
    row = np.where(sign > 0, first_block * P - 1, (first_block + pair) * P)
    block = np.where(sign > 0, first_block, first_block + pair - 1)
    parts = [e, e * P, row, sign, block, k, (k[:, None] * sign[None, :]).ravel(), E ** (k % pack)]
    return np.concatenate(parts).astype(np.float32)


def kernel(**inputs):
    import numpy as np
    import concourse.bacc as bacc
    from concourse.bass_utils import run_bass_kernel_spmd as run

    nc = bacc.Bacc("TRN2", target_bir_lowering=False, num_devices=1)
    a = {k: np.asarray(v) for k, v in inputs.items()}
    flat = np.ascontiguousarray
    T = a["x"].shape[1]
    CC = a["ctx_768"].shape[2]
    P = 128
    sent = {
        "x": flat(a["x"]),
        "ctxT": flat(a["ctx_768"].reshape(-1, CC).T),
        "wqT": flat(a["L0_attn_wq"].reshape(-1, 8, 128).transpose(2, 1, 0)),
        "wkd": flat(a["L0_attn_wk_down"]), "wvd": flat(a["L0_attn_wv_down"]),
        "wkuT": flat(a["L0_attn_wk_up"].T), "wvuT": flat(a["L0_attn_wv_up"].T), "wo": flat(a["L0_attn_wo"]),
        "xwqT": flat(a["L0_xattn_Wq"].T.reshape(8, P, -1).transpose(1, 0, 2)),
        "xwkT": flat(a["L0_xattn_Wk"].T.reshape(8, P, -1).transpose(1, 0, 2)),
        "xwv": flat(a["L0_xattn_Wv"]), "xwo": flat(a["L0_xattn_Wo"]), "xbo": flat(a["L0_xattn_bo"]),
        "ug": flat(np.concatenate([a["L0_ffn_up"], a["L0_ffn_gate"]], axis=1).transpose(2, 0, 1)),
        "dn": flat(a["L0_ffn_down"].transpose(2, 0, 1).reshape(2, P, 8, P).transpose(1, 2, 0, 3).reshape(P, 8, 2 * P)),
        "router": flat(a["L0_ffn_router"].T),
        "ug_s": flat(np.concatenate([a["L0_ffn_w_up_s"], a["L0_ffn_w_gate_s"]]).T),
        "dn_s": flat(a["L0_ffn_w_down_s"].T.reshape(2, P, P).transpose(1, 0, 2)),
        "ident": np.eye(P, dtype=np.float32),
        "mask": np.where(np.tril(np.ones((T, T), bool)), 0.0, -3.0e38).astype(np.float32),
        "tri": np.triu(np.ones((P, P), np.float32)),
        "steps": sort_constants(P, a["x"].shape[0] * T),
        "tokens": flat(np.arange(a["x"].shape[0] * T).reshape(-1, T).T.astype(np.float32)),
    }
    aps = {k: nc.dram_tensor("in_" + k, v.shape, mybir.dt.from_np(v.dtype), kind="ExternalInput").ap() for k, v in sent.items()}
    out = nc.dram_tensor("out", a["x"].shape, F32, kind="ExternalOutput").ap()
    build_layer(nc, *aps.values(), out)
    r = run(nc, [{"in_" + k: v for k, v in sent.items()}], core_ids=[0])
    return r.results[0]["out"]
```
